# Optimizing a Trainium2 kernel written in Bass

```python
import numpy as np
import jax
import jax.numpy as jnp

def _softmax(x, axis=-1):
    return jax.nn.softmax(x, axis=axis)

def _gelu(x):
    return jax.nn.gelu(x, approximate=True)

def _silu(x):
    return jax.nn.silu(x)

def _sigmoid(x):
    return jax.nn.sigmoid(x)

def _layernorm(x, axis=-1, eps=1e-05):
    m = jnp.mean(x, axis=axis, keepdims=True)
    v = jnp.var(x, axis=axis, keepdims=True)
    return (x - m) / jnp.sqrt(v + eps)

def _scatter_add(tgt, idx, src, axis=0):
    return tgt.at[idx].add(src)

def _segment_sum(src, seg, n):
    return jax.ops.segment_sum(src, seg, n)
kernel_name = 'mk_cond_seq_d2_seqx_r8_e3419c'

def setup_inputs(seed: int=0):
    np.random.seed(seed)
    _w = jnp.asarray

    def _rec_inputs():
        import jax
        import jax.numpy as jnp
        _rk = jax.random.key(seed)
        x = 7.22e-05 + 1 * jax.random.normal(jax.random.fold_in(_rk, 1), (8, 128, 128), jnp.float32)
        _lenS = 128 - jax.random.randint(jax.random.fold_in(_rk, 7), (8,), 0, max(1, 128 // 4) + 1, jnp.int32)
        _lenS2 = 128 - jax.random.randint(jax.random.fold_in(_rk, 8), (8,), 0, max(1, 128 // 4) + 1, jnp.int32)
        cond_1024 = 0.0061147 + 1.02565 * jax.random.normal(jax.random.fold_in(_rk, 11), (8, 128), jnp.float32)
        return (x, cond_1024)
    x, cond_1024 = _rec_inputs()

    def _L0_cond_setup():
        import jax, jax.numpy as jnp
        import numpy as np
        C = 128
        H = 16
        HD = C // H
        DFF = 4 * C
        EPS = 1e-06
        ROPE_BASE = 10000.0

        def _ln(t):
            m = jnp.mean(t, axis=-1, keepdims=True)
            v = jnp.mean(jnp.square(t - m), axis=-1, keepdims=True)
            return (t - m) * jax.lax.rsqrt(v + EPS)

        def _rope_cos_sin(L, dtype):
            inv_freq = 1.0 / ROPE_BASE ** (jnp.arange(0, HD, 2, dtype=jnp.float32) / HD)
            freqs = jnp.arange(L, dtype=jnp.float32)[:, None] * inv_freq[None, :]
            emb = jnp.concatenate([freqs, freqs], axis=-1)
            return (jnp.cos(emb)[None, :, None, :].astype(dtype), jnp.sin(emb)[None, :, None, :].astype(dtype))

        def _rotate_half(t):
            t1, t2 = jnp.split(t, 2, axis=-1)
            return jnp.concatenate([-t2, t1], axis=-1)
        key = jax.random.key(seed)
        ks = jax.random.split(key, 16)
        B, L = (4, 256)
        s = 0.02
        return {'x': jax.random.normal(ks[0], (B, L, C), jnp.float32), 'cond': jax.random.normal(ks[1], (B, C), jnp.float32), 'ada_w': jax.random.normal(ks[2], (6 * C, C), jnp.float32) * s, 'ada_b': jnp.zeros((6 * C,), jnp.float32), 'qkv_w': jax.random.normal(ks[3], (3 * C, C), jnp.float32) * s, 'qkv_b': jnp.zeros((3 * C,), jnp.float32), 'proj_w': jax.random.normal(ks[4], (C, C), jnp.float32) * s, 'proj_b': jnp.zeros((C,), jnp.float32), 'fc1_w': jax.random.normal(ks[5], (DFF, C), jnp.float32) * s, 'fc1_b': jnp.zeros((DFF,), jnp.float32), 'fc2_w': jax.random.normal(ks[6], (C, DFF), jnp.float32) * s, 'fc2_b': jnp.zeros((C,), jnp.float32)}
    _L0_cond_all = _L0_cond_setup()
    _L0_cond_in = {k: v for k, v in _L0_cond_all.items() if k in ('ada_w', 'ada_b', 'qkv_w', 'qkv_b', 'proj_w', 'proj_b', 'fc1_w', 'fc1_b', 'fc2_w', 'fc2_b')}
    del _L0_cond_all

    def _L1_cond_setup():
        import jax, jax.numpy as jnp
        import numpy as np
        B, N, D = (2, 256, 128)
        H, HD = (16, 64)
        E, DD = (8, 512)
        EPS = 1e-05

        def _ln(x, g, b):
            m = jnp.mean(x, axis=-1, keepdims=True)
            v = jnp.var(x, axis=-1, keepdims=True)
            return (x - m) * jax.lax.rsqrt(v + EPS) * g + b
        key = jax.random.key(seed)
        ks = jax.random.split(key, 16)
        s = 0.02
        return {'x': jax.random.normal(ks[0], (B, N, D), jnp.float32), 't': jax.random.normal(ks[1], (B, 1, D), jnp.float32), 'W_ada': jax.random.normal(ks[2], (D, D), jnp.float32) * s, 'b_ada': jnp.zeros((D,), jnp.float32), 'ln1_g': jnp.ones((D,), jnp.float32), 'ln1_b': jnp.zeros((D,), jnp.float32), 'Wqkv': jax.random.normal(ks[3], (3 * H * HD, D), jnp.float32) * s, 'qn_g': jnp.ones((HD,), jnp.float32), 'qn_b': jnp.zeros((HD,), jnp.float32), 'kn_g': jnp.ones((HD,), jnp.float32), 'kn_b': jnp.zeros((HD,), jnp.float32), 'Wout': jax.random.normal(ks[4], (D, H * HD), jnp.float32) * s, 'mlp_g': jnp.ones((D,), jnp.float32), 'mlp_b': jnp.zeros((D,), jnp.float32), 'Wgate': jax.random.normal(ks[5], (E, D), jnp.float32) * s, 'fc1s': jax.random.normal(ks[6], (E, DD, D), jnp.float32) * s, 'b1s': jnp.zeros((E, DD), jnp.float32), 'fc2s': jax.random.normal(ks[7], (E, D, DD), jnp.float32) * s, 'b2s': jnp.zeros((E, D), jnp.float32)}
    _L1_cond_all = _L1_cond_setup()
    _L1_cond_in = {k: v for k, v in _L1_cond_all.items() if k in ('W_ada', 'b_ada', 'ln1_g', 'ln1_b', 'Wqkv', 'qn_g', 'qn_b', 'kn_g', 'kn_b', 'Wout', 'mlp_g', 'mlp_b', 'Wgate', 'fc1s', 'b1s', 'fc2s', 'b2s')}
    del _L1_cond_all
    return {'x': x, 'cond_1024': cond_1024, 'L0_cond_ada_w': _L0_cond_in['ada_w'], 'L0_cond_ada_b': _L0_cond_in['ada_b'], 'L0_cond_qkv_w': _L0_cond_in['qkv_w'], 'L0_cond_qkv_b': _L0_cond_in['qkv_b'], 'L0_cond_proj_w': _L0_cond_in['proj_w'], 'L0_cond_proj_b': _L0_cond_in['proj_b'], 'L0_cond_fc1_w': _L0_cond_in['fc1_w'], 'L0_cond_fc1_b': _L0_cond_in['fc1_b'], 'L0_cond_fc2_w': _L0_cond_in['fc2_w'], 'L0_cond_fc2_b': _L0_cond_in['fc2_b'], 'L1_cond_W_ada': _L1_cond_in['W_ada'], 'L1_cond_b_ada': _L1_cond_in['b_ada'], 'L1_cond_ln1_g': _L1_cond_in['ln1_g'], 'L1_cond_ln1_b': _L1_cond_in['ln1_b'], 'L1_cond_Wqkv': _L1_cond_in['Wqkv'], 'L1_cond_qn_g': _L1_cond_in['qn_g'], 'L1_cond_qn_b': _L1_cond_in['qn_b'], 'L1_cond_kn_g': _L1_cond_in['kn_g'], 'L1_cond_kn_b': _L1_cond_in['kn_b'], 'L1_cond_Wout': _L1_cond_in['Wout'], 'L1_cond_mlp_g': _L1_cond_in['mlp_g'], 'L1_cond_mlp_b': _L1_cond_in['mlp_b'], 'L1_cond_Wgate': _L1_cond_in['Wgate'], 'L1_cond_fc1s': _L1_cond_in['fc1s'], 'L1_cond_b1s': _L1_cond_in['b1s'], 'L1_cond_fc2s': _L1_cond_in['fc2s'], 'L1_cond_b2s': _L1_cond_in['b2s']}

def reference(x, cond_1024, L0_cond_ada_w, L0_cond_ada_b, L0_cond_qkv_w, L0_cond_qkv_b, L0_cond_proj_w, L0_cond_proj_b, L0_cond_fc1_w, L0_cond_fc1_b, L0_cond_fc2_w, L0_cond_fc2_b, L1_cond_W_ada, L1_cond_b_ada, L1_cond_ln1_g, L1_cond_ln1_b, L1_cond_Wqkv, L1_cond_qn_g, L1_cond_qn_b, L1_cond_kn_g, L1_cond_kn_b, L1_cond_Wout, L1_cond_mlp_g, L1_cond_mlp_b, L1_cond_Wgate, L1_cond_fc1s, L1_cond_b1s, L1_cond_fc2s, L1_cond_b2s):
    import jax
    import jax.numpy as jnp

    def _L0_cond_ref(x, cond, ada_w, ada_b, qkv_w, qkv_b, proj_w, proj_b, fc1_w, fc1_b, fc2_w, fc2_b):
        import jax, jax.numpy as jnp
        import numpy as np
        C = 128
        H = 16
        HD = C // H
        DFF = 4 * C
        EPS = 1e-06
        ROPE_BASE = 10000.0

        def _ln(t):
            m = jnp.mean(t, axis=-1, keepdims=True)
            v = jnp.mean(jnp.square(t - m), axis=-1, keepdims=True)
            return (t - m) * jax.lax.rsqrt(v + EPS)

        def _rope_cos_sin(L, dtype):
            inv_freq = 1.0 / ROPE_BASE ** (jnp.arange(0, HD, 2, dtype=jnp.float32) / HD)
            freqs = jnp.arange(L, dtype=jnp.float32)[:, None] * inv_freq[None, :]
            emb = jnp.concatenate([freqs, freqs], axis=-1)
            return (jnp.cos(emb)[None, :, None, :].astype(dtype), jnp.sin(emb)[None, :, None, :].astype(dtype))

        def _rotate_half(t):
            t1, t2 = jnp.split(t, 2, axis=-1)
            return jnp.concatenate([-t2, t1], axis=-1)
        B, L, _ = x.shape
        ada = jax.nn.silu(cond) @ ada_w.T + ada_b
        g1, g2, s1, s2, sh1, sh2 = [a[:, None, :] for a in jnp.split(ada, 6, axis=-1)]
        h = _ln(x) * (1.0 + s1) + sh1
        qkv = (h @ qkv_w.T + qkv_b).reshape(B, L, 3, H, HD)
        q, k, v = (qkv[:, :, 0], qkv[:, :, 1], qkv[:, :, 2])
        cos, sin = _rope_cos_sin(L, x.dtype)
        q = q * cos + _rotate_half(q) * sin
        k = k * cos + _rotate_half(k) * sin
        scale = 1.0 / np.sqrt(HD)
        scores = jnp.einsum('bqhd,bkhd->bhqk', q, k) * scale
        attn = jax.nn.softmax(scores, axis=-1)
        o = jnp.einsum('bhqk,bkhd->bqhd', attn, v).reshape(B, L, C)
        x = x + (o @ proj_w.T + proj_b) * g1
        h2 = _ln(x) * (1.0 + s2) + sh2
        ff = jax.nn.gelu(h2 @ fc1_w.T + fc1_b, approximate=True) @ fc2_w.T + fc2_b
        return x + ff * g2

    def _L1_cond_ref(x, t, W_ada, b_ada, ln1_g, ln1_b, Wqkv, qn_g, qn_b, kn_g, kn_b, Wout, mlp_g, mlp_b, Wgate, fc1s, b1s, fc2s, b2s):
        import jax, jax.numpy as jnp
        import numpy as np
        B, N, D = (2, 256, 128)
        H, HD = (16, 64)
        E, DD = (8, 512)
        EPS = 1e-05

        def _ln(x, g, b):
            m = jnp.mean(x, axis=-1, keepdims=True)
            v = jnp.var(x, axis=-1, keepdims=True)
            return (x - m) * jax.lax.rsqrt(v + EPS) * g + b
        b, n, d = x.shape
        shift = jax.nn.silu(t) @ W_ada.T + b_ada
        h = _ln(x, ln1_g, ln1_b) + shift
        qkv = (h @ Wqkv.T).reshape(b, n, 3, H, HD)
        q = _ln(qkv[:, :, 0].transpose(0, 2, 1, 3), qn_g, qn_b)
        k = _ln(qkv[:, :, 1].transpose(0, 2, 1, 3), kn_g, kn_b)
        v = qkv[:, :, 2].transpose(0, 2, 1, 3)
        scores = jnp.einsum('bhnd,bhmd->bhnm', q, k) / jnp.sqrt(jnp.float32(HD))
        attn = jax.nn.softmax(scores, axis=-1)
        o = jnp.einsum('bhnm,bhmd->bhnd', attn, v)
        o = o.transpose(0, 2, 1, 3).reshape(b, n, H * HD)
        x = x + o @ Wout.T
        tok = x.reshape(-1, d)
        bs = tok.shape[0]
        gate = jax.nn.softmax(tok @ Wgate.T, axis=-1)
        k_cap = bs // E
        vals, idx = jax.lax.top_k(gate.T, k_cap)
        idx_flat = idx.T.reshape(-1)
        w = vals.T
        g = _ln(tok[idx_flat], mlp_g, mlp_b).reshape(k_cap, E, d)
        y = jnp.einsum('ked,ehd->keh', g, fc1s) + b1s
        y = jax.nn.gelu(y, approximate=True)
        y = jnp.einsum('keh,edh->ked', y, fc2s) + b2s
        y = y * w[..., None]
        tok = tok.at[idx_flat].add(y.reshape(-1, d))
        return tok.reshape(x.shape)
    x = _L0_cond_ref(x, cond_1024, L0_cond_ada_w, L0_cond_ada_b, L0_cond_qkv_w, L0_cond_qkv_b, L0_cond_proj_w, L0_cond_proj_b, L0_cond_fc1_w, L0_cond_fc1_b, L0_cond_fc2_w, L0_cond_fc2_b)
    x = _L1_cond_ref(x, cond_1024[:, None, :], L1_cond_W_ada, L1_cond_b_ada, L1_cond_ln1_g, L1_cond_ln1_b, L1_cond_Wqkv, L1_cond_qn_g, L1_cond_qn_b, L1_cond_kn_g, L1_cond_kn_b, L1_cond_Wout, L1_cond_mlp_g, L1_cond_mlp_b, L1_cond_Wgate, L1_cond_fc1s, L1_cond_b1s, L1_cond_fc2s, L1_cond_b2s)
    return x

_drawn_inputs = setup_inputs


def setup_inputs(seed=0):
    import zlib

    import numpy as np

    out = dict(_drawn_inputs(seed))
    spreads = {'L0_cond_ada_b': (0.0, 0.558),
     'L0_cond_qkv_b': (0.0, 0.8),
     'L0_cond_proj_b': (0.0, 0.443),
     'L0_cond_fc1_b': (0.0, 0.8),
     'L0_cond_fc2_b': (0.0, 0.542),
     'L1_cond_b_ada': (0.0, 0.543),
     'L1_cond_ln1_g': (1.0, 0.6),
     'L1_cond_ln1_b': (0.0, 0.526),
     'L1_cond_qn_g': (1.0, 0.6),
     'L1_cond_qn_b': (0.0, 0.8),
     'L1_cond_kn_g': (1.0, 0.6),
     'L1_cond_kn_b': (0.0, 0.8),
     'L1_cond_mlp_g': (1.0, 0.6),
     'L1_cond_mlp_b': (0.0, 0.8),
     'L1_cond_b1s': (0.0, 0.8),
     'L1_cond_b2s': (0.0, 0.468)}
    factors = {'L0_cond_ada_w': 2.738,
     'L0_cond_qkv_w': 8.0,
     'L0_cond_proj_w': 8.0,
     'L0_cond_fc1_w': 6.354,
     'L0_cond_fc2_w': 6.0,
     'L1_cond_W_ada': 2.878,
     'L1_cond_Wgate': 2.991,
     'L1_cond_fc1s': 5.752,
     'L1_cond_fc2s': 5.192}
    for name, (base, spread) in spreads.items():
        noise = np.random.default_rng([zlib.crc32(name.encode()), seed]).standard_normal(out[name].shape)
        drawn = base * np.exp(spread * noise) if base else spread * noise
        out[name] = jnp.asarray(drawn.astype(out[name].dtype))
    for name, factor in factors.items():
        out[name] = (out[name] * factor).astype(out[name].dtype)
    return out
```

```python
from contextlib import ExitStack

import concourse.bass as bass
import numpy as np
from concourse import mybir

F32 = mybir.dt.float32
BF16 = mybir.dt.bfloat16
I32 = mybir.dt.int32
ALU = mybir.AluOpType
ACT = mybir.ActivationFunctionType
AX = mybir.AxisListType.X

P = 128
B, L, C = 8, 128, 128
NG = 4
HG = 4
H = NG * HG
HD0, HD1 = C // H, 64
DFF = 4 * C
NCH = DFF // P
E = 8
CAP = B * L // E
EPS0, EPS1 = 1e-6, 1e-5
KEY_HALF = 15

COLS = {}
_at = 0
for _name, _n in (("cond", B), ("ada_b", 6), ("fc1_b", NCH), ("b_ada", 1), ("ln1_g", 1), ("ln1_b", 1),
                  ("qn_g", 1), ("qn_b", 1), ("kn_g", 1), ("kn_b", 1), ("mlp_g", 1), ("mlp_b", 1),
                  ("b1s", E * NCH), ("wgate", E)):
    COLS[_name] = (_at, _at + _n)
    _at += _n
N_COLS = _at
ROWS = {}
_at = 0
for _name, _n in (("qkv_b", 3 * C), ("proj_b", C), ("fc2_b", C), ("ada_b", 2 * C), ("b2s", E * C)):
    ROWS[_name] = (_at, _at + _n)
    _at += _n
N_ROWS = _at
CONST = {}
_at = 0
for _name, _n in (("ident", P), ("before", P), ("iota1", P), ("cos", HD0), ("sin", HD0), ("mask", H), ("same", P),
                  ("bits", KEY_HALF), ("steps", KEY_HALF)):
    CONST[_name] = (_at, _at + _n)
    _at += _n
N_CONST = _at


def wait(eng, sem, count):
    if isinstance(count, int) and count <= 0:
        return
    eng.wait_ge(sem, count)


def back(b, g, lag):
    g -= lag
    while g < 0:
        g += NG
        b = b - 1
    return b, g


def real(b):
    return not isinstance(b, int) or 0 <= b < B


def at(ap, b):
    return ap.unsqueeze(2)[:, b, :]


def bc(ap, shape, axis):
    return ap.unsqueeze(axis).broadcast_to(shape)


def program(nc, t):
    with ExitStack() as ctx:
        def sb(name, shape, dt=F32):
            return ctx.enter_context(nc.sbuf_tensor(name, [P] + shape, dt))

        def sem(name):
            return ctx.enter_context(nc.semaphore(name))

        bank = [ctx.enter_context(nc.psum_tensor(f"bank{i}", [P, 512], F32)) for i in range(8)]

        x = sb("x_sb", [B, C])
        cols, rows, const = sb("cols_sb", [N_COLS]), sb("rows_sb", [N_ROWS]), sb("const_sb", [N_CONST])
        ada_w, w_ada = sb("ada_w_sb", [6 * C]), sb("w_ada_sb", [C])
        qkv_w, proj_w = sb("qkv_w_sb", [3 * C]), sb("proj_w_sb", [C])
        fc1_w, fc2_w = sb("fc1_w_sb", [DFF]), sb("fc2_w_sb", [NCH, C])
        wqk, wv = sb("wqk_sb", [NG, 2 * HG * HD1]), sb("wv_sb", [NG, HG * HD1])
        wout = sb("wout_sb", [2 * NG, C])
        fc1s, fc2s = sb("fc1s_sb", [E, DFF]), sb("fc2s_sb", [E, NCH, C])

        def col(name, i=0, n=1):
            return cols[:, COLS[name][0] + i:COLS[name][0] + i + n]

        def row(name):
            return rows[:, ROWS[name][0]:ROWS[name][1]]

        def cst(name):
            return const[:, CONST[name][0]:CONST[name][1]]

        ident = cst("ident")

        silu_c = sb("silu_c", [B])
        mod = sb("mod", [4, B])
        shift1 = sb("shift1", [B])
        gates = sb("gates", [B, 2 * C])
        pg1, fg2 = sb("pg1", [B, C]), sb("fg2", [B, C])

        stats, mv = sb("stats", [B, 6]), sb("mv", [B, 2])
        var_eps, rstd = sb("var_eps", [B]), sb("rstd", [B])
        minus_half = sb("minus_half", [B])
        z = sb("z", [C])
        hT = sb("hT", [L])

        qkv0 = sb("qkv0", [3 * C])
        rope_a, rope_b, roped = sb("rope_a", [2 * C]), sb("rope_b", [2 * C]), sb("roped", [2 * C])
        qkT0 = sb("qkT0", [2, L])
        kx = sb("kx", [NG, HG, L])
        v0 = sb("v0", [H, HD0 + 1])
        smax = sb("smax", [NG, HG])
        prob = sb("prob", [NG, HG * L])
        probT = sb("probT", [2, HG * L])
        rsum = sb("rsum", [NG, HG])
        o0 = sb("o0", [C])
        oT0 = sb("oT0", [L])
        delta = sb("delta", [C])
        z4, h4T = sb("z4", [NG, C]), sb("h4T", [NG * L])
        hid = sb("hid", [NCH, NG * L])

        wsum = sb("wsum", [2 * H])
        sq, sumsq, head_var, head_rstd = sb("sq", [2 * HG * HD1]), sb("sumsq", [2 * HG]), sb("head_var", [2 * HG]), sb("head_rstd", [2 * HG])
        qkn = sb("qkn", [2 * HG * HD1])
        qkT1 = sb("qkT1", [NG, HG, L])
        v1 = sb("v1", [NG, HG, HD1 + 1])
        o1 = sb("o1", [HG * HD1])
        oT1 = sb("oT1", [2 * NG, L])
        NT = B
        NTE = NT * E
        xT = fg2[:].rearrange("p b c -> p (b c)")
        zx, zr = gates[:, 0:NT // 2, :].rearrange("p b (a c) -> p (b a) c", a=2), pg1[:]
        xgT = qkT1[:, 0:NG // 2, :, :].rearrange("p g h l -> p (g h) l")
        gate, gate_max, gate_sum = sb("gate", [NTE]), sb("gate_max", [NT]), sb("gate_sum", [NT])
        keys, key_hi, key_lo, key_i = sb("keys", [P]), sb("key_hi", [P]), sb("key_lo", [P]), sb("key_i", [2, P], I32)
        above, eq_part = sb("above", [P]), sb("eq_part", [P])
        hits, count = sb("hits", [P], BF16), sb("count", [1], BF16)
        cand, cand_low, step_up = sb("cand", [1]), sb("cand_low", [1]), sb("step_up", [1])
        masksT = sb("masksT", [2, P], BF16)
        masks = sb("masks", [2, NTE], BF16)
        tied = sb("tied", [NTE], BF16)
        chosen = sb("chosen", [NTE], BF16)
        slot1 = sb("slot1", [NTE])
        ident_b, before_b, ones_b = sb("ident_b", [P], BF16), sb("before_b", [P], BF16), sb("ones_b", [P], BF16)
        iota_b, same_b = sb("iota_b", [P], BF16), sb("same_b", [P], BF16)
        S = sb("S", [NT, E, CAP], BF16)
        ST = sb("ST", [E, NT * P], BF16)
        zpart = sb("zpart", [3, NT, C], BF16)
        gr, gpart = sb("gr", [NTE]), sb("gpart", [NTE, 3], BF16)
        weight = sb("weight", [E])
        hidE = hid[:].rearrange("p c (e s) -> p e c s", e=NG)
        yb, yw, yr = sb("yb", [2, C]), sb("yw", [2, C]), sb("yr", [2, 2, C])
        ypart = kx[:, 0:3, :, :].rearrange("p g h l -> p g (h l)").bitcast(BF16).rearrange("p g (e c) -> p g e c", e=E)

        s_x, s_small, s_l0, s_l1, s_moe = sem("x_loaded"), sem("small_loaded"), sem("l0_loaded"), sem("l1_loaded"), sem("moe_loaded")
        silu_done, ada_ready, mod_done, gates_ready, gates_done = sem("silu_done"), sem("ada_ready"), sem("mod_done"), sem("gates_ready"), sem("gates_done")
        consts_set, stat_link, var_done, rstd_done = sem("consts_set"), sem("stat_link"), sem("var_done"), sem("rstd_done")
        z_ready, zT_ready, hT_ready, qkv_ready, qkv_saved = sem("z_ready"), sem("zT_ready"), sem("hT_ready"), sem("qkv_ready"), sem("qkv_saved")
        rope_link, roped_done, qkT_ready, qkT_done, kx_done, v_done = sem("rope_link"), sem("roped_done"), sem("qkT_ready"), sem("qkT_done"), sem("kx_done"), sem("v_done")
        s_ready, max_done, sub_done, exp_done = sem("s_ready"), sem("max_done"), sem("sub_done"), sem("exp_done")
        pT_ready, pT_done, o_ready, rec_done, o_done = sem("pT_ready"), sem("pT_done"), sem("o_ready"), sem("rec_done"), sem("o_done")
        oT_ready, oT_done, proj_ready, xb_done, gated_done, res_done = sem("oT_ready"), sem("oT_done"), sem("proj_ready"), sem("xb_done"), sem("gated_done"), sem("res_done")
        z4_done, z4T_ready, h4T_done, hid_ready, hid_done, ff_ready = sem("z4_done"), sem("z4T_ready"), sem("h4T_done"), sem("hid_ready"), sem("hid_done"), sem("ff_ready")
        ffg_done, l0_done, xf_done = sem("ffg_done"), sem("l0_done"), sem("xf_done")
        wsum_done, wqk_done, z1_ready, z1T_ready, h1T_done, qkv1_ready = sem("wsum_done"), sem("wqk_done"), sem("z1_ready"), sem("z1T_ready"), sem("h1T_done"), sem("qkv1_ready")
        squared, sumsq_done, hvar_done, hrstd_done, qkn_done, v1_done = sem("squared"), sem("sumsq_done"), sem("hvar_done"), sem("hrstd_done"), sem("qkn_done"), sem("v1_done")
        qkT1_ready, qkT1_done, s1_ready, max1_done, sub1_done, exp1_done = sem("qkT1_ready"), sem("qkT1_done"), sem("s1_ready"), sem("max1_done"), sem("sub1_done"), sem("exp1_done")
        pT1_ready, pT1_done, o1_ready, rec1_done, o1_done = sem("pT1_ready"), sem("pT1_done"), sem("o1_ready"), sem("rec1_done"), sem("o1_done")
        oT1_ready, oT1_done, proj1_ready, res1_done = sem("oT1_ready"), sem("oT1_done"), sem("proj1_ready"), sem("res1_done")
        xT_ready, xT_done, logits_ready, gate_link, gate_exp, gate_done = sem("xT_ready"), sem("xT_done"), sem("logits_ready"), sem("gate_link"), sem("gate_exp"), sem("gate_done")
        gateT_ready, key_link, counted, totalled, cand_link, narrowed = sem("gateT_ready"), sem("key_link"), sem("counted"), sem("totalled"), sem("cand_link"), sem("narrowed")
        masksT_done, masks_ready, masks_done, tie_rank_ready, chosen_link, chosen_done = sem("masksT_done"), sem("masks_ready"), sem("masks_done"), sem("tie_rank_ready"), sem("chosen_link"), sem("chosen_done")
        slots_ready, slots_done, s_dve, s_pool, cast_done = sem("slots_ready"), sem("slots_done"), sem("s_dve"), sem("s_pool"), sem("cast_done")
        zx_done, zcast, zrest, gcast, grest = sem("zx_done"), sem("zcast"), sem("zrest"), sem("gcast"), sem("grest")
        gathered, xgT_done, weight_ready, weight_done, st_ready, st_act, st_dve = sem("gathered"), sem("xgT_done"), sem("weight_ready"), sem("weight_done"), sem("st_ready"), sem("st_act"), sem("st_dve")
        hidE_ready, hidE_done, y_ready, yb_done, yw_done, scattered, final_done = sem("hidE_ready"), sem("hidE_done"), sem("y_ready"), sem("yb_done"), sem("yw_done"), sem("scattered"), sem("final_done")
        y_link, xT_done2 = sem("y_link"), sem("xT_done2")
        s_out = sem("out_stored")

        qkv_ps, tp_ps, pT_ps, o_ps, misc_ps = bank[0], bank[1], bank[4], bank[5], bank[6]
        s_ps = [bank[2], bank[3]]
        v_ps, tp1_ps = bank[1], bank[7]

        block = ctx.enter_context(nc.Block())

        @block.sync
        def _(sp):
            sp.dma_start(x[:], t["x"].rearrange("b t c -> t b c")).then_inc(s_x, 16)
            sp.dma_start(cols[:], t["cols"]).then_inc(s_small, 16)
            sp.dma_start(ada_w[:], t["ada_w"]).then_inc(s_small, 16)
            sp.dma_start(w_ada[:], t["w_ada"]).then_inc(s_small, 16)
            sp.dma_start(const[:], t["consts"]).then_inc(s_small, 16)
            sp.dma_start(rows[:], t["rows"].partition_broadcast(P)).then_inc(s_small, 16)
            sp.dma_start(qkv_w[:], t["qkv_w"]).then_inc(s_l0, 16)
            sp.dma_start(proj_w[:], t["proj_w"]).then_inc(s_l0, 16)
            sp.dma_start(fc1_w[:], t["fc1_w"]).then_inc(s_l0, 16)
            sp.dma_start(fc2_w[:], t["fc2_w"]).then_inc(s_l0, 16)
            sp.dma_start(wqk[:], t["wqk"]).then_inc(s_l1, 16)
            sp.dma_start(wv[:], t["wv"]).then_inc(s_l1, 16)
            sp.dma_start(wout[:], t["wout"]).then_inc(s_l1, 16)
            sp.dma_start(fc1s[:], t["fc1s"]).then_inc(s_moe, 16)
            sp.dma_start(fc2s[:], t["fc2s"]).then_inc(s_moe, 16)
            for i in range(2):
                sp.wait_ge(final_done, NT // 2 * (i + 1))
                half = slice(i * NT // 2, (i + 1) * NT // 2)
                sp.dma_start(t["out"][half].rearrange("b t c -> t b c"), x[:, half, :]).then_inc(s_out, 16)
            sp.wait_ge(s_out, 32)

        @block.tensor
        def _(pe):
            pe.wait_ge(s_small, 80)
            pe.wait_ge(silu_done, 1)
            for i, chunk in enumerate((2, 3, 4, 5)):
                pe.matmul(bank[7][:, i * B:(i + 1) * B], ada_w[:, chunk * C:(chunk + 1) * C], silu_c[:], start=True, stop=True)
            pe.matmul(bank[7][:, 4 * B:5 * B], w_ada[:], silu_c[:], start=True, stop=True).then_inc(ada_ready, 1)
            for b in range(B):
                pe.matmul(bank[b // 2][:, (b % 2) * 2 * C:(b % 2 + 1) * 2 * C], silu_c[:, b:b + 1].broadcast_to([P, P]),
                          ada_w[:, 0:2 * C], start=True, stop=True).then_inc(gates_ready, 1)
            pe.wait_ge(s_l0, 64)
            pe.wait_ge(gates_done, 4)

            def zT(b):
                pe.wait_ge(z_ready, b + 1)
                pe.transpose(misc_ps[:, 0:L], z[:], ident).then_inc(zT_ready, 1)

            def qkv(b):
                pe.wait_ge(hT_ready, b + 1)
                wait(pe, qkv_saved, b)
                pe.matmul(qkv_ps[:, 0:3 * C], hT[:], qkv_w[:], start=True, stop=True).then_inc(qkv_ready, 1)

            def qkT(b):
                pe.wait_ge(roped_done, b + 1)
                wait(pe, qkT_done, b)
                pe.transpose(tp_ps[:, 0:L], roped[:, 0:C], ident)
                pe.transpose(tp_ps[:, L:2 * L], roped[:, C:2 * C], ident).then_inc(qkT_ready, 1)

            def scores(b, g):
                n = NG * b + g
                pe.wait_ge(kx_done, n + 1)
                wait(pe, sub_done, n - 1)
                pe.matmul(s_ps[g % 2][:], qkT0[:, 0, :], kx[:, g, :, :], start=True, stop=True).then_inc(s_ready, 1)

            def probsT(b, g):
                n = NG * b + g
                pe.wait_ge(exp_done, n + 1)
                wait(pe, pT_done, n)
                for i in range(HG):
                    tr = pe.transpose(pT_ps[:, i * L:(i + 1) * L], prob[:, g, i * L:(i + 1) * L], ident)
                tr.then_inc(pT_ready, 1)

            def values(b, g):
                n = NG * b + g
                pe.wait_ge(pT_done, n + 1)
                pe.wait_ge(v_done, b + 1)
                wait(pe, o_done, n)
                for i in range(HG):
                    mm = pe.matmul(o_ps[:, i * (HD0 + 1):(i + 1) * (HD0 + 1)], probT[:, g % 2, i * L:(i + 1) * L],
                                   v0[:, g * HG + i, :], start=True, stop=True)
                mm.then_inc(o_ready, 1)

            def oT(b):
                pe.wait_ge(o_done, NG * (b + 1))
                pe.transpose(misc_ps[:, 0:L], o0[:], ident).then_inc(oT_ready, 1)

            def proj(b):
                pe.wait_ge(oT_done, b + 1)
                pe.matmul(misc_ps[:, 0:C], oT0[:], proj_w[:], start=True, stop=True).then_inc(proj_ready, 1)

            def step(b, ahead):
                for g in range(NG):
                    late = back(b, g, 2)
                    if real(late[0]):
                        probsT(*late)
                    if g == 1 and ahead:
                        qkv(b + 1)
                    if real(b):
                        scores(b, g)
                    if real(late[0]):
                        values(*late)
                    if g == 0 and ahead:
                        zT(b + 1)
                    if g == 1 and real(b - 1):
                        oT(b - 1)
                    if g == 2 and real(b - 1):
                        proj(b - 1)
                    if g == 3 and ahead:
                        qkT(b + 1)

            zT(0)
            qkv(0)
            qkT(0)
            step(0, True)
            step(1, True)
            with pe.Fori(2, B - 1) as b:
                step(b, True)
            step(B - 1, False)
            step(B, False)
            for half in range(2):
                pe.wait_ge(z4_done, NG * (half + 1))
                wait(pe, h4T_done, NG * half)
                for i in range(NG):
                    tr = pe.transpose(tp_ps[:, i * L:(i + 1) * L], z4[:, i, :], ident)
                tr.then_inc(z4T_ready, 1)
                pe.wait_ge(h4T_done, NG * (half + 1))
                for c in range(NCH):
                    n = NCH * half + c
                    wait(pe, hid_done, n - 1)
                    pe.matmul(s_ps[c % 2][:], fc1_w[:, c * P:(c + 1) * P], h4T[:], start=True, stop=True).then_inc(hid_ready, 1)
                pe.wait_ge(hid_done, NCH * (half + 1))
                for i in range(NG):
                    n = NG * half + i
                    wait(pe, ffg_done, n - 1)
                    for c in range(NCH):
                        mm = pe.matmul((o_ps, misc_ps)[i % 2][:, 0:C], hid[:, c, i * L:(i + 1) * L], fc2_w[:, c, :],
                                       start=(c == 0), stop=(c == NCH - 1))
                    mm.then_inc(ff_ready, 1)

            def z1T(b):
                pe.wait_ge(z1_ready, b + 1)
                wait(pe, oT1_done, NG * (b - 1))
                pe.transpose(misc_ps[:, 0:L], z[:], ident).then_inc(z1T_ready, 1)

            def qkv1(b, g):
                n = NG * b + g
                pe.wait_ge(h1T_done, b + 1)
                wait(pe, qkn_done, n)
                wait(pe, v1_done, n)
                pe.matmul(qkv_ps[:], hT[:], wqk[:, g, :], start=True, stop=True)
                pe.matmul(v_ps[:, 0:HG * HD1], hT[:], wv[:, g, :], start=True, stop=True).then_inc(qkv1_ready, 1)

            def qk1T(b, g):
                n = NG * b + g
                pe.wait_ge(qkn_done, n + 1)
                wait(pe, qkT1_done, 2 * n)
                for i in range(HG):
                    tr = pe.transpose(tp1_ps[:, i * L:(i + 1) * L], qkn[:, i * P:(i + 1) * P], ident)
                tr.then_inc(qkT1_ready, 1)

            def scores1(b, g):
                n = NG * b + g
                pe.wait_ge(qkT1_done, 2 * n + 2)
                wait(pe, sub1_done, n)
                for i in range(2):
                    for odd in range(2):
                        rows_ = slice(odd * HD1, (odd + 1) * HD1)
                        mm = pe.matmul(s_ps[odd][:, i * L:(i + 1) * L], qkT1[rows_, g, i, :], qkT1[rows_, g, 2 + i, :], start=True, stop=True)
                mm.then_inc(s1_ready, 1)

            def probs1T(b, g):
                n = NG * b + g
                pe.wait_ge(exp1_done, n + 1)
                wait(pe, pT1_done, n)
                for i in range(HG):
                    tr = pe.transpose(pT_ps[:, i * L:(i + 1) * L], prob[:, g, i * L:(i + 1) * L], ident)
                tr.then_inc(pT1_ready, 1)

            def values1(b, g):
                n = NG * b + g
                pe.wait_ge(pT1_done, n + 1)
                wait(pe, o1_done, n)
                for i in range(HG):
                    mm = pe.matmul(o_ps[:, i * (HD1 + 1):(i + 1) * (HD1 + 1)], probT[:, g % 2, i * L:(i + 1) * L],
                                   v1[:, g, i, :], start=True, stop=True)
                mm.then_inc(o1_ready, 1)

            def o1T(b, g):
                n = NG * b + g
                pe.wait_ge(o1_done, n + 1)
                if g == 0:
                    wait(pe, res1_done, b)
                    if not isinstance(b, int) or b + 1 < B:
                        pe.wait_ge(h1T_done, b + 2)
                else:
                    wait(pe, oT1_done, n)
                for i in range(2):
                    tr = pe.transpose(misc_ps[:, i * L:(i + 1) * L], o1[:, i * P:(i + 1) * P], ident)
                tr.then_inc(oT1_ready, 1)

            def proj1(b):
                pe.wait_ge(oT1_done, NG * (b + 1))
                if not isinstance(b, int) or b + 2 < B:
                    pe.wait_ge(h1T_done, b + 3)
                for i in range(2 * NG):
                    mm = pe.matmul(misc_ps[:, 0:C], oT1[:, i, :], wout[:, i, :], start=(i == 0), stop=(i == 2 * NG - 1))
                mm.then_inc(proj1_ready, 1)

            def step1(b, ahead):
                for g in range(NG):
                    one, two, three = (back(b, g, lag) for lag in (1, 2, 3))
                    if real(three[0]):
                        probs1T(*three)
                    if real(two[0]):
                        scores1(*two)
                    if real(b):
                        qkv1(b, g)
                    if g == NG - 1 and ahead:
                        z1T(b + 1)
                    if real(three[0]):
                        values1(*three)
                    if real(one[0]):
                        qk1T(*one)
                    if g == NG - 1 and real(b - 1):
                        proj1(b - 1)
                    if real(three[0]):
                        o1T(*three)

            pe.wait_ge(wqk_done, 1)
            z1T(0)
            step1(0, True)
            step1(1, True)
            with pe.Fori(2, B - 1) as b:
                step1(b, True)
            step1(B - 1, False)
            step1(B, False)

            pe.wait_ge(res1_done, B)
            for i in range(2):
                for j in range(NG):
                    tr = pe.transpose(bank[i][:, j * P:(j + 1) * P], x[:, NG * i + j, :], ident)
                tr.then_inc(xT_ready, 1)
            for i in range(NT):
                pe.wait_ge((xT_done, xT_done2)[i // NG], 1)
                mm = pe.matmul(bank[2][:, i * E:(i + 1) * E], xT[:, i * P:(i + 1) * P], col("wgate", 0, E), start=True, stop=True)
            mm.then_inc(logits_ready, 1)
            pe.wait_ge(gate_done, 1)
            pe.transpose(bank[3][0:NTE, 0:P], gate[:], ident).then_inc(gateT_ready, 1)
            pe.wait_ge(cast_done, 1)
            with pe.Fori(0, 2 * KEY_HALF) as k:
                pe.wait_ge(counted, k + 1)
                pe.matmul(bank[4][:, 0:1], same_b[:], count[:], start=True, stop=True).then_inc(totalled, 1)
            pe.wait_ge(masksT_done, 2)
            masks_ps = bank[3][:].bitcast(BF16)
            for i in range(2):
                tr = pe.transpose(masks_ps[:, i * NTE:(i + 1) * NTE], masksT[0:NTE, i, :], ident_b[0:NTE, 0:NTE])
            tr.then_inc(masks_ready, 1)
            pe.wait_ge(masks_done, 1)

            def ranks(ps, m, more):
                pe.matmul(ps[:, 0:NTE], before_b[:], m[:, 0:NTE], start=True, stop=False, skip_group_check=True)
                for i in range(1, NT):
                    mm = pe.matmul(ps[:, i * E:NTE], ones_b[:], m[:, 0:NTE - i * E], start=False, stop=(not more and i == NT - 1), skip_group_check=True)
                return mm

            ranks(bank[5], masks[:, 1, :], True)
            for i in range(NT):
                mm = pe.matmul(bank[5][:, 0:NTE].rearrange("p (t e) -> p t e", t=NT), ones_b[:],
                               bc(masks[:, 0, i * E:(i + 1) * E], [P, NT, E], 1), start=False, stop=(i == NT - 1), skip_group_check=True)
            mm.then_inc(tie_rank_ready, 1)
            pe.wait_ge(chosen_done, 1)
            ranks(bank[6], chosen[:], False).then_inc(slots_ready, 1)
            for i in range(2):
                pe.wait_ge(s_dve, NTE // 4 * (i + 1))
                pe.wait_ge(s_pool, NTE // 4 * (i + 1))
                if i == 0:
                    pe.wait_ge(zcast, 3)
                for tile in range(NT):
                    for part in range(3):
                        mm = pe.matmul(bank[i][:], zpart[:, part, tile, :], S[:, tile, NG * i:NG * (i + 1), :],
                                       start=(tile == 0 and part == 0), stop=(tile == NT - 1 and part == 2))
                mm.then_inc(gathered, 1)
            pe.wait_ge(gcast, 3)
            for e in range(E):
                for tile in range(NT):
                    mm = pe.matmul(bank[2][:, 3 * e:3 * e + 3], S[:, tile, e, :], gpart[:, tile * E + e, :], start=(tile == 0), stop=(tile == NT - 1))
            mm.then_inc(weight_ready, 1)
            for e in range(E):
                if e >= 2:
                    pe.wait_ge(st_act if e % 2 == 0 else st_dve, e // 2)
                for tile in range(NT):
                    tr = pe.transpose(bank[3 + e % 2][:].bitcast(BF16)[:, tile * P:(tile + 1) * P], S[:, tile, e, :], ident_b[:])
                tr.then_inc(st_ready, 1)
            pe.wait_ge(s_moe, 32)
            for e in range(E + 1):
                if e < E:
                    pe.wait_ge(xgT_done, e // NG + 1)
                    wait(pe, hidE_done, NCH * (e - 1))
                    for c in range(NCH):
                        mm = pe.matmul(bank[5 + e % 2][:, c * CAP:(c + 1) * CAP], fc1s[:, e, c * P:(c + 1) * P], xgT[:, e, :], start=True, stop=True)
                    mm.then_inc(hidE_ready, 1)
                if e > 0:
                    pe.wait_ge(hidE_done, NCH * e)
                    if e == 1:
                        pe.wait_ge(weight_done, 1)
                    wait(pe, yb_done, e - 2)
                    for c in range(NCH):
                        mm = pe.matmul((bank[7], bank[2])[e % 2][:, 0:C], hidE[:, (e - 1) % 2, c, :], fc2s[:, e - 1, c, :], start=(c == 0), stop=(c == NCH - 1))
                    mm.then_inc(y_ready, 1)
            pe.wait_ge(st_act, E // 2)
            pe.wait_ge(st_dve, E // 2)
            pe.wait_ge(yw_done, E)
            for tile in range(NT):
                wait(pe, final_done, tile - 1)
                for e in range(E):
                    for i in range(3):
                        mm = pe.matmul(bank[tile % 2][:, 0:C], ST[:, e, tile * P:(tile + 1) * P], ypart[:, i, e, :],
                                       start=(e == 0 and i == 0), stop=(e == E - 1 and i == 2))
                mm.then_inc(scattered, 1)

        @block.vector
        def _(dve):
            dve.memset(count[:], 0.0)
            dve.memset(minus_half[:], -0.5).then_inc(consts_set, 1)
            dve.memset(v0[:, :, HD0:HD0 + 1], 1.0).then_inc(consts_set, 1)
            dve.wait_ge(s_x, 16)
            for b in range(B):
                dve.bn_stats(stats[:, b, :], x[:, b, :]).then_inc(stat_link, 1)
            for b in range(B):
                dve.wait_ge(stat_link, b + 1)
                dve.bn_aggr(mv[:, b, :], stats[:, b, :]).then_inc(stat_link, 1)
            dve.wait_ge(stat_link, 2 * B)
            dve.tensor_scalar(var_eps[:], mv[:, :, 1], EPS0, None, ALU.add).then_inc(var_done, 1)
            dve.wait_ge(s_small, 80)
            dve.wait_ge(ada_ready, 1)
            for i, (chunk, one) in enumerate(((2, 1.0), (3, 1.0), (4, 0.0), (5, 0.0))):
                dve.tensor_scalar(mod[:, i, :], bank[7][:, i * B:(i + 1) * B], col("ada_b", chunk), one, ALU.add, ALU.add).then_inc(mod_done, 1)
            dve.tensor_scalar(shift1[:], bank[7][:, 4 * B:5 * B], col("b_ada"), col("ln1_b"), ALU.add, ALU.add).then_inc(mod_done, 1)
            for i in range(4):
                dve.wait_ge(gates_ready, 2 * i + 2)
                dve.tensor_tensor(gates[:, 2 * i:2 * i + 2, :], bank[i][:].rearrange("p (b c) -> p b c", b=2),
                                  bc(row("ada_b"), [P, 2, 2 * C], 1), ALU.add).then_inc(gates_done, 1)
            dve.wait_ge(gates_done, 4)
            dve.tensor_tensor(pg1[:], gates[:, :, 0:C], bc(row("proj_b"), [P, B, C], 1), ALU.mult).then_inc(gates_done, 1)
            dve.tensor_tensor(fg2[:], gates[:, :, C:2 * C], bc(row("fc2_b"), [P, B, C], 1), ALU.mult).then_inc(gates_done, 1)
            dve.wait_ge(gates_done, 6)
            dve.wait_ge(rstd_done, 1)

            def norm(b):
                wait(dve, zT_ready, b)
                dve.tensor_scalar(z[:], x[:, b, :], mv[:, b, 0:1], at(rstd[:], b), ALU.subtract, ALU.mult).then_inc(z_ready, 1)

            def save(b):
                dve.wait_ge(qkv_ready, b + 1)
                wait(dve, rope_link, 3 * b)
                wait(dve, v_done, b)
                dve.tensor_tensor(qkv0[:], qkv_ps[:, 0:3 * C], row("qkv_b"), ALU.add).then_inc(qkv_saved, 1)

            def shifted(b, g):
                n = NG * b + g
                s = s_ps[g % 2][:].rearrange("p (h k) -> p h k", h=HG)
                dve.wait_ge(s_ready, n + 1)
                dve.reduce_max(smax[:, g, :], s, AX).then_inc(max_done, 1)
                dve.wait_ge(max_done, n + 1)
                dve.tensor_tensor(prob[:, g, :].rearrange("p (h k) -> p h k", h=HG), s,
                                  bc(smax[:, g, :], [P, HG, L], 2), ALU.subtract).then_inc(sub_done, 1)

            def outputs(b, g):
                n = NG * b + g
                o = o_ps[:, 0:HG * (HD0 + 1)].rearrange("p (h d) -> p h d", h=HG)
                dve.wait_ge(o_ready, n + 1)
                dve.reciprocal(rsum[:, g, :], o[:, :, HD0]).then_inc(rec_done, 1)
                dve.wait_ge(rec_done, n + 1)
                if g == 0:
                    wait(dve, oT_ready, b)
                dve.tensor_tensor(o0[:, g * HG * HD0:(g + 1) * HG * HD0].rearrange("p (h d) -> p h d", h=HG), o[:, :, 0:HD0],
                                  bc(rsum[:, g, :], [P, HG, HD0], 2), ALU.mult).then_inc(o_done, 1)

            def residual(b):
                dve.tensor_tensor(x[:, b, :], x[:, b, :], pg1[:, b, :], ALU.add).then_inc(xb_done, 1)
                dve.wait_ge(proj_ready, b + 1)
                dve.tensor_tensor(delta[:], misc_ps[:, 0:C], gates[:, b, 0:C], ALU.mult).then_inc(gated_done, 1)
                dve.wait_ge(gated_done, b + 1)
                dve.wait_ge(xb_done, b + 1)
                dve.tensor_tensor(x[:, b, :], x[:, b, :], delta[:], ALU.add).then_inc(res_done, 1)

            def step(b, ahead):
                for g in range(NG):
                    late = back(b, g, 2)
                    if g == 0 and ahead:
                        norm(b + 1)
                    if real(b):
                        shifted(b, g)
                    if real(late[0]):
                        outputs(*late)
                    if g == 1 and ahead:
                        save(b + 1)
                    if g == 2 and real(b - 1):
                        residual(b - 1)

            norm(0)
            save(0)
            step(0, True)
            step(1, True)
            with dve.Fori(2, B - 1) as b:
                step(b, True)
            step(B - 1, False)
            step(B, False)
            for b in range(B):
                dve.wait_ge(res_done, b + 1)
                dve.bn_stats(stats[:, b, :], x[:, b, :]).then_inc(stat_link, 1)
            for b in range(B):
                dve.wait_ge(stat_link, 2 * B + b + 1)
                dve.bn_aggr(mv[:, b, :], stats[:, b, :]).then_inc(stat_link, 1)
            dve.wait_ge(stat_link, 4 * B)
            dve.tensor_scalar(var_eps[:], mv[:, :, 1], EPS0, None, ALU.add).then_inc(var_done, 1)
            dve.wait_ge(rstd_done, 2)
            for half in range(2):
                for i in range(NG):
                    b = NG * half + i
                    wait(dve, z4T_ready, half)
                    dve.tensor_scalar(z4[:, i, :], x[:, b, :], mv[:, b, 0:1], at(rstd[:], b), ALU.subtract, ALU.mult).then_inc(z4_done, 1)
                for i in range(NG):
                    b = NG * half + i
                    dve.wait_ge(z4_done, b + 1)
                    dve.tensor_tensor(x[:, b, :], x[:, b, :], fg2[:, b, :], ALU.add).then_inc(xf_done, 1)
                for i in range(NG):
                    b = NG * half + i
                    dve.wait_ge(ff_ready, b + 1)
                    dve.tensor_tensor(delta[:], (o_ps, misc_ps)[i % 2][:, 0:C], gates[:, b, C:2 * C], ALU.mult).then_inc(ffg_done, 1)
                    dve.wait_ge(ffg_done, b + 1)
                    dve.wait_ge(xf_done, b + 1)
                    dve.tensor_tensor(x[:, b, :], x[:, b, :], delta[:], ALU.add).then_inc(l0_done, 1)
                    dve.wait_ge(l0_done, b + 1)

            wqk_h = wqk[:].rearrange("p g (h d) -> p (g h) d", d=HD1)
            dve.wait_ge(s_l1, 48)
            dve.reduce_sum(wsum[:], wqk_h, AX).then_inc(wsum_done, 1)
            dve.wait_ge(wsum_done, 1)
            dve.scalar_tensor_tensor(wqk_h, bc(wsum[:], [P, 2 * H, HD1], 2), -1.0 / HD1, wqk_h, ALU.mult, ALU.add).then_inc(wqk_done, 1)
            dve.memset(v1[:, :, :, HD1:HD1 + 1], 1.0).then_inc(consts_set, 1)

            def token_stats(k, eps):
                for b in range(B):
                    dve.bn_stats(stats[:, b, :], x[:, b, :]).then_inc(stat_link, 1)
                for b in range(B):
                    dve.wait_ge(stat_link, 2 * B * k + b + 1)
                    dve.bn_aggr(mv[:, b, :], stats[:, b, :]).then_inc(stat_link, 1)
                dve.wait_ge(stat_link, 2 * B * (k + 1))
                dve.tensor_scalar(var_eps[:], mv[:, :, 1], eps, None, ALU.add).then_inc(var_done, 1)

            token_stats(2, EPS1)
            dve.wait_ge(rstd_done, 3)

            def norm1(b):
                wait(dve, z1T_ready, b)
                dve.tensor_scalar(z[:], x[:, b, :], mv[:, b, 0:1], at(rstd[:], b), ALU.subtract, ALU.mult).then_inc(z1_ready, 1)

            def shifted1(b, g):
                n = NG * b + g
                two = [prob[:, g, :].rearrange("p (i a k) -> p a i k", i=2, a=2)[:, a, :, :] for a in range(2)]
                dve.wait_ge(s1_ready, n + 1)
                for a in range(2):
                    dve.reduce_max(smax[:, g, 2 * a:2 * a + 2], s_ps[a][:, 0:2 * L].rearrange("p (i k) -> p i k", i=2), AX).then_inc(max1_done, 1)
                for a in range(2):
                    dve.wait_ge(max1_done, 2 * n + a + 1)
                    dst = dve.tensor_tensor(two[a], s_ps[a][:, 0:2 * L].rearrange("p (i k) -> p i k", i=2),
                                            bc(smax[:, g, 2 * a:2 * a + 2], [P, 2, L], 2), ALU.subtract)
                dst.then_inc(sub1_done, 1)

            def sums(b, g):
                n = NG * b + g
                dve.wait_ge(squared, n + 1)
                dve.reduce_sum(sumsq[:], sq[:].rearrange("p (h d) -> p h d", d=HD1), AX).then_inc(sumsq_done, 1)
                dve.wait_ge(sumsq_done, n + 1)
                wait(dve, hrstd_done, n)
                dve.tensor_scalar(head_var[:], sumsq[:], 1.0 / HD1, EPS1, ALU.mult, ALU.add).then_inc(hvar_done, 1)

            def qk_normed(b, g):
                n = NG * b + g
                dve.wait_ge(hrstd_done, n + 1)
                wait(dve, qkT1_ready, n)
                dve.tensor_tensor(qkn[:].rearrange("p (h d) -> p h d", d=HD1), qkv_ps[:].rearrange("p (h d) -> p h d", d=HD1),
                                  bc(head_rstd[:], [P, 2 * HG, HD1], 2), ALU.mult).then_inc(qkn_done, 1)

            def outputs1(b, g):
                n = NG * b + g
                o = o_ps[:, 0:HG * (HD1 + 1)].rearrange("p (h d) -> p h d", h=HG)
                dve.wait_ge(o1_ready, n + 1)
                dve.reciprocal(rsum[:, g, :], o[:, :, HD1]).then_inc(rec1_done, 1)
                dve.wait_ge(rec1_done, n + 1)
                wait(dve, oT1_ready, n)
                dve.tensor_tensor(o1[:].rearrange("p (h d) -> p h d", h=HG), o[:, :, 0:HD1],
                                  bc(rsum[:, g, :], [P, HG, HD1], 2), ALU.mult).then_inc(o1_done, 1)

            def residual1(b):
                dve.wait_ge(proj1_ready, b + 1)
                dve.tensor_tensor(x[:, b, :], x[:, b, :], misc_ps[:, 0:C], ALU.add).then_inc(res1_done, 1)

            def step1(b, ahead):
                for g in range(NG):
                    two, three = back(b, g, 2), back(b, g, 3)
                    if real(two[0]):
                        shifted1(*two)
                    if g == NG - 2 and ahead:
                        norm1(b + 1)
                    if real(b):
                        sums(b, g)
                    if real(three[0]):
                        outputs1(*three)
                    if real(b):
                        qk_normed(b, g)
                    if g == NG - 1 and real(b - 1):
                        residual1(b - 1)

            norm1(0)
            step1(0, True)
            step1(1, True)
            with dve.Fori(2, B - 1) as b:
                step1(b, True)
            step1(B - 1, False)
            step1(B, False)

            dve.wait_ge(res1_done, B)
            token_stats(3, EPS1)
            dve.wait_ge(xT_ready, 2)
            dve.tensor_copy(xT[:, NG * P:2 * NG * P], bank[1][:]).then_inc(xT_done2, 1)
            g3 = gate[:].rearrange("p (t e) -> p t e", e=E)
            logits = bank[2][:, 0:NTE].rearrange("p (t e) -> p t e", e=E)
            dve.wait_ge(logits_ready, 1)
            dve.reduce_max(gate_max[:], logits, AX).then_inc(gate_link, 1)
            dve.wait_ge(gate_link, 1)
            dve.tensor_tensor(g3, logits, bc(gate_max[:], [P, NT, E], 2), ALU.subtract).then_inc(gate_link, 1)
            dve.wait_ge(gate_exp, 1)
            dve.reduce_sum(gate_sum[:], g3, AX).then_inc(gate_link, 1)
            dve.wait_ge(gate_link, 3)
            dve.reciprocal(gate_max[:], gate_sum[:]).then_inc(gate_link, 1)
            dve.wait_ge(gate_link, 4)
            dve.tensor_tensor(g3, g3, bc(gate_max[:], [P, NT, E], 2), ALU.mult).then_inc(gate_done, 1)
            R = slice(0, NTE)
            dve.wait_ge(gateT_ready, 1)
            dve.tensor_copy(keys[R, :], bank[3][R, 0:P]).then_inc(key_link, 1)
            dve.wait_ge(key_link, 1)
            dve.tensor_scalar(key_i[R, 0, :], keys[R, :].bitcast(I32), KEY_HALF, None, ALU.logical_shift_right).then_inc(key_link, 1)
            dve.tensor_scalar(key_i[R, 1, :], keys[R, :].bitcast(I32), 2 ** KEY_HALF - 1, None, ALU.bitwise_and).then_inc(key_link, 1)
            dve.memset(cand[R, :], 2.0 ** (KEY_HALF - 1)).then_inc(narrowed, 1)
            dve.wait_ge(key_link, 3)
            dve.tensor_copy(key_hi[R, :], key_i[R, 0, :]).then_inc(key_link, 1)
            dve.tensor_copy(key_lo[R, :], key_i[R, 1, :]).then_inc(key_link, 1)
            dve.wait_ge(key_link, 5)

            def search(key, start):
                with dve.Fori(0, KEY_HALF) as k:
                    n = start + k
                    dve.wait_ge(narrowed, n + 1 + (1 if start else 0))
                    dve.tensor_scalar(hits[R, :], key[R, :], cand[R, :], 0.0, ALU.is_ge, ALU.add, accum_out=count[R, :]).then_inc(counted, 1)
                    dve.tensor_scalar(cand_low[R, :], cand[R, :], at(cst("steps")[R, :], k), None, ALU.subtract).then_inc(cand_link, 1)
                    dve.wait_ge(totalled, n + 1)
                    dve.tensor_scalar(step_up[R, :], bank[4][R, 0:1], CAP - 0.5, at(cst("bits")[R, :], k), ALU.is_ge, ALU.mult).then_inc(cand_link, 1)
                    dve.wait_ge(cand_link, 2 * n + 2)
                    dve.tensor_tensor(cand[R, :], step_up[R, :], cand_low[R, :], ALU.add).then_inc(narrowed, 1)

            search(key_hi, 0)
            dve.wait_ge(narrowed, KEY_HALF + 1)
            dve.tensor_scalar(above[R, :], key_hi[R, :], cand[R, :], 2.0 ** (KEY_HALF + 1), ALU.is_gt, ALU.mult).then_inc(key_link, 1)
            dve.tensor_scalar(eq_part[R, :], key_hi[R, :], cand[R, :], None, ALU.is_equal).then_inc(key_link, 1)
            dve.tensor_scalar(key_lo[R, :], key_lo[R, :], 1.0, None, ALU.add).then_inc(key_link, 1)
            dve.wait_ge(key_link, 8)
            dve.tensor_tensor(eq_part[R, :], eq_part[R, :], key_lo[R, :], ALU.mult).then_inc(key_link, 1)
            dve.memset(cand[R, :], 2.0 ** (KEY_HALF - 1)).then_inc(narrowed, 1)
            dve.wait_ge(key_link, 9)
            dve.scalar_tensor_tensor(keys[R, :], above[R, :], -1.0, eq_part[R, :], ALU.add, ALU.add).then_inc(key_link, 1)
            dve.wait_ge(key_link, 10)
            search(keys, KEY_HALF)
            dve.wait_ge(narrowed, 2 * KEY_HALF + 2)
            dve.tensor_scalar(masksT[R, 0, :], keys[R, :], cand[R, :], None, ALU.is_gt).then_inc(masksT_done, 1)
            dve.tensor_scalar(masksT[R, 1, :], keys[R, :], cand[R, :], None, ALU.is_equal).then_inc(masksT_done, 1)
            dve.wait_ge(masks_ready, 1)
            dve.tensor_copy(masks[:], bank[3][:].bitcast(BF16)[:, 0:2 * NTE].rearrange("p (a n) -> p a n", a=2)).then_inc(masks_done, 1)
            dve.wait_ge(masks_done, 1)
            dve.wait_ge(tie_rank_ready, 1)
            dve.scalar_tensor_tensor(tied[:], bank[5][:, 0:NTE], CAP - 0.5, masks[:, 1, :], ALU.is_lt, ALU.mult).then_inc(chosen_link, 1)
            dve.wait_ge(chosen_link, 1)
            dve.tensor_tensor(chosen[:], tied[:], masks[:, 0, :], ALU.add).then_inc(chosen_done, 1)
            dve.wait_ge(chosen_done, 1)
            dve.wait_ge(slots_ready, 1)
            dve.scalar_tensor_tensor(slot1[:], bank[6][:, 0:NTE], 1.0, chosen[:], ALU.add, ALU.mult).then_inc(slots_done, 1)
            dve.wait_ge(slots_done, 1)
            for half in range(2):
                for tile in range(NT):
                    for e in range(NG * half, NG * half + NG // 2):
                        dve.tensor_scalar(S[:, tile, e, :], iota_b[:], slot1[:, tile * E + e:tile * E + e + 1], None, ALU.is_equal).then_inc(s_dve, 1)
            dve.wait_ge(weight_ready, 1)
            dve.reduce_sum(weight[:], bank[2][:, 0:3 * E].rearrange("p (e a) -> p e a", a=3), AX).then_inc(weight_done, 1)
            dve.wait_ge(weight_done, 1)
            for e in range(1, E, 2):
                dve.wait_ge(st_ready, e + 1)
                dve.tensor_copy(ST[:, e, :], bank[4][:].bitcast(BF16)).then_inc(st_dve, 1)
            for e in range(E):
                dve.wait_ge(y_ready, e + 1)
                dve.tensor_tensor(yb[:, e % 2, :], (bank[2], bank[7])[e % 2][:, 0:C], row("b2s")[:, e * C:(e + 1) * C], ALU.add).then_inc(yb_done, 1)
                dve.wait_ge(yb_done, e + 1)
                dve.tensor_scalar(yw[:, e % 2, :], yb[:, e % 2, :], weight[:, e:e + 1], None, ALU.mult).then_inc(y_link, 1)
                rest = yw[:, e % 2, :]
                for i in range(3):
                    dve.wait_ge(y_link, 5 * e + 2 * i + 1)
                    part = dve.tensor_copy(ypart[:, i, e, :], rest)
                    if i < 2:
                        part.then_inc(y_link, 1)
                        dve.wait_ge(y_link, 5 * e + 2 * i + 2)
                        dve.tensor_tensor(yr[:, e % 2, i, :], rest, ypart[:, i, e, :], ALU.subtract).then_inc(y_link, 1)
                        rest = yr[:, e % 2, i, :]
                part.then_inc(yw_done, 1)
            for tile in range(NT):
                dve.wait_ge(scattered, tile + 1)
                dve.tensor_tensor(x[:, tile, :], x[:, tile, :], bank[tile % 2][:, 0:C], ALU.add).then_inc(final_done, 1)

        @block.scalar
        def _(act):
            act.wait_ge(s_small, 80)
            act.activation(silu_c[:], col("cond", 0, B), ACT.Silu).then_inc(silu_done, 1)
            act.wait_ge(mod_done, 5)

            def evac_hT(b):
                act.wait_ge(zT_ready, b + 1)
                wait(act, qkv_ready, b)
                act.activation(hT[:], misc_ps[:, 0:L], ACT.Identity, scale=at(mod[:, 0, :], b), bias=at(mod[:, 2, :], b)).then_inc(hT_ready, 1)

            def evac_qkT(b):
                act.wait_ge(qkT_ready, b + 1)
                wait(act, s_ready, NG * b)
                wait(act, kx_done, NG * b)
                act.activation(qkT0[:], tp_ps[:, 0:2 * L].rearrange("p (a k) -> p a k", a=2), ACT.Copy).then_inc(qkT_done, 1)

            def copy_v(b):
                act.wait_ge(qkv_saved, b + 1)
                wait(act, o_ready, NG * b)
                if isinstance(b, int) and b == 0:
                    act.wait_ge(consts_set, 2)
                act.activation(v0[:, :, 0:HD0], qkv0[:, 2 * C:3 * C].rearrange("p (h d) -> p h d", h=H), ACT.Copy).then_inc(v_done, 1)

            def exps(b, g):
                n = NG * b + g
                act.wait_ge(sub_done, n + 1)
                act.activation(prob[:, g, :], prob[:, g, :], ACT.Exp, scale=float(HD0) ** -0.5).then_inc(exp_done, 1)

            def evac_pT(b, g):
                n = NG * b + g
                act.wait_ge(pT_ready, n + 1)
                wait(act, o_ready, n - 1)
                act.activation(probT[:, g % 2, :], pT_ps[:], ACT.Copy).then_inc(pT_done, 1)

            def evac_oT(b):
                act.wait_ge(oT_ready, b + 1)
                wait(act, proj_ready, b)
                act.activation(oT0[:], misc_ps[:, 0:L], ACT.Copy).then_inc(oT_done, 1)

            def step(b, ahead):
                for g in range(NG):
                    late = back(b, g, 2)
                    if real(late[0]):
                        evac_pT(*late)
                    if g == 0 and ahead:
                        evac_hT(b + 1)
                    if real(b):
                        exps(b, g)
                    if g == 1 and real(b):
                        copy_v(b)
                    if g == 1 and real(b - 1):
                        evac_oT(b - 1)
                    if g == 3 and ahead:
                        evac_qkT(b + 1)

            evac_hT(0)
            evac_qkT(0)
            step(0, True)
            step(1, True)
            with act.Fori(2, B - 1) as b:
                step(b, True)
            step(B - 1, False)
            step(B, False)
            for half in range(2):
                for i in range(NG):
                    b = NG * half + i
                    act.wait_ge(z4T_ready, half + 1)
                    wait(act, hid_ready, NCH * half)
                    act.activation(h4T[:, i * L:(i + 1) * L], tp_ps[:, i * L:(i + 1) * L], ACT.Identity,
                                   scale=mod[:, 1, b:b + 1], bias=mod[:, 3, b:b + 1]).then_inc(h4T_done, 1)
                for c in range(NCH):
                    act.wait_ge(hid_ready, NCH * half + c + 1)
                    wait(act, ff_ready, NG * half)
                    act.activation(hid[:, c, :], s_ps[c % 2][:], ACT.Gelu_apprx_tanh, bias=col("fc1_b", c)).then_inc(hid_done, 1)

            def evac_h1T(b):
                act.wait_ge(z1T_ready, b + 1)
                wait(act, qkv1_ready, NG * b)
                act.activation(hT[:], misc_ps[:, 0:L], ACT.Identity, scale=col("ln1_g"), bias=at(shift1[:], b)).then_inc(h1T_done, 1)

            def square(b, g):
                n = NG * b + g
                act.wait_ge(qkv1_ready, n + 1)
                wait(act, sumsq_done, n)
                act.activation(sq[:], qkv_ps[:], ACT.Square).then_inc(squared, 1)

            def evac_v1(b, g):
                n = NG * b + g
                wait(act, o1_ready, n - NG + 1)
                act.activation(v1[:, g, :, 0:HD1], v_ps[:, 0:HG * HD1].rearrange("p (h d) -> p h d", h=HG), ACT.Copy).then_inc(v1_done, 1)

            def evac_qk1T(b, g):
                n = NG * b + g
                act.wait_ge(qkT1_ready, n + 1)
                wait(act, s1_ready, n - NG + 1)
                for i, (gain, bias) in enumerate((("qn_g", "qn_b"), ("kn_g", "kn_b"))):
                    act.activation(qkT1[:, g, 2 * i:2 * i + 2, :], tp1_ps[:, 2 * i * L:2 * (i + 1) * L].rearrange("p (a k) -> p a k", a=2),
                                   ACT.Identity, scale=col(gain), bias=col(bias)).then_inc(qkT1_done, 1)

            def exps1(b, g):
                n = NG * b + g
                act.wait_ge(sub1_done, n + 1)
                act.activation(prob[:, g, :], prob[:, g, :], ACT.Exp, scale=float(HD1) ** -0.5).then_inc(exp1_done, 1)

            def evac_p1T(b, g):
                n = NG * b + g
                act.wait_ge(pT1_ready, n + 1)
                wait(act, o1_ready, n - 1)
                act.activation(probT[:, g % 2, :], pT_ps[:], ACT.Copy).then_inc(pT1_done, 1)

            def evac_o1T(b, g):
                n = NG * b + g
                act.wait_ge(oT1_ready, n + 1)
                wait(act, proj1_ready, b)
                act.activation(oT1[:, 2 * g:2 * g + 2, :], misc_ps[:, 0:2 * L].rearrange("p (a k) -> p a k", a=2), ACT.Copy).then_inc(oT1_done, 1)

            def step1(b, ahead):
                for g in range(NG):
                    one, two, three = (back(b, g, lag) for lag in (1, 2, 3))
                    if real(three[0]):
                        evac_p1T(*three)
                    if real(two[0]):
                        exps1(*two)
                    if real(b):
                        square(b, g)
                        evac_v1(b, g)
                    if g == NG - 1 and ahead:
                        evac_h1T(b + 1)
                    if real(one[0]):
                        evac_qk1T(*one)
                    if real(three[0]):
                        evac_o1T(*three)

            evac_h1T(0)
            act.wait_ge(consts_set, 3)
            step1(0, True)
            step1(1, True)
            with act.Fori(2, B - 1) as b:
                step1(b, True)
            step1(B - 1, False)
            step1(B, False)
            act.wait_ge(xT_ready, 1)
            act.activation(xT[:, 0:NG * P], bank[0][:], ACT.Copy).then_inc(xT_done, 1)
            act.wait_ge(gate_link, 2)
            act.activation(gate[:], gate[:], ACT.Exp).then_inc(gate_exp, 1)
            act.wait_ge(zx_done, NT)
            act.activation(zpart[:, 0, :, :], zx, ACT.Copy).then_inc(zcast, 1)
            for i in range(1, 3):
                act.wait_ge(zrest, i)
                act.activation(zpart[:, i, :, :], zr, ACT.Copy).then_inc(zcast, 1)
            act.wait_ge(gate_done, 1)
            act.activation(gpart[:, :, 0], gate[:], ACT.Copy).then_inc(gcast, 1)
            for i in range(1, 3):
                act.wait_ge(grest, i)
                act.activation(gpart[:, :, i], gr[:], ACT.Copy).then_inc(gcast, 1)
            for i in range(2):
                act.wait_ge(gathered, i + 1)
                act.activation(xgT[:, NG * i:NG * (i + 1), :], bank[i][:].rearrange("p (e s) -> p e s", e=NG), ACT.Identity,
                               scale=col("mlp_g"), bias=col("mlp_b")).then_inc(xgT_done, 1)
            for e in range(0, E, 2):
                act.wait_ge(st_ready, e + 1)
                act.activation(ST[:, e, :], bank[3][:].bitcast(BF16), ACT.Copy).then_inc(st_act, 1)
            for e in range(E):
                act.wait_ge(hidE_ready, e + 1)
                wait(act, y_ready, e - 1)
                for c in range(NCH):
                    act.activation(hidE[:, e % 2, c, :], bank[5 + e % 2][:, c * CAP:(c + 1) * CAP], ACT.Gelu_apprx_tanh,
                                   bias=col("b1s", e * NCH + c)).then_inc(hidE_done, 1)

        @block.gpsimd
        def _(pool):
            pool.wait_ge(consts_set, 1)
            pool.wait_ge(var_done, 1)
            pool.tensor_tensor(rstd[:], var_eps[:], minus_half[:], ALU.pow).then_inc(rstd_done, 1)
            pool.wait_ge(s_small, 80)

            def rope(b):
                src = qkv0[:, 0:2 * C].rearrange("p (h a d) -> p h a d", h=2 * H, a=2)
                dst = rope_b[:].rearrange("p (h a d) -> p h a d", h=2 * H, a=2)
                half = HD0 // 2
                pool.wait_ge(qkv_saved, b + 1)
                wait(pool, roped_done, b)
                pool.tensor_tensor(rope_a[:].rearrange("p (h d) -> p h d", h=2 * H), qkv0[:, 0:2 * C].rearrange("p (h d) -> p h d", h=2 * H),
                                   bc(cst("cos"), [P, 2 * H, HD0], 1), ALU.mult).then_inc(rope_link, 1)
                for a in range(2):
                    pool.tensor_tensor(dst[:, :, a, :], src[:, :, 1 - a, :],
                                       bc(cst("sin")[:, a * half:(a + 1) * half], [P, 2 * H, half], 1), ALU.mult).then_inc(rope_link, 1)
                pool.wait_ge(rope_link, 3 * b + 3)
                wait(pool, qkT_ready, b)
                pool.tensor_tensor(roped[:], rope_a[:], rope_b[:], ALU.add).then_inc(roped_done, 1)

            def spread(b, g):
                n = NG * b + g
                pool.wait_ge(qkT_done, b + 1)
                wait(pool, s_ready, n - NG + 1)
                pool.tensor_tensor(kx[:, g, :, :], bc(qkT0[:, 1, :], [P, HG, L], 1),
                                   bc(cst("mask")[:, g * HG:(g + 1) * HG], [P, HG, L], 2), ALU.mult).then_inc(kx_done, 1)

            def step(b, ahead):
                for g in range(1, NG):
                    spread(b, g)
                    if g == 1 and ahead:
                        rope(b + 1)
                if ahead:
                    spread(b + 1, 0)

            rope(0)
            spread(0, 0)
            step(0, True)
            step(1, True)
            with pool.Fori(2, B - 1) as b:
                step(b, True)
            step(B - 1, False)
            pool.wait_ge(var_done, 2)
            pool.tensor_tensor(rstd[:], var_eps[:], minus_half[:], ALU.pow).then_inc(rstd_done, 1)
            for dst, name in ((ident_b, "ident"), (before_b, "before"), (iota_b, "iota1"), (same_b, "same")):
                pool.tensor_copy(dst[:], cst(name))
            pool.memset(ones_b[:], 1.0).then_inc(cast_done, 1)
            pool.wait_ge(var_done, 3)
            pool.tensor_tensor(rstd[:], var_eps[:], minus_half[:], ALU.pow).then_inc(rstd_done, 1)

            def head_scales(b, g):
                n = NG * b + g
                pool.wait_ge(hvar_done, n + 1)
                wait(pool, qkn_done, n)
                pool.tensor_tensor(head_rstd[:], head_var[:], minus_half[:], ALU.pow).then_inc(hrstd_done, 1)

            for g in range(NG):
                head_scales(0, g)
            with pool.Fori(1, B) as b:
                for g in range(NG):
                    head_scales(b, g)
            pool.wait_ge(var_done, 4)
            pool.tensor_tensor(rstd[:], var_eps[:], minus_half[:], ALU.pow).then_inc(rstd_done, 1)
            pool.wait_ge(rstd_done, 4)
            for b in range(NT):
                pool.tensor_scalar(zx[:, b, :], x[:, b, :], mv[:, b, 0:1], rstd[:, b:b + 1], ALU.subtract, ALU.mult).then_inc(zx_done, 1)
            pool.wait_ge(zx_done, NT)
            pool.wait_ge(zcast, 1)
            pool.tensor_tensor(zr, zx, zpart[:, 0, :, :], ALU.subtract).then_inc(zrest, 1)
            pool.wait_ge(zcast, 2)
            pool.wait_ge(zrest, 1)
            pool.tensor_tensor(zr, zr, zpart[:, 1, :, :], ALU.subtract).then_inc(zrest, 1)
            pool.wait_ge(gcast, 1)
            pool.tensor_tensor(gr[:], gate[:], gpart[:, :, 0], ALU.subtract).then_inc(grest, 1)
            pool.wait_ge(gcast, 2)
            pool.wait_ge(grest, 1)
            pool.tensor_tensor(gr[:], gr[:], gpart[:, :, 1], ALU.subtract).then_inc(grest, 1)
            pool.wait_ge(slots_done, 1)
            for half in range(2):
                for tile in range(NT):
                    for e in range(NG * half + NG // 2, NG * (half + 1)):
                        pool.tensor_scalar(S[:, tile, e, :], iota_b[:], slot1[:, tile * E + e:tile * E + e + 1], None, ALU.is_equal).then_inc(s_pool, 1)


def constants():
    c = np.zeros((P, N_CONST), np.float32)

    def put(name, a):
        c[:a.shape[0], CONST[name][0]:CONST[name][1]] = a

    put("ident", np.eye(P))
    put("before", np.triu(np.ones((P, P)), 1))
    put("iota1", np.tile(np.arange(1, P + 1), (P, 1)))
    inv = (1.0 / np.float32(10000.0) ** (np.arange(0, HD0, 2, dtype=np.float32) / HD0)).astype(np.float32)
    ang = np.arange(L, dtype=np.float32)[:, None] * inv[None, :]
    put("cos", np.concatenate([np.cos(ang), np.cos(ang)], 1))
    put("sin", np.concatenate([-np.sin(ang), np.sin(ang)], 1))
    put("mask", np.arange(P)[:, None] // HD0 == np.arange(H)[None, :])
    bits = 2.0 ** np.arange(KEY_HALF - 1, -1, -1)
    put("bits", np.tile(bits, (P, 1)))
    put("steps", np.tile(np.maximum(bits / 2, 1.0), (P, 1)))
    same = np.zeros((P, P))
    same[:B * E, :B * E] = np.arange(B * E)[:, None] % E == np.arange(B * E)[None, :] % E
    put("same", same)
    return c


def laid_out(a):
    two = lambda v: np.concatenate([v, v]).reshape(P, 1)
    vec = lambda v, n: v.reshape(n, P).T
    wqkv = a["L1_cond_Wqkv"].reshape(3, NG, HG * HD1, C)
    parts = {
        "cond": a["cond_1024"].T, "ada_b": vec(a["L0_cond_ada_b"], 6), "fc1_b": vec(a["L0_cond_fc1_b"], NCH),
        "b_ada": vec(a["L1_cond_b_ada"], 1), "ln1_g": vec(a["L1_cond_ln1_g"], 1), "ln1_b": vec(a["L1_cond_ln1_b"], 1),
        "qn_g": two(a["L1_cond_qn_g"]), "qn_b": two(a["L1_cond_qn_b"]), "kn_g": two(a["L1_cond_kn_g"]), "kn_b": two(a["L1_cond_kn_b"]),
        "mlp_g": vec(a["L1_cond_mlp_g"], 1), "mlp_b": vec(a["L1_cond_mlp_b"], 1),
        "b1s": a["L1_cond_b1s"].reshape(E * NCH, P).T, "wgate": a["L1_cond_Wgate"].T,
    }
    rows = {"qkv_b": a["L0_cond_qkv_b"], "proj_b": a["L0_cond_proj_b"], "fc2_b": a["L0_cond_fc2_b"],
            "ada_b": a["L0_cond_ada_b"][:2 * C], "b2s": a["L1_cond_b2s"].reshape(-1)}
    out = {
        "x": a["x"],
        "cols": np.concatenate([parts[n] for n in COLS], 1),
        "rows": np.concatenate([rows[n] for n in ROWS]),
        "consts": constants(),
        "ada_w": a["L0_cond_ada_w"].T, "w_ada": a["L1_cond_W_ada"].T,
        "qkv_w": a["L0_cond_qkv_w"].T, "proj_w": a["L0_cond_proj_w"].T,
        "fc1_w": a["L0_cond_fc1_w"].T,
        "fc2_w": a["L0_cond_fc2_w"].reshape(C, NCH, P).transpose(2, 1, 0),
        "wqk": np.concatenate([wqkv[0], wqkv[1]], 1).transpose(2, 0, 1),
        "wv": wqkv[2].transpose(2, 0, 1),
        "wout": a["L1_cond_Wout"].reshape(C, 2 * NG, P).transpose(2, 1, 0),
        "fc1s": a["L1_cond_fc1s"].transpose(2, 0, 1),
        "fc2s": a["L1_cond_fc2s"].reshape(E, C, NCH, P).transpose(3, 0, 2, 1),
    }
    return {n: np.ascontiguousarray(v) for n, v in out.items()}


def kernel(**inputs):
    import concourse.bacc as bacc
    from concourse.bass_utils import run_bass_kernel_spmd

    arrays = laid_out({n: np.asarray(v) for n, v in inputs.items()})
    nc = bacc.Bacc("TRN2", target_bir_lowering=False, num_devices=1)
    t = {n: nc.dram_tensor(f"in_{n}", v.shape, mybir.dt.from_np(v.dtype), kind="ExternalInput").ap() for n, v in arrays.items()}
    t["out"] = nc.dram_tensor("out", (B, L, C), F32, kind="ExternalOutput").ap()
    program(nc, t)
    r = run_bass_kernel_spmd(nc, [{f"in_{n}": v for n, v in arrays.items()}], core_ids=[0])
    return r.results[0]["out"]
```

```python
from contextlib import ExitStack

import concourse.bass as bass
import numpy as np
from concourse import mybir

F32 = mybir.dt.float32
BF16 = mybir.dt.bfloat16
I32 = mybir.dt.int32
ALU = mybir.AluOpType
ACT = mybir.ActivationFunctionType
AX = mybir.AxisListType.X

P = 128
B, L, C = 8, 128, 128
NG = 4
HG = 4
H = NG * HG
HD0, HD1 = C // H, 64
DFF = 4 * C
NCH = DFF // P
E = 8
CAP = B * L // E
EPS0, EPS1 = 1e-6, 1e-5
KEY_HALF = 15

COLS = {}
_at = 0
for _name, _n in (("cond", B), ("ada_b", 6), ("fc1_b", NCH), ("b_ada", 1), ("ln1_g", 1), ("ln1_b", 1),
                  ("qn_g", 1), ("qn_b", 1), ("kn_g", 1), ("kn_b", 1), ("mlp_g", 1), ("mlp_b", 1),
                  ("b1s", E * NCH), ("wgate", E)):
    COLS[_name] = (_at, _at + _n)
    _at += _n
N_COLS = _at
ROWS = {}
_at = 0
for _name, _n in (("qkv_b", 3 * C), ("proj_b", C), ("fc2_b", C), ("ada_b", 2 * C), ("b2s", E * C)):
    ROWS[_name] = (_at, _at + _n)
    _at += _n
N_ROWS = _at
CONST = {}
_at = 0
for _name, _n in (("ident", P), ("before", P), ("iota1", P), ("cos", HD0), ("sin", HD0), ("mask", H), ("same", P),
                  ("bits", KEY_HALF), ("steps", KEY_HALF)):
    CONST[_name] = (_at, _at + _n)
    _at += _n
N_CONST = _at


def wait(eng, sem, count):
    if isinstance(count, int) and count <= 0:
        return
    eng.wait_ge(sem, count)


def back(b, g, lag):
    g -= lag
    while g < 0:
        g += NG
        b = b - 1
    return b, g


def real(b):
    return not isinstance(b, int) or 0 <= b < B


def at(ap, b):
    return ap.unsqueeze(2)[:, b, :]


def bc(ap, shape, axis):
    return ap.unsqueeze(axis).broadcast_to(shape)


def program(nc, t):
    with ExitStack() as ctx:
        def sb(name, shape, dt=F32):
            return ctx.enter_context(nc.sbuf_tensor(name, [P] + shape, dt))

        def sem(name):
            return ctx.enter_context(nc.semaphore(name))

        bank = [ctx.enter_context(nc.psum_tensor(f"bank{i}", [P, 512], F32)) for i in range(8)]

        x = sb("x_sb", [B, C])
        cols, rows, const = sb("cols_sb", [N_COLS]), sb("rows_sb", [N_ROWS]), sb("const_sb", [N_CONST])
        ada_w, w_ada = sb("ada_w_sb", [6 * C]), sb("w_ada_sb", [C])
        qkv_w, proj_w = sb("qkv_w_sb", [3 * C]), sb("proj_w_sb", [C])
        fc1_w, fc2_w = sb("fc1_w_sb", [DFF]), sb("fc2_w_sb", [NCH, C])
        wqk, wv = sb("wqk_sb", [NG, 2 * HG * HD1]), sb("wv_sb", [NG, HG * HD1])
        wout = sb("wout_sb", [2 * NG, C])
        fc1s, fc2s = sb("fc1s_sb", [E, DFF]), sb("fc2s_sb", [E, NCH, C])

        def col(name, i=0, n=1):
            return cols[:, COLS[name][0] + i:COLS[name][0] + i + n]

        def row(name):
            return rows[:, ROWS[name][0]:ROWS[name][1]]

        def cst(name):
            return const[:, CONST[name][0]:CONST[name][1]]

        ident = cst("ident")

        silu_c = sb("silu_c", [B])
        mod = sb("mod", [4, B])
        shift1 = sb("shift1", [B])
        gates = sb("gates", [B, 2 * C])
        pg1, fg2 = sb("pg1", [B, C]), sb("fg2", [B, C])

        stats, mv = sb("stats", [B, 6]), sb("mv", [B, 2])
        var_eps, rstd = sb("var_eps", [B]), sb("rstd", [B])
        minus_half = sb("minus_half", [B])
        z = sb("z", [C])
        hT = sb("hT", [L])

        qk0 = sb("qk0", [2 * C])
        rope_a, rope_b, roped = sb("rope_a", [2 * C]), sb("rope_b", [2 * C]), sb("roped", [2 * C])
        qT0, kT0 = sb("qT0", [L]), sb("kT0", [L])
        kx = sb("kx", [NG, HG, L])
        v0 = sb("v0", [B, H, HD0 + 1])
        neg_max = sb("neg_max", [NG, HG])
        prob = sb("prob", [NG, HG * L])
        probT = sb("probT", [2, HG * L])
        rsum, rinv = sb("rsum", [NG, HG]), sb("rinv", [NG, HG])
        o0 = sb("o0", [C])
        oT0 = sb("oT0", [L])
        delta = sb("delta", [C])
        z4, h4T = sb("z4", [NG, C]), sb("h4T", [NG * L])
        hid = sb("hid", [NCH, NG * L])

        wsum = sb("wsum", [2 * H])
        q_gain, q_bias = sb("q_gain", [1]), sb("q_bias", [1])
        sq, sumsq, head_var, head_rstd = sb("sq", [2 * HG * HD1]), sb("sumsq", [2 * HG]), sb("head_var", [2 * HG]), sb("head_rstd", [2 * HG])
        qkn = sb("qkn", [2 * HG * HD1])
        qkT1 = sb("qkT1", [NG, HG, L])
        v1 = sb("v1", [NG, HG * HD1])
        o1 = sb("o1", [HG * HD1])
        oT1 = sb("oT1", [2 * NG, L])
        NT = B
        NTE = NT * E
        xT = fg2[:].rearrange("p b c -> p (b c)")
        zx, zr = gates[:, 0:NT // 2, :].rearrange("p b (a c) -> p (b a) c", a=2), pg1[:]
        xgT = qkT1[:, 0:NG // 2, :, :].rearrange("p g h l -> p (g h) l")
        gate, gate_max, gate_sum = sb("gate", [NTE]), sb("gate_max", [NT]), sb("gate_sum", [NT])
        keys, key_hi, key_lo, key_i = sb("keys", [P]), sb("key_hi", [P]), sb("key_lo", [P]), sb("key_i", [2, P], I32)
        above, eq_part = sb("above", [P]), sb("eq_part", [P])
        hits, count = sb("hits", [P], BF16), sb("count", [1], BF16)
        cand, cand_low, step_up = sb("cand", [1]), sb("cand_low", [1]), sb("step_up", [1])
        masksT = sb("masksT", [2, P], BF16)
        masks = sb("masks", [2, NTE], BF16)
        tied = sb("tied", [NTE], BF16)
        chosen = sb("chosen", [NTE], BF16)
        slot1 = sb("slot1", [NTE])
        ident_b, before_b, ones_b = sb("ident_b", [P], BF16), sb("before_b", [P], BF16), sb("ones_b", [P], BF16)
        iota_b, same_b = sb("iota_b", [P], BF16), sb("same_b", [P], BF16)
        S = sb("S", [NT, E, CAP], BF16)
        ST = sb("ST", [E, NT * P], BF16)
        zpart = sb("zpart", [3, NT, C], BF16)
        gr, gpart = sb("gr", [NTE]), sb("gpart", [NTE, 3], BF16)
        weight = sb("weight", [E])
        hidE = hid[:].rearrange("p c (e s) -> p e c s", e=NG)
        yb, yw, yr = sb("yb", [2, C]), sb("yw", [2, C]), sb("yr", [2, 2, C])
        ypart = kx[:, 0:3, :, :].rearrange("p g h l -> p g (h l)").bitcast(BF16).rearrange("p g (e c) -> p g e c", e=E)

        s_x, s_small, s_l0, s_l1, s_moe = sem("x_loaded"), sem("small_loaded"), sem("l0_loaded"), sem("l1_loaded"), sem("moe_loaded")
        silu_done, ada_ready, mod_done, gates_ready, gates_done = sem("silu_done"), sem("ada_ready"), sem("mod_done"), sem("gates_ready"), sem("gates_done")
        consts_set, stat_link, var_done, rstd_done = sem("consts_set"), sem("stat_link"), sem("var_done"), sem("rstd_done")
        z_ready, zT_ready, hT_ready, qkv_ready, qkv_saved = sem("z_ready"), sem("zT_ready"), sem("hT_ready"), sem("qkv_ready"), sem("qkv_saved")
        rope_link, roped_done, qkT_ready, qT_done, kT_done, kx_done, v_done = sem("rope_link"), sem("roped_done"), sem("qkT_ready"), sem("qT_done"), sem("kT_done"), sem("kx_done"), sem("v_done")
        s_ready, max_done, sub_done, exp_done = sem("s_ready"), sem("max_done"), sem("sub_done"), sem("exp_done")
        pT_ready, pT_done, o_ready, rec_done, o_done = sem("pT_ready"), sem("pT_done"), sem("o_ready"), sem("rec_done"), sem("o_done")
        oT_ready, oT_done, proj_ready, xb_done, gated_done, res_done = sem("oT_ready"), sem("oT_done"), sem("proj_ready"), sem("xb_done"), sem("gated_done"), sem("res_done")
        z4_done, z4T_ready, h4T_done, hid_ready, hid_done, ff_ready = sem("z4_done"), sem("z4T_ready"), sem("h4T_done"), sem("hid_ready"), sem("hid_done"), sem("ff_ready")
        ffg_done, l0_done, xf_done = sem("ffg_done"), sem("l0_done"), sem("xf_done")
        wsum_done, wqk_done, z1_ready, z1T_ready, h1T_done, qk1_ready, qkv1_ready = sem("wsum_done"), sem("wqk_done"), sem("z1_ready"), sem("z1T_ready"), sem("h1T_done"), sem("qk1_ready"), sem("qkv1_ready")
        squared, sumsq_done, hvar_done, hrstd_done, qkn_done, v1_done = sem("squared"), sem("sumsq_done"), sem("hvar_done"), sem("hrstd_done"), sem("qkn_done"), sem("v1_done")
        qkT1_ready, qkT1_done, s1_ready, max1_done, rsum1_done, exp1_done = sem("qkT1_ready"), sem("qkT1_done"), sem("s1_ready"), sem("max1_done"), sem("rsum1_done"), sem("exp1_done")
        pT1_ready, pT1_done, o1_ready, rec1_done, o1_done = sem("pT1_ready"), sem("pT1_done"), sem("o1_ready"), sem("rec1_done"), sem("o1_done")
        oT1_ready, oT1_done, proj1_ready, res1_done = sem("oT1_ready"), sem("oT1_done"), sem("proj1_ready"), sem("res1_done")
        xT_ready, xT_done, logits_ready, gate_link, gate_exp, gate_done = sem("xT_ready"), sem("xT_done"), sem("logits_ready"), sem("gate_link"), sem("gate_exp"), sem("gate_done")
        gateT_ready, key_link, counted, totalled, cand_link, narrowed = sem("gateT_ready"), sem("key_link"), sem("counted"), sem("totalled"), sem("cand_link"), sem("narrowed")
        masksT_done, masks_ready, masks_done, tie_rank_ready, chosen_link, chosen_done = sem("masksT_done"), sem("masks_ready"), sem("masks_done"), sem("tie_rank_ready"), sem("chosen_link"), sem("chosen_done")
        slots_ready, slots_done, s_dve, s_pool, cast_done = sem("slots_ready"), sem("slots_done"), sem("s_dve"), sem("s_pool"), sem("cast_done")
        zx_done, zcast, zrest, gcast, grest = sem("zx_done"), sem("zcast"), sem("zrest"), sem("gcast"), sem("grest")
        gathered, xgT_done, weight_ready, weight_done, st_ready, st_act, st_dve = sem("gathered"), sem("xgT_done"), sem("weight_ready"), sem("weight_done"), sem("st_ready"), sem("st_act"), sem("st_dve")
        hidE_ready, hidE_done, y_ready, yb_done, yw_done, scattered, final_done = sem("hidE_ready"), sem("hidE_done"), sem("y_ready"), sem("yb_done"), sem("yw_done"), sem("scattered"), sem("final_done")
        y_link, xT_done2 = sem("y_link"), sem("xT_done2")
        s_out = sem("out_stored")

        qkv_ps, tp_ps, pT_ps, o_ps, misc_ps = bank[0], bank[1], bank[4], bank[5], bank[6]
        s_ps = [bank[2], bank[3]]
        qk_ps, v_ps, zp_ps, tp1_ps = [bank[0], bank[6]], bank[1], bank[1][:, HG * HD1:], bank[7]

        block = ctx.enter_context(nc.Block())

        @block.sync
        def _(sp):
            sp.dma_start(x[:], t["x"].rearrange("b t c -> t b c")).then_inc(s_x, 16)
            sp.dma_start(cols[:], t["cols"]).then_inc(s_small, 16)
            sp.dma_start(ada_w[:], t["ada_w"]).then_inc(s_small, 16)
            sp.dma_start(w_ada[:], t["w_ada"]).then_inc(s_small, 16)
            sp.dma_start(const[:], t["consts"]).then_inc(s_small, 16)
            sp.dma_start(rows[:], t["rows"].partition_broadcast(P)).then_inc(s_small, 16)
            sp.dma_start(qkv_w[:], t["qkv_w"]).then_inc(s_l0, 16)
            sp.dma_start(proj_w[:], t["proj_w"]).then_inc(s_l0, 16)
            sp.dma_start(fc1_w[:], t["fc1_w"]).then_inc(s_l0, 16)
            sp.dma_start(fc2_w[:], t["fc2_w"]).then_inc(s_l0, 16)
            sp.dma_start(wqk[:], t["wqk"]).then_inc(s_l1, 16)
            sp.dma_start(wv[:], t["wv"]).then_inc(s_l1, 16)
            sp.dma_start(wout[:], t["wout"]).then_inc(s_l1, 16)
            sp.dma_start(fc1s[:], t["fc1s"]).then_inc(s_moe, 16)
            sp.dma_start(fc2s[:], t["fc2s"]).then_inc(s_moe, 16)
            for i in range(2):
                sp.wait_ge(final_done, NT // 2 * (i + 1))
                half = slice(i * NT // 2, (i + 1) * NT // 2)
                sp.dma_start(t["out"][half].rearrange("b t c -> t b c"), x[:, half, :]).then_inc(s_out, 16)
            sp.wait_ge(s_out, 32)

        @block.tensor
        def _(pe):
            pe.wait_ge(s_small, 80)
            pe.wait_ge(silu_done, 1)
            for i, chunk in enumerate((2, 3, 4, 5)):
                pe.matmul(bank[7][:, i * B:(i + 1) * B], ada_w[:, chunk * C:(chunk + 1) * C], silu_c[:], start=True, stop=True)
            pe.matmul(bank[7][:, 4 * B:5 * B], w_ada[:], silu_c[:], start=True, stop=True).then_inc(ada_ready, 1)
            for b in range(B):
                pe.matmul(bank[b // 2][:, (b % 2) * 2 * C:(b % 2 + 1) * 2 * C], silu_c[:, b:b + 1].broadcast_to([P, P]),
                          ada_w[:, 0:2 * C], start=True, stop=True).then_inc(gates_ready, 1)
            pe.wait_ge(s_l0, 64)
            pe.wait_ge(gates_done, 4)

            def zT(b):
                pe.wait_ge(z_ready, b + 1)
                wait(pe, res_done, b - 2)
                pe.transpose(misc_ps[:, 0:L], z[:], ident).then_inc(zT_ready, 1)

            def qkv(b):
                pe.wait_ge(hT_ready, b + 1)
                wait(pe, v_done, b)
                pe.matmul(qkv_ps[:, 0:3 * C], hT[:], qkv_w[:], start=True, stop=True).then_inc(qkv_ready, 1)

            def qkT(b):
                pe.wait_ge(roped_done, b + 1)
                wait(pe, qT_done, b)
                pe.transpose(tp_ps[:, 0:L], roped[:, 0:C], ident)
                pe.transpose(tp_ps[:, L:2 * L], roped[:, C:2 * C], ident).then_inc(qkT_ready, 1)

            def scores(b, g):
                n = NG * b + g
                pe.wait_ge(kx_done, n + 1)
                if g == 0:
                    pe.wait_ge(qT_done, b + 1)
                wait(pe, exp_done, n - 1)
                pe.matmul(s_ps[g % 2][:], qT0[:], kx[:, g, :, :], start=True, stop=True).then_inc(s_ready, 1)

            def probsT(b, g):
                n = NG * b + g
                pe.wait_ge(exp_done, n + 1)
                wait(pe, pT_done, n)
                for i in range(HG):
                    tr = pe.transpose(pT_ps[:, i * L:(i + 1) * L], prob[:, g, i * L:(i + 1) * L], ident)
                tr.then_inc(pT_ready, 1)

            def values(b, g):
                n = NG * b + g
                pe.wait_ge(pT_done, n + 1)
                pe.wait_ge(v_done, b + 1)
                wait(pe, o_done, n)
                for i in range(HG):
                    mm = pe.matmul(o_ps[:, i * (HD0 + 1):(i + 1) * (HD0 + 1)], probT[:, g % 2, i * L:(i + 1) * L],
                                   v0[:, b, g * HG + i, :], start=True, stop=True)
                mm.then_inc(o_ready, 1)

            def oT(b):
                pe.wait_ge(o_done, NG * (b + 1))
                if not isinstance(b, int) or b + 2 < B:
                    pe.wait_ge(hT_ready, b + 3)
                pe.transpose(misc_ps[:, 0:L], o0[:], ident).then_inc(oT_ready, 1)

            def proj(b):
                pe.wait_ge(oT_done, b + 1)
                pe.matmul(misc_ps[:, 0:C], oT0[:], proj_w[:], start=True, stop=True).then_inc(proj_ready, 1)

            def step(b, ahead):
                for g in range(NG):
                    late = back(b, g, 2)
                    if real(late[0]):
                        probsT(*late)
                    if g == 3 and real(b - 1):
                        proj(b - 1)
                    if real(b):
                        scores(b, g)
                    if g == 0 and ahead:
                        zT(b + 1)
                    if real(late[0]):
                        values(*late)
                    if g == 0 and ahead:
                        qkv(b + 1)
                    if g == 2 and real(b - 1):
                        oT(b - 1)
                    if g == 2 and ahead:
                        qkT(b + 1)

            zT(0)
            qkv(0)
            qkT(0)
            step(0, True)
            step(1, True)
            with pe.Fori(2, B - 1) as b:
                step(b, True)
            step(B - 1, False)
            step(B, False)
            for half in range(2):
                pe.wait_ge(z4_done, NG * (half + 1))
                wait(pe, h4T_done, NG * half)
                for i in range(NG):
                    tr = pe.transpose(tp_ps[:, i * L:(i + 1) * L], z4[:, i, :], ident)
                tr.then_inc(z4T_ready, 1)
                pe.wait_ge(h4T_done, NG * (half + 1))
                for c in range(NCH):
                    n = NCH * half + c
                    wait(pe, hid_done, n - 1)
                    pe.matmul(s_ps[c % 2][:], fc1_w[:, c * P:(c + 1) * P], h4T[:], start=True, stop=True).then_inc(hid_ready, 1)
                pe.wait_ge(hid_done, NCH * (half + 1))
                for i in range(NG):
                    n = NG * half + i
                    wait(pe, ffg_done, n - 1)
                    for c in range(NCH):
                        mm = pe.matmul((o_ps, misc_ps)[i % 2][:, 0:C], hid[:, c, i * L:(i + 1) * L], fc2_w[:, c, :],
                                       start=(c == 0), stop=(c == NCH - 1))
                    mm.then_inc(ff_ready, 1)

            def z1T(b):
                pe.wait_ge(z1_ready, b + 1)
                wait(pe, v1_done, NG * b)
                pe.transpose(zp_ps[:, 0:L], z[:], ident).then_inc(z1T_ready, 1)

            def qkv1(b, g):
                n = NG * b + g
                pe.wait_ge(h1T_done, b + 1)
                wait(pe, qkn_done, n - 1)
                pe.matmul(qk_ps[g % 2][:], hT[:], wqk[:, g, :], start=True, stop=True).then_inc(qk1_ready, 1)
                wait(pe, v1_done, n)
                if g == 0:
                    wait(pe, res1_done, b - 1)
                pe.matmul(v_ps[:, 0:HG * HD1], hT[:], wv[:, g, :], start=True, stop=True).then_inc(qkv1_ready, 1)

            def qk1T(b, g):
                n = NG * b + g
                pe.wait_ge(qkn_done, n + 1)
                wait(pe, qkT1_done, 2 * n)
                for i in range(HG):
                    tr = pe.transpose(tp1_ps[:, i * L:(i + 1) * L], qkn[:, i * P:(i + 1) * P], ident)
                tr.then_inc(qkT1_ready, 1)

            def scores1(b, g):
                n = NG * b + g
                pe.wait_ge(qkT1_done, 2 * n + 2)
                wait(pe, exp1_done, n)
                for i in range(2):
                    for odd in range(2):
                        rows_ = slice(odd * HD1, (odd + 1) * HD1)
                        mm = pe.matmul(s_ps[odd][:, i * L:(i + 1) * L], qkT1[rows_, g, i, :], qkT1[rows_, g, 2 + i, :], start=True, stop=True)
                mm.then_inc(s1_ready, 1)

            def probs1T(b, g):
                n = NG * b + g
                pe.wait_ge(exp1_done, n + 1)
                wait(pe, pT1_done, n)
                for i in range(HG):
                    tr = pe.transpose(pT_ps[:, i * L:(i + 1) * L], prob[:, g, i * L:(i + 1) * L], ident)
                tr.then_inc(pT1_ready, 1)

            def values1(b, g):
                n = NG * b + g
                pe.wait_ge(pT1_done, n + 1)
                wait(pe, oT1_done, n)
                for i in range(HG):
                    mm = pe.matmul(o_ps[:, i * HD1:(i + 1) * HD1], probT[:, g % 2, i * L:(i + 1) * L],
                                   v1[:, g, i * HD1:(i + 1) * HD1], start=True, stop=True)
                mm.then_inc(o1_ready, 1)

            def o1T(b, g):
                n = NG * b + g
                pe.wait_ge(o1_done, n + 1)
                for i in range(2):
                    tr = pe.transpose(o_ps[:, HG * HD1 + i * L:HG * HD1 + (i + 1) * L], o1[:, i * P:(i + 1) * P], ident)
                tr.then_inc(oT1_ready, 1)

            def proj1(b):
                pe.wait_ge(oT1_done, NG * (b + 1))
                if not isinstance(b, int) or b + 2 < B:
                    pe.wait_ge(h1T_done, b + 3)
                if not isinstance(b, int) or b + 1 < B:
                    pe.wait_ge(v1_done, NG * (b + 2))
                for i in range(2 * NG):
                    mm = pe.matmul(zp_ps[:, L:L + C], oT1[:, i, :], wout[:, i, :], start=(i == 0), stop=(i == 2 * NG - 1))
                mm.then_inc(proj1_ready, 1)

            def step1(b, ahead):
                for g in range(NG):
                    one, two, three, four = (back(b, g, lag) for lag in (1, 2, 3, 4))
                    if real(b):
                        qkv1(b, g)
                    if real(three[0]):
                        probs1T(*three)
                    if real(four[0]):
                        o1T(*four)
                    if real(two[0]):
                        scores1(*two)
                    if g == NG - 1 and ahead:
                        z1T(b + 1)
                    if real(one[0]):
                        qk1T(*one)
                    if real(three[0]):
                        values1(*three)
                    if g == NG - 1 and real(b - 1):
                        proj1(b - 1)

            pe.wait_ge(wqk_done, 1)
            z1T(0)
            step1(0, True)
            step1(1, True)
            with pe.Fori(2, B - 1) as b:
                step1(b, True)
            step1(B - 1, False)
            step1(B, False)

            pe.wait_ge(res1_done, B)
            for i in range(2):
                for j in range(NG):
                    tr = pe.transpose(bank[i][:, j * P:(j + 1) * P], x[:, NG * i + j, :], ident)
                tr.then_inc(xT_ready, 1)
            for i in range(NT):
                pe.wait_ge((xT_done, xT_done2)[i // NG], 1)
                mm = pe.matmul(bank[2][:, i * E:(i + 1) * E], xT[:, i * P:(i + 1) * P], col("wgate", 0, E), start=True, stop=True)
            mm.then_inc(logits_ready, 1)
            pe.wait_ge(gate_done, 1)
            pe.transpose(bank[3][0:NTE, 0:P], gate[:], ident).then_inc(gateT_ready, 1)
            pe.wait_ge(cast_done, 1)
            with pe.Fori(0, 2 * KEY_HALF) as k:
                pe.wait_ge(counted, k + 1)
                pe.matmul(bank[4][:, 0:1], same_b[:], count[:], start=True, stop=True).then_inc(totalled, 1)
            pe.wait_ge(masksT_done, 2)
            masks_ps = bank[3][:].bitcast(BF16)
            for i in range(2):
                tr = pe.transpose(masks_ps[:, i * NTE:(i + 1) * NTE], masksT[0:NTE, i, :], ident_b[0:NTE, 0:NTE])
            tr.then_inc(masks_ready, 1)
            pe.wait_ge(masks_done, 1)

            def ranks(ps, m, more):
                pe.matmul(ps[:, 0:NTE], before_b[:], m[:, 0:NTE], start=True, stop=False, skip_group_check=True)
                for i in range(1, NT):
                    mm = pe.matmul(ps[:, i * E:NTE], ones_b[:], m[:, 0:NTE - i * E], start=False, stop=(not more and i == NT - 1), skip_group_check=True)
                return mm

            ranks(bank[5], masks[:, 1, :], True)
            for i in range(NT):
                mm = pe.matmul(bank[5][:, 0:NTE].rearrange("p (t e) -> p t e", t=NT), ones_b[:],
                               bc(masks[:, 0, i * E:(i + 1) * E], [P, NT, E], 1), start=False, stop=(i == NT - 1), skip_group_check=True)
            mm.then_inc(tie_rank_ready, 1)
            pe.wait_ge(chosen_done, 1)
            ranks(bank[6], chosen[:], False).then_inc(slots_ready, 1)
            for i in range(2):
                pe.wait_ge(s_dve, NTE // 4 * (i + 1))
                pe.wait_ge(s_pool, NTE // 4 * (i + 1))
                if i == 0:
                    pe.wait_ge(zcast, 3)
                for tile in range(NT):
                    for part in range(3):
                        mm = pe.matmul(bank[i][:], zpart[:, part, tile, :], S[:, tile, NG * i:NG * (i + 1), :],
                                       start=(tile == 0 and part == 0), stop=(tile == NT - 1 and part == 2))
                mm.then_inc(gathered, 1)
            pe.wait_ge(gcast, 3)
            for e in range(E):
                for tile in range(NT):
                    mm = pe.matmul(bank[2][:, 3 * e:3 * e + 3], S[:, tile, e, :], gpart[:, tile * E + e, :], start=(tile == 0), stop=(tile == NT - 1))
            mm.then_inc(weight_ready, 1)
            for e in range(E):
                if e >= 2:
                    pe.wait_ge(st_act if e % 2 == 0 else st_dve, e // 2)
                for tile in range(NT):
                    tr = pe.transpose(bank[3 + e % 2][:].bitcast(BF16)[:, tile * P:(tile + 1) * P], S[:, tile, e, :], ident_b[:])
                tr.then_inc(st_ready, 1)
            pe.wait_ge(s_moe, 32)
            for e in range(E + 1):
                if e < E:
                    pe.wait_ge(xgT_done, e // NG + 1)
                    wait(pe, hidE_done, NCH * (e - 1))
                    for c in range(NCH):
                        mm = pe.matmul(bank[5 + e % 2][:, c * CAP:(c + 1) * CAP], fc1s[:, e, c * P:(c + 1) * P], xgT[:, e, :], start=True, stop=True)
                    mm.then_inc(hidE_ready, 1)
                if e > 0:
                    pe.wait_ge(hidE_done, NCH * e)
                    if e == 1:
                        pe.wait_ge(weight_done, 1)
                    wait(pe, yb_done, e - 2)
                    for c in range(NCH):
                        mm = pe.matmul((bank[7], bank[2])[e % 2][:, 0:C], hidE[:, (e - 1) % 2, c, :], fc2s[:, e - 1, c, :], start=(c == 0), stop=(c == NCH - 1))
                    mm.then_inc(y_ready, 1)
            pe.wait_ge(st_act, E // 2)
            pe.wait_ge(st_dve, E // 2)
            pe.wait_ge(yw_done, E)
            for tile in range(NT):
                wait(pe, final_done, tile - 1)
                for e in range(E):
                    for i in range(3):
                        mm = pe.matmul(bank[tile % 2][:, 0:C], ST[:, e, tile * P:(tile + 1) * P], ypart[:, i, e, :],
                                       start=(e == 0 and i == 0), stop=(e == E - 1 and i == 2))
                mm.then_inc(scattered, 1)

        @block.vector
        def _(dve):
            dve.memset(count[:], 0.0)
            dve.memset(minus_half[:], -0.5).then_inc(consts_set, 1)
            dve.memset(v0[:, :, :, HD0:HD0 + 1], 1.0)
            dve.wait_ge(s_x, 16)
            for b in range(B):
                dve.bn_stats(stats[:, b, :], x[:, b, :]).then_inc(stat_link, 1)
            for b in range(B):
                dve.wait_ge(stat_link, b + 1)
                dve.bn_aggr(mv[:, b, :], stats[:, b, :]).then_inc(stat_link, 1)
            dve.wait_ge(stat_link, 2 * B)
            dve.tensor_scalar(var_eps[:], mv[:, :, 1], EPS0, None, ALU.add).then_inc(var_done, 1)
            dve.wait_ge(s_small, 80)
            dve.wait_ge(ada_ready, 1)
            for i, (chunk, one) in enumerate(((2, 1.0), (3, 1.0), (4, 0.0), (5, 0.0))):
                dve.tensor_scalar(mod[:, i, :], bank[7][:, i * B:(i + 1) * B], col("ada_b", chunk), one, ALU.add, ALU.add).then_inc(mod_done, 1)
            dve.tensor_scalar(shift1[:], bank[7][:, 4 * B:5 * B], col("b_ada"), col("ln1_b"), ALU.add, ALU.add).then_inc(mod_done, 1)
            for i in range(4):
                dve.wait_ge(gates_ready, 2 * i + 2)
                dve.tensor_tensor(gates[:, 2 * i:2 * i + 2, :], bank[i][:].rearrange("p (b c) -> p b c", b=2),
                                  bc(row("ada_b"), [P, 2, 2 * C], 1), ALU.add).then_inc(gates_done, 1)
            dve.wait_ge(gates_done, 4)
            dve.tensor_tensor(pg1[:], gates[:, :, 0:C], bc(row("proj_b"), [P, B, C], 1), ALU.mult).then_inc(gates_done, 1)
            dve.tensor_tensor(fg2[:], gates[:, :, C:2 * C], bc(row("fc2_b"), [P, B, C], 1), ALU.mult).then_inc(gates_done, 1)
            dve.wait_ge(gates_done, 6)
            dve.wait_ge(rstd_done, 1)

            def norm(b):
                wait(dve, zT_ready, b)
                dve.tensor_scalar(z[:], x[:, b, :], mv[:, b, 0:1], at(rstd[:], b), ALU.subtract, ALU.mult).then_inc(z_ready, 1)

            def save_qk(b):
                dve.wait_ge(qkv_ready, b + 1)
                wait(dve, rope_link, 3 * b)
                dve.tensor_tensor(qk0[:], qkv_ps[:, 0:2 * C], row("qkv_b")[:, 0:2 * C], ALU.add).then_inc(qkv_saved, 1)

            def save_v(b):
                dve.tensor_tensor(v0[:, b, :, 0:HD0], qkv_ps[:, 2 * C:3 * C].rearrange("p (h d) -> p h d", h=H),
                                  row("qkv_b")[:, 2 * C:3 * C].rearrange("p (h d) -> p h d", h=H), ALU.add).then_inc(v_done, 1)

            def row_max(b, g):
                n = NG * b + g
                dve.wait_ge(s_ready, n + 1)
                dve.tensor_reduce(neg_max[:, g, :], s_ps[g % 2][:].rearrange("p (h k) -> p h k", h=HG), AX, ALU.max, negate=True).then_inc(max_done, 1)

            def outputs(b, g):
                n = NG * b + g
                o = o_ps[:, 0:HG * (HD0 + 1)].rearrange("p (h d) -> p h d", h=HG)
                dve.wait_ge(o_ready, n + 1)
                dve.reciprocal(rinv[:, g, :], o[:, :, HD0]).then_inc(rec_done, 1)
                dve.wait_ge(rec_done, n + 1)
                if g == 0:
                    wait(dve, oT_ready, b)
                dve.tensor_tensor(o0[:, g * HG * HD0:(g + 1) * HG * HD0].rearrange("p (h d) -> p h d", h=HG), o[:, :, 0:HD0],
                                  bc(rinv[:, g, :], [P, HG, HD0], 2), ALU.mult).then_inc(o_done, 1)

            def offset(b):
                dve.tensor_tensor(x[:, b, :], x[:, b, :], pg1[:, b, :], ALU.add).then_inc(xb_done, 1)

            def residual(b):
                dve.wait_ge(proj_ready, b + 1)
                dve.tensor_tensor(delta[:], misc_ps[:, 0:C], gates[:, b, 0:C], ALU.mult).then_inc(gated_done, 1)
                dve.wait_ge(gated_done, b + 1)
                dve.wait_ge(xb_done, b + 1)
                dve.tensor_tensor(x[:, b, :], x[:, b, :], delta[:], ALU.add).then_inc(res_done, 1)

            def step(b, ahead):
                for g in range(NG):
                    late = back(b, g, 3)
                    if g == 0 and ahead:
                        norm(b + 1)
                    if real(late[0]):
                        outputs(*late)
                    if g == 1 and ahead:
                        save_qk(b + 1)
                    if g == 3 and real(b - 1):
                        offset(b - 1)
                    if real(b):
                        row_max(b, g)
                    if g == 1 and ahead:
                        save_v(b + 1)
                    if g == 3 and real(b - 1):
                        residual(b - 1)

            norm(0)
            save_qk(0)
            save_v(0)
            step(0, True)
            step(1, True)
            with dve.Fori(2, B - 1) as b:
                step(b, True)
            step(B - 1, False)
            step(B, False)
            for b in range(B):
                dve.wait_ge(res_done, b + 1)
                dve.bn_stats(stats[:, b, :], x[:, b, :]).then_inc(stat_link, 1)
            for b in range(B):
                dve.wait_ge(stat_link, 2 * B + b + 1)
                dve.bn_aggr(mv[:, b, :], stats[:, b, :]).then_inc(stat_link, 1)
            dve.wait_ge(stat_link, 4 * B)
            dve.tensor_scalar(var_eps[:], mv[:, :, 1], EPS0, None, ALU.add).then_inc(var_done, 1)
            dve.wait_ge(rstd_done, 2)
            for half in range(2):
                for i in range(NG):
                    b = NG * half + i
                    wait(dve, z4T_ready, half)
                    dve.tensor_scalar(z4[:, i, :], x[:, b, :], mv[:, b, 0:1], at(rstd[:], b), ALU.subtract, ALU.mult).then_inc(z4_done, 1)
                for i in range(NG):
                    b = NG * half + i
                    dve.wait_ge(z4_done, b + 1)
                    dve.tensor_tensor(x[:, b, :], x[:, b, :], fg2[:, b, :], ALU.add).then_inc(xf_done, 1)
                for i in range(NG):
                    b = NG * half + i
                    dve.wait_ge(ff_ready, b + 1)
                    dve.tensor_tensor(delta[:], (o_ps, misc_ps)[i % 2][:, 0:C], gates[:, b, C:2 * C], ALU.mult).then_inc(ffg_done, 1)
                    dve.wait_ge(ffg_done, b + 1)
                    dve.wait_ge(xf_done, b + 1)
                    dve.tensor_tensor(x[:, b, :], x[:, b, :], delta[:], ALU.add).then_inc(l0_done, 1)
                    dve.wait_ge(l0_done, b + 1)

            wqk_h = wqk[:].rearrange("p g (h d) -> p (g h) d", d=HD1)
            dve.wait_ge(s_l1, 48)
            dve.reduce_sum(wsum[:], wqk_h, AX).then_inc(wsum_done, 1)
            dve.wait_ge(wsum_done, 1)
            dve.scalar_tensor_tensor(wqk_h, bc(wsum[:], [P, 2 * H, HD1], 2), -1.0 / HD1, wqk_h, ALU.mult, ALU.add).then_inc(wqk_done, 1)
            dve.tensor_scalar(q_gain[:], col("qn_g"), float(HD1) ** -0.5, None, ALU.mult)
            dve.tensor_scalar(q_bias[:], col("qn_b"), float(HD1) ** -0.5, None, ALU.mult).then_inc(consts_set, 1)

            def token_stats(k, eps):
                for b in range(B):
                    dve.bn_stats(stats[:, b, :], x[:, b, :]).then_inc(stat_link, 1)
                for b in range(B):
                    dve.wait_ge(stat_link, 2 * B * k + b + 1)
                    dve.bn_aggr(mv[:, b, :], stats[:, b, :]).then_inc(stat_link, 1)
                dve.wait_ge(stat_link, 2 * B * (k + 1))
                dve.tensor_scalar(var_eps[:], mv[:, :, 1], eps, None, ALU.add).then_inc(var_done, 1)

            token_stats(2, EPS1)
            dve.wait_ge(rstd_done, 3)

            def norm1(b):
                wait(dve, z1T_ready, b)
                dve.tensor_scalar(z[:], x[:, b, :], mv[:, b, 0:1], at(rstd[:], b), ALU.subtract, ALU.mult).then_inc(z1_ready, 1)

            def row_max1(b, g):
                n = NG * b + g
                dve.wait_ge(s1_ready, n + 1)
                for a in range(2):
                    mx = dve.tensor_reduce(neg_max[:, g, 2 * a:2 * a + 2], s_ps[a][:, 0:2 * L].rearrange("p (i k) -> p i k", i=2), AX, ALU.max, negate=True)
                mx.then_inc(max1_done, 1)

            def sums(b, g):
                n = NG * b + g
                dve.wait_ge(squared, n + 1)
                dve.reduce_sum(sumsq[:], sq[:].rearrange("p (h d) -> p h d", d=HD1), AX).then_inc(sumsq_done, 1)
                dve.wait_ge(sumsq_done, n + 1)
                wait(dve, hrstd_done, n)
                dve.tensor_scalar(head_var[:], sumsq[:], 1.0 / HD1, EPS1, ALU.mult, ALU.add).then_inc(hvar_done, 1)

            def qk_normed(b, g):
                n = NG * b + g
                dve.wait_ge(hrstd_done, n + 1)
                wait(dve, qkT1_ready, n)
                dve.tensor_tensor(qkn[:].rearrange("p (h d) -> p h d", d=HD1), qk_ps[g % 2][:].rearrange("p (h d) -> p h d", d=HD1),
                                  bc(head_rstd[:], [P, 2 * HG, HD1], 2), ALU.mult).then_inc(qkn_done, 1)

            def row_sums1(b, g):
                n = NG * b + g
                dve.wait_ge(exp1_done, n + 1)
                dve.reduce_sum(rsum[:, g, :], prob[:, g, :].rearrange("p (h k) -> p h k", h=HG), AX).then_inc(rsum1_done, 1)

            def row_scales1(b, g):
                n = NG * b + g
                dve.wait_ge(rsum1_done, n + 1)
                dve.reciprocal(rinv[:, g, :], rsum[:, g, :]).then_inc(rec1_done, 1)

            def outputs1(b, g):
                n = NG * b + g
                dve.wait_ge(o1_ready, n + 1)
                dve.wait_ge(rec1_done, n + 1)
                wait(dve, oT1_ready, n)
                dve.tensor_tensor(o1[:].rearrange("p (h d) -> p h d", h=HG), o_ps[:, 0:HG * HD1].rearrange("p (h d) -> p h d", h=HG),
                                  bc(rinv[:, g, :], [P, HG, HD1], 2), ALU.mult).then_inc(o1_done, 1)

            def residual1(b):
                dve.wait_ge(proj1_ready, b + 1)
                dve.tensor_tensor(x[:, b, :], x[:, b, :], zp_ps[:, L:L + C], ALU.add).then_inc(res1_done, 1)

            def step1(b, ahead):
                for g in range(NG):
                    one, two, three, four = (back(b, g, lag) for lag in (1, 2, 3, 4))
                    if real(four[0]):
                        row_scales1(*four)
                    if g == 0 and real(b - 2):
                        residual1(b - 2)
                    if real(four[0]):
                        outputs1(*four)
                    if real(one[0]):
                        qk_normed(*one)
                    if g == NG - 2 and ahead:
                        norm1(b + 1)
                    if real(two[0]):
                        row_max1(*two)
                    if real(b):
                        sums(b, g)
                    if real(three[0]):
                        row_sums1(*three)

            norm1(0)
            step1(0, True)
            step1(1, True)
            with dve.Fori(2, B - 1) as b:
                step1(b, True)
            step1(B - 1, False)
            step1(B, False)
            residual1(B - 1)

            dve.wait_ge(res1_done, B)
            token_stats(3, EPS1)
            dve.wait_ge(xT_ready, 2)
            dve.tensor_copy(xT[:, NG * P:2 * NG * P], bank[1][:]).then_inc(xT_done2, 1)
            g3 = gate[:].rearrange("p (t e) -> p t e", e=E)
            logits = bank[2][:, 0:NTE].rearrange("p (t e) -> p t e", e=E)
            dve.wait_ge(logits_ready, 1)
            dve.reduce_max(gate_max[:], logits, AX).then_inc(gate_link, 1)
            dve.wait_ge(gate_link, 1)
            dve.tensor_tensor(g3, logits, bc(gate_max[:], [P, NT, E], 2), ALU.subtract).then_inc(gate_link, 1)
            dve.wait_ge(gate_exp, 1)
            dve.reduce_sum(gate_sum[:], g3, AX).then_inc(gate_link, 1)
            dve.wait_ge(gate_link, 3)
            dve.reciprocal(gate_max[:], gate_sum[:]).then_inc(gate_link, 1)
            dve.wait_ge(gate_link, 4)
            dve.tensor_tensor(g3, g3, bc(gate_max[:], [P, NT, E], 2), ALU.mult).then_inc(gate_done, 1)
            R = slice(0, NTE)
            dve.wait_ge(gateT_ready, 1)
            dve.tensor_copy(keys[R, :], bank[3][R, 0:P]).then_inc(key_link, 1)
            dve.wait_ge(key_link, 1)
            dve.tensor_scalar(key_i[R, 0, :], keys[R, :].bitcast(I32), KEY_HALF, None, ALU.logical_shift_right).then_inc(key_link, 1)
            dve.tensor_scalar(key_i[R, 1, :], keys[R, :].bitcast(I32), 2 ** KEY_HALF - 1, None, ALU.bitwise_and).then_inc(key_link, 1)
            dve.memset(cand[R, :], 2.0 ** (KEY_HALF - 1)).then_inc(narrowed, 1)
            dve.wait_ge(key_link, 3)
            dve.tensor_copy(key_hi[R, :], key_i[R, 0, :]).then_inc(key_link, 1)
            dve.tensor_copy(key_lo[R, :], key_i[R, 1, :]).then_inc(key_link, 1)
            dve.wait_ge(key_link, 5)

            def search(key, start):
                with dve.Fori(0, KEY_HALF) as k:
                    n = start + k
                    dve.wait_ge(narrowed, n + 1 + (1 if start else 0))
                    dve.tensor_scalar(hits[R, :], key[R, :], cand[R, :], 0.0, ALU.is_ge, ALU.add, accum_out=count[R, :]).then_inc(counted, 1)
                    dve.tensor_scalar(cand_low[R, :], cand[R, :], at(cst("steps")[R, :], k), None, ALU.subtract).then_inc(cand_link, 1)
                    dve.wait_ge(totalled, n + 1)
                    dve.tensor_scalar(step_up[R, :], bank[4][R, 0:1], CAP - 0.5, at(cst("bits")[R, :], k), ALU.is_ge, ALU.mult).then_inc(cand_link, 1)
                    dve.wait_ge(cand_link, 2 * n + 2)
                    dve.tensor_tensor(cand[R, :], step_up[R, :], cand_low[R, :], ALU.add).then_inc(narrowed, 1)

            search(key_hi, 0)
            dve.wait_ge(narrowed, KEY_HALF + 1)
            dve.tensor_scalar(above[R, :], key_hi[R, :], cand[R, :], 2.0 ** (KEY_HALF + 1), ALU.is_gt, ALU.mult).then_inc(key_link, 1)
            dve.tensor_scalar(eq_part[R, :], key_hi[R, :], cand[R, :], None, ALU.is_equal).then_inc(key_link, 1)
            dve.tensor_scalar(key_lo[R, :], key_lo[R, :], 1.0, None, ALU.add).then_inc(key_link, 1)
            dve.wait_ge(key_link, 8)
            dve.tensor_tensor(eq_part[R, :], eq_part[R, :], key_lo[R, :], ALU.mult).then_inc(key_link, 1)
            dve.memset(cand[R, :], 2.0 ** (KEY_HALF - 1)).then_inc(narrowed, 1)
            dve.wait_ge(key_link, 9)
            dve.scalar_tensor_tensor(keys[R, :], above[R, :], -1.0, eq_part[R, :], ALU.add, ALU.add).then_inc(key_link, 1)
            dve.wait_ge(key_link, 10)
            search(keys, KEY_HALF)
            dve.wait_ge(narrowed, 2 * KEY_HALF + 2)
            dve.tensor_scalar(masksT[R, 0, :], keys[R, :], cand[R, :], None, ALU.is_gt).then_inc(masksT_done, 1)
            dve.tensor_scalar(masksT[R, 1, :], keys[R, :], cand[R, :], None, ALU.is_equal).then_inc(masksT_done, 1)
            dve.wait_ge(masks_ready, 1)
            dve.tensor_copy(masks[:], bank[3][:].bitcast(BF16)[:, 0:2 * NTE].rearrange("p (a n) -> p a n", a=2)).then_inc(masks_done, 1)
            dve.wait_ge(masks_done, 1)
            dve.wait_ge(tie_rank_ready, 1)
            dve.scalar_tensor_tensor(tied[:], bank[5][:, 0:NTE], CAP - 0.5, masks[:, 1, :], ALU.is_lt, ALU.mult).then_inc(chosen_link, 1)
            dve.wait_ge(chosen_link, 1)
            dve.tensor_tensor(chosen[:], tied[:], masks[:, 0, :], ALU.add).then_inc(chosen_done, 1)
            dve.wait_ge(chosen_done, 1)
            dve.wait_ge(slots_ready, 1)
            dve.scalar_tensor_tensor(slot1[:], bank[6][:, 0:NTE], 1.0, chosen[:], ALU.add, ALU.mult).then_inc(slots_done, 1)
            dve.wait_ge(slots_done, 1)
            for half in range(2):
                for tile in range(NT):
                    for e in range(NG * half, NG * half + NG // 2):
                        dve.tensor_scalar(S[:, tile, e, :], iota_b[:], slot1[:, tile * E + e:tile * E + e + 1], None, ALU.is_equal).then_inc(s_dve, 1)
            dve.wait_ge(weight_ready, 1)
            dve.reduce_sum(weight[:], bank[2][:, 0:3 * E].rearrange("p (e a) -> p e a", a=3), AX).then_inc(weight_done, 1)
            dve.wait_ge(weight_done, 1)
            for e in range(1, E, 2):
                dve.wait_ge(st_ready, e + 1)
                dve.tensor_copy(ST[:, e, :], bank[4][:].bitcast(BF16)).then_inc(st_dve, 1)
            for e in range(E):
                dve.wait_ge(y_ready, e + 1)
                dve.tensor_tensor(yb[:, e % 2, :], (bank[2], bank[7])[e % 2][:, 0:C], row("b2s")[:, e * C:(e + 1) * C], ALU.add).then_inc(yb_done, 1)
                dve.wait_ge(yb_done, e + 1)
                dve.tensor_scalar(yw[:, e % 2, :], yb[:, e % 2, :], weight[:, e:e + 1], None, ALU.mult).then_inc(y_link, 1)
                rest = yw[:, e % 2, :]
                for i in range(3):
                    dve.wait_ge(y_link, 5 * e + 2 * i + 1)
                    part = dve.tensor_copy(ypart[:, i, e, :], rest)
                    if i < 2:
                        part.then_inc(y_link, 1)
                        dve.wait_ge(y_link, 5 * e + 2 * i + 2)
                        dve.tensor_tensor(yr[:, e % 2, i, :], rest, ypart[:, i, e, :], ALU.subtract).then_inc(y_link, 1)
                        rest = yr[:, e % 2, i, :]
                part.then_inc(yw_done, 1)
            for tile in range(NT):
                dve.wait_ge(scattered, tile + 1)
                dve.tensor_tensor(x[:, tile, :], x[:, tile, :], bank[tile % 2][:, 0:C], ALU.add).then_inc(final_done, 1)

        @block.scalar
        def _(act):
            act.wait_ge(s_small, 80)
            act.activation(silu_c[:], col("cond", 0, B), ACT.Silu).then_inc(silu_done, 1)
            act.wait_ge(mod_done, 5)

            def evac_hT(b):
                act.wait_ge(zT_ready, b + 1)
                wait(act, qkv_ready, b)
                act.activation(hT[:], misc_ps[:, 0:L], ACT.Identity, scale=at(mod[:, 0, :], b), bias=at(mod[:, 2, :], b)).then_inc(hT_ready, 1)

            def evac_kT(b):
                act.wait_ge(qkT_ready, b + 1)
                wait(act, kx_done, NG * b)
                act.activation(kT0[:], tp_ps[:, L:2 * L], ACT.Copy).then_inc(kT_done, 1)

            def evac_qT(b):
                act.wait_ge(qkT_ready, b + 1)
                wait(act, s_ready, NG * b)
                act.activation(qT0[:], tp_ps[:, 0:L], ACT.Copy, scale=float(HD0) ** -0.5).then_inc(qT_done, 1)

            def exps(b, g):
                n = NG * b + g
                act.wait_ge(max_done, n + 1)
                for i in range(HG):
                    ex = act.activation(prob[:, g, i * L:(i + 1) * L], s_ps[g % 2][:, i * L:(i + 1) * L], ACT.Exp,
                                        bias=neg_max[:, g, i:i + 1])
                ex.then_inc(exp_done, 1)

            def evac_pT(b, g):
                n = NG * b + g
                act.wait_ge(pT_ready, n + 1)
                wait(act, o_ready, n - 1)
                act.activation(probT[:, g % 2, :], pT_ps[:], ACT.Copy).then_inc(pT_done, 1)

            def evac_oT(b):
                act.wait_ge(oT_ready, b + 1)
                wait(act, proj_ready, b)
                act.activation(oT0[:], misc_ps[:, 0:L], ACT.Copy).then_inc(oT_done, 1)

            def step(b, ahead):
                for g in range(NG):
                    one, late = back(b, g, 1), back(b, g, 2)
                    if g == 0 and real(b):
                        evac_qT(b)
                    if g == 3 and real(b - 1):
                        evac_oT(b - 1)
                    if real(late[0]):
                        evac_pT(*late)
                    if g == 0 and ahead:
                        evac_hT(b + 1)
                    if real(one[0]):
                        exps(*one)
                    if g == 2 and ahead:
                        evac_kT(b + 1)

            evac_hT(0)
            evac_kT(0)
            step(0, True)
            step(1, True)
            with act.Fori(2, B - 1) as b:
                step(b, True)
            step(B - 1, False)
            step(B, False)
            for half in range(2):
                for i in range(NG):
                    b = NG * half + i
                    act.wait_ge(z4T_ready, half + 1)
                    wait(act, hid_ready, NCH * half)
                    act.activation(h4T[:, i * L:(i + 1) * L], tp_ps[:, i * L:(i + 1) * L], ACT.Identity,
                                   scale=mod[:, 1, b:b + 1], bias=mod[:, 3, b:b + 1]).then_inc(h4T_done, 1)
                for c in range(NCH):
                    act.wait_ge(hid_ready, NCH * half + c + 1)
                    wait(act, ff_ready, NG * half)
                    act.activation(hid[:, c, :], s_ps[c % 2][:], ACT.Gelu_apprx_tanh, bias=col("fc1_b", c)).then_inc(hid_done, 1)

            def evac_h1T(b):
                act.wait_ge(z1T_ready, b + 1)
                wait(act, qkv1_ready, NG * b)
                act.activation(hT[:], zp_ps[:, 0:L], ACT.Identity, scale=col("ln1_g"), bias=at(shift1[:], b)).then_inc(h1T_done, 1)

            def square(b, g):
                n = NG * b + g
                act.wait_ge(qk1_ready, n + 1)
                wait(act, sumsq_done, n)
                act.activation(sq[:], qk_ps[g % 2][:], ACT.Square).then_inc(squared, 1)

            def evac_v1(b, g):
                n = NG * b + g
                act.wait_ge(qkv1_ready, n + 1)
                wait(act, o1_ready, n - NG + 1)
                act.activation(v1[:, g, :], v_ps[:, 0:HG * HD1], ACT.Copy).then_inc(v1_done, 1)

            def evac_qk1T(b, g):
                n = NG * b + g
                act.wait_ge(qkT1_ready, n + 1)
                wait(act, s1_ready, n - NG + 1)
                for i, (gain, bias) in enumerate(((q_gain[:], q_bias[:]), (col("kn_g"), col("kn_b")))):
                    act.activation(qkT1[:, g, 2 * i:2 * i + 2, :], tp1_ps[:, 2 * i * L:2 * (i + 1) * L].rearrange("p (a k) -> p a k", a=2),
                                   ACT.Identity, scale=gain, bias=bias).then_inc(qkT1_done, 1)

            def exps1(b, g):
                n = NG * b + g
                act.wait_ge(max1_done, n + 1)
                for i in range(2):
                    for a in range(2):
                        ex = act.activation(prob[:, g, (2 * i + a) * L:(2 * i + a + 1) * L], s_ps[a][:, i * L:(i + 1) * L], ACT.Exp,
                                            bias=neg_max[:, g, 2 * a + i:2 * a + i + 1])
                ex.then_inc(exp1_done, 1)

            def evac_p1T(b, g):
                n = NG * b + g
                act.wait_ge(pT1_ready, n + 1)
                wait(act, o1_ready, n - 1)
                act.activation(probT[:, g % 2, :], pT_ps[:], ACT.Copy).then_inc(pT1_done, 1)

            def evac_o1T(b, g):
                n = NG * b + g
                act.wait_ge(oT1_ready, n + 1)
                wait(act, proj1_ready, b)
                act.activation(oT1[:, 2 * g:2 * g + 2, :], o_ps[:, HG * HD1:2 * HG * HD1].rearrange("p (a k) -> p a k", a=2), ACT.Copy).then_inc(oT1_done, 1)

            def step1(b, ahead):
                for g in range(NG):
                    two, three, four = (back(b, g, lag) for lag in (2, 3, 4))
                    if real(two[0]):
                        evac_qk1T(*two)
                    if real(three[0]):
                        evac_p1T(*three)
                    if real(four[0]):
                        evac_o1T(*four)
                    if real(b):
                        evac_v1(b, g)
                        square(b, g)
                    if g == NG - 1 and ahead:
                        evac_h1T(b + 1)
                    if real(two[0]):
                        exps1(*two)

            evac_h1T(0)
            act.wait_ge(consts_set, 2)
            step1(0, True)
            step1(1, True)
            with act.Fori(2, B - 1) as b:
                step1(b, True)
            step1(B - 1, False)
            step1(B, False)
            act.wait_ge(xT_ready, 1)
            act.activation(xT[:, 0:NG * P], bank[0][:], ACT.Copy).then_inc(xT_done, 1)
            act.wait_ge(gate_link, 2)
            act.activation(gate[:], gate[:], ACT.Exp).then_inc(gate_exp, 1)
            act.wait_ge(zx_done, NT)
            act.activation(zpart[:, 0, :, :], zx, ACT.Copy).then_inc(zcast, 1)
            for i in range(1, 3):
                act.wait_ge(zrest, i)
                act.activation(zpart[:, i, :, :], zr, ACT.Copy).then_inc(zcast, 1)
            act.wait_ge(gate_done, 1)
            act.activation(gpart[:, :, 0], gate[:], ACT.Copy).then_inc(gcast, 1)
            for i in range(1, 3):
                act.wait_ge(grest, i)
                act.activation(gpart[:, :, i], gr[:], ACT.Copy).then_inc(gcast, 1)
            for i in range(2):
                act.wait_ge(gathered, i + 1)
                act.activation(xgT[:, NG * i:NG * (i + 1), :], bank[i][:].rearrange("p (e s) -> p e s", e=NG), ACT.Identity,
                               scale=col("mlp_g"), bias=col("mlp_b")).then_inc(xgT_done, 1)
            for e in range(0, E, 2):
                act.wait_ge(st_ready, e + 1)
                act.activation(ST[:, e, :], bank[3][:].bitcast(BF16), ACT.Copy).then_inc(st_act, 1)
            for e in range(E):
                act.wait_ge(hidE_ready, e + 1)
                wait(act, y_ready, e - 1)
                for c in range(NCH):
                    act.activation(hidE[:, e % 2, c, :], bank[5 + e % 2][:, c * CAP:(c + 1) * CAP], ACT.Gelu_apprx_tanh,
                                   bias=col("b1s", e * NCH + c)).then_inc(hidE_done, 1)

        @block.gpsimd
        def _(pool):
            pool.wait_ge(consts_set, 1)
            pool.wait_ge(var_done, 1)
            pool.tensor_tensor(rstd[:], var_eps[:], minus_half[:], ALU.pow).then_inc(rstd_done, 1)
            pool.wait_ge(s_small, 80)

            def rope(b):
                src = qk0[:].rearrange("p (h a d) -> p h a d", h=2 * H, a=2)
                dst = rope_b[:].rearrange("p (h a d) -> p h a d", h=2 * H, a=2)
                half = HD0 // 2
                pool.wait_ge(qkv_saved, b + 1)
                wait(pool, roped_done, b)
                pool.tensor_tensor(rope_a[:].rearrange("p (h d) -> p h d", h=2 * H), qk0[:].rearrange("p (h d) -> p h d", h=2 * H),
                                   bc(cst("cos"), [P, 2 * H, HD0], 1), ALU.mult).then_inc(rope_link, 1)
                for a in range(2):
                    pool.tensor_tensor(dst[:, :, a, :], src[:, :, 1 - a, :],
                                       bc(cst("sin")[:, a * half:(a + 1) * half], [P, 2 * H, half], 1), ALU.mult).then_inc(rope_link, 1)
                pool.wait_ge(rope_link, 3 * b + 3)
                wait(pool, qkT_ready, b)
                pool.tensor_tensor(roped[:], rope_a[:], rope_b[:], ALU.add).then_inc(roped_done, 1)

            def spread(b, g):
                n = NG * b + g
                pool.wait_ge(kT_done, b + 1)
                wait(pool, s_ready, n - NG + 1)
                pool.tensor_tensor(kx[:, g, :, :], bc(kT0[:], [P, HG, L], 1),
                                   bc(cst("mask")[:, g * HG:(g + 1) * HG], [P, HG, L], 2), ALU.mult).then_inc(kx_done, 1)

            def front(b):
                rope(b)
                for g in range(NG):
                    spread(b, g)

            for b in range(2):
                front(b)
            with pool.Fori(2, B) as b:
                front(b)
            pool.wait_ge(var_done, 2)
            pool.tensor_tensor(rstd[:], var_eps[:], minus_half[:], ALU.pow).then_inc(rstd_done, 1)
            for dst, name in ((ident_b, "ident"), (before_b, "before"), (iota_b, "iota1"), (same_b, "same")):
                pool.tensor_copy(dst[:], cst(name))
            pool.memset(ones_b[:], 1.0).then_inc(cast_done, 1)
            pool.wait_ge(var_done, 3)
            pool.tensor_tensor(rstd[:], var_eps[:], minus_half[:], ALU.pow).then_inc(rstd_done, 1)

            def head_scales(b, g):
                n = NG * b + g
                pool.wait_ge(hvar_done, n + 1)
                wait(pool, qkn_done, n)
                pool.tensor_tensor(head_rstd[:], head_var[:], minus_half[:], ALU.pow).then_inc(hrstd_done, 1)

            for g in range(NG):
                head_scales(0, g)
            with pool.Fori(1, B) as b:
                for g in range(NG):
                    head_scales(b, g)
            pool.wait_ge(var_done, 4)
            pool.tensor_tensor(rstd[:], var_eps[:], minus_half[:], ALU.pow).then_inc(rstd_done, 1)
            pool.wait_ge(rstd_done, 4)
            for b in range(NT):
                pool.tensor_scalar(zx[:, b, :], x[:, b, :], mv[:, b, 0:1], rstd[:, b:b + 1], ALU.subtract, ALU.mult).then_inc(zx_done, 1)
            pool.wait_ge(zx_done, NT)
            pool.wait_ge(zcast, 1)
            pool.tensor_tensor(zr, zx, zpart[:, 0, :, :], ALU.subtract).then_inc(zrest, 1)
            pool.wait_ge(zcast, 2)
            pool.wait_ge(zrest, 1)
            pool.tensor_tensor(zr, zr, zpart[:, 1, :, :], ALU.subtract).then_inc(zrest, 1)
            pool.wait_ge(gcast, 1)
            pool.tensor_tensor(gr[:], gate[:], gpart[:, :, 0], ALU.subtract).then_inc(grest, 1)
            pool.wait_ge(gcast, 2)
            pool.wait_ge(grest, 1)
            pool.tensor_tensor(gr[:], gr[:], gpart[:, :, 1], ALU.subtract).then_inc(grest, 1)
            pool.wait_ge(slots_done, 1)
            for half in range(2):
                for tile in range(NT):
                    for e in range(NG * half + NG // 2, NG * (half + 1)):
                        pool.tensor_scalar(S[:, tile, e, :], iota_b[:], slot1[:, tile * E + e:tile * E + e + 1], None, ALU.is_equal).then_inc(s_pool, 1)


def constants():
    c = np.zeros((P, N_CONST), np.float32)

    def put(name, a):
        c[:a.shape[0], CONST[name][0]:CONST[name][1]] = a

    put("ident", np.eye(P))
    put("before", np.triu(np.ones((P, P)), 1))
    put("iota1", np.tile(np.arange(1, P + 1), (P, 1)))
    inv = (1.0 / np.float32(10000.0) ** (np.arange(0, HD0, 2, dtype=np.float32) / HD0)).astype(np.float32)
    ang = np.arange(L, dtype=np.float32)[:, None] * inv[None, :]
    put("cos", np.concatenate([np.cos(ang), np.cos(ang)], 1))
    put("sin", np.concatenate([-np.sin(ang), np.sin(ang)], 1))
    put("mask", np.arange(P)[:, None] // HD0 == np.arange(H)[None, :])
    bits = 2.0 ** np.arange(KEY_HALF - 1, -1, -1)
    put("bits", np.tile(bits, (P, 1)))
    put("steps", np.tile(np.maximum(bits / 2, 1.0), (P, 1)))
    same = np.zeros((P, P))
    same[:B * E, :B * E] = np.arange(B * E)[:, None] % E == np.arange(B * E)[None, :] % E
    put("same", same)
    return c


def laid_out(a):
    two = lambda v: np.concatenate([v, v]).reshape(P, 1)
    vec = lambda v, n: v.reshape(n, P).T
    wqkv = a["L1_cond_Wqkv"].reshape(3, NG, HG * HD1, C)
    parts = {
        "cond": a["cond_1024"].T, "ada_b": vec(a["L0_cond_ada_b"], 6), "fc1_b": vec(a["L0_cond_fc1_b"], NCH),
        "b_ada": vec(a["L1_cond_b_ada"], 1), "ln1_g": vec(a["L1_cond_ln1_g"], 1), "ln1_b": vec(a["L1_cond_ln1_b"], 1),
        "qn_g": two(a["L1_cond_qn_g"]), "qn_b": two(a["L1_cond_qn_b"]), "kn_g": two(a["L1_cond_kn_g"]), "kn_b": two(a["L1_cond_kn_b"]),
        "mlp_g": vec(a["L1_cond_mlp_g"], 1), "mlp_b": vec(a["L1_cond_mlp_b"], 1),
        "b1s": a["L1_cond_b1s"].reshape(E * NCH, P).T, "wgate": a["L1_cond_Wgate"].T,
    }
    rows = {"qkv_b": a["L0_cond_qkv_b"], "proj_b": a["L0_cond_proj_b"], "fc2_b": a["L0_cond_fc2_b"],
            "ada_b": a["L0_cond_ada_b"][:2 * C], "b2s": a["L1_cond_b2s"].reshape(-1)}
    out = {
        "x": a["x"],
        "cols": np.concatenate([parts[n] for n in COLS], 1),
        "rows": np.concatenate([rows[n] for n in ROWS]),
        "consts": constants(),
        "ada_w": a["L0_cond_ada_w"].T, "w_ada": a["L1_cond_W_ada"].T,
        "qkv_w": a["L0_cond_qkv_w"].T, "proj_w": a["L0_cond_proj_w"].T,
        "fc1_w": a["L0_cond_fc1_w"].T,
        "fc2_w": a["L0_cond_fc2_w"].reshape(C, NCH, P).transpose(2, 1, 0),
        "wqk": np.concatenate([wqkv[0], wqkv[1]], 1).transpose(2, 0, 1),
        "wv": wqkv[2].transpose(2, 0, 1),
        "wout": a["L1_cond_Wout"].reshape(C, 2 * NG, P).transpose(2, 1, 0),
        "fc1s": a["L1_cond_fc1s"].transpose(2, 0, 1),
        "fc2s": a["L1_cond_fc2s"].reshape(E, C, NCH, P).transpose(3, 0, 2, 1),
    }
    return {n: np.ascontiguousarray(v) for n, v in out.items()}


def kernel(**inputs):
    import concourse.bacc as bacc
    from concourse.bass_utils import run_bass_kernel_spmd

    arrays = laid_out({n: np.asarray(v) for n, v in inputs.items()})
    nc = bacc.Bacc("TRN2", target_bir_lowering=False, num_devices=1)
    t = {n: nc.dram_tensor(f"in_{n}", v.shape, mybir.dt.from_np(v.dtype), kind="ExternalInput").ap() for n, v in arrays.items()}
    t["out"] = nc.dram_tensor("out", (B, L, C), F32, kind="ExternalOutput").ap()
    program(nc, t)
    r = run_bass_kernel_spmd(nc, [{f"in_{n}": v for n, v in arrays.items()}], core_ids=[0])
    return r.results[0]["out"]
```

```python
from contextlib import ExitStack

import concourse.bass as bass
import numpy as np
from concourse import mybir

F32 = mybir.dt.float32
BF16 = mybir.dt.bfloat16
F32R = mybir.dt.float32r
I32 = mybir.dt.int32
ALU = mybir.AluOpType
ACT = mybir.ActivationFunctionType
AX = mybir.AxisListType.X

P = 128
B, L, C = 8, 128, 128
NG = 4
HG = 4
H = NG * HG
HD0, HD1 = C // H, 64
DFF = 4 * C
NCH = DFF // P
E = 8
CAP = B * L // E
EPS0, EPS1 = 1e-6, 1e-5
KEY_HALF = 15
DIGIT = 3
STEPS = KEY_HALF // DIGIT
TRIES = 2 ** DIGIT

COLS = {}
_at = 0
for _name, _n in (("cond", B), ("ada_b", 6), ("fc1_b", NCH), ("b_ada", 1), ("ln1_g", 1), ("ln1_b", 1),
                  ("qn_g", 1), ("qn_b", 1), ("kn_g", 1), ("kn_b", 1), ("mlp_g", 1), ("mlp_b", 1),
                  ("b1s", E * NCH), ("wgate", E)):
    COLS[_name] = (_at, _at + _n)
    _at += _n
N_COLS = _at
ROWS = {}
_at = 0
for _name, _n in (("qkv_b", 3 * C), ("proj_b", C), ("fc2_b", C), ("ada_b", 2 * C)):
    ROWS[_name] = (_at, _at + _n)
    _at += _n
N_ROWS = _at
CONST = {}
_at = 0
for _name, _n in (("ident", P), ("before", P), ("iota1", P), ("cos", HD0), ("sin", HD0), ("mask", H), ("same", 2 * P),
                  ("tries", STEPS * (TRIES // 2 + 1))):
    CONST[_name] = (_at, _at + _n)
    _at += _n
N_CONST = _at


def wait(eng, sem, count):
    if isinstance(count, int) and count <= 0:
        return
    eng.wait_ge(sem, count)


def back(b, g, lag):
    g -= lag
    while g < 0:
        g += NG
        b = b - 1
    return b, g


def real(b):
    return not isinstance(b, int) or 0 <= b < B


def at(ap, b):
    return ap.unsqueeze(2)[:, b, :]


def bc(ap, shape, axis):
    return ap.unsqueeze(axis).broadcast_to(shape)


def program(nc, t):
    with ExitStack() as ctx:
        def sb(name, shape, dt=F32):
            return ctx.enter_context(nc.sbuf_tensor(name, [P] + shape, dt))

        def sem(name):
            return ctx.enter_context(nc.semaphore(name))

        bank = [ctx.enter_context(nc.psum_tensor(f"bank{i}", [P, 512], F32)) for i in range(8)]

        x = sb("x_sb", [B, C])
        cols, rows, const = sb("cols_sb", [N_COLS]), sb("rows_sb", [N_ROWS]), sb("const_sb", [N_CONST])
        ada_w, w_ada = sb("ada_w_sb", [6 * C]), sb("w_ada_sb", [C])
        qkv_w, proj_w = sb("qkv_w_sb", [3 * C]), sb("proj_w_sb", [C])
        fc1_w, fc2_w = sb("fc1_w_sb", [DFF]), sb("fc2_w_sb", [NCH, C])
        wout = sb("wout_sb", [2 * NG, C])
        fc1s, fc2s, b2s = sb("fc1s_sb", [E, DFF]), sb("fc2s_sb", [E, NCH, C]), sb("b2s_sb", [E * C])

        def col(name, i=0, n=1):
            return cols[:, COLS[name][0] + i:COLS[name][0] + i + n]

        def row(name):
            return rows[:, ROWS[name][0]:ROWS[name][1]]

        def cst(name):
            return const[:, CONST[name][0]:CONST[name][1]]

        ident = cst("ident")

        silu_c, unused = sb("silu_c", [B]), sb("unused", [5])
        mod = sb("mod", [4, B])
        shift1 = sb("shift1", [B])
        gates = sb("gates", [B, 2 * C])
        fg2 = sb("fg2", [B, C])

        stats, mv = sb("stats", [B, 6]), sb("mv", [B, 2])
        var_eps, rstd = sb("var_eps", [B]), sb("rstd", [B])
        minus_half = sb("minus_half", [B])
        z = sb("z", [C])
        hT, h_hi, h_lo = sb("hT", [L]), sb("h_hi", [L], F32R), sb("h_lo", [L], F32R)

        qk0 = sb("qk0", [2 * C])
        rope_a, rope_b, roped = sb("rope_a", [2 * C]), sb("rope_b", [2 * C]), sb("roped", [2 * C])
        qT0, kT0 = sb("qT0", [L]), sb("kT0", [L])
        v0 = sb("v0", [B, H, HD0 + 1])
        neg_max = sb("neg_max", [NG, HG])
        prob = sb("prob", [NG, HG * L])
        probT = sb("probT", [2, HG * L])
        rsum, rinv = sb("rsum", [NG, HG]), sb("rinv", [NG, HG])
        o0 = sb("o0", [C])
        oT0 = sb("oT0", [L])
        delta = sb("delta", [2, C])
        z4, h4T = sb("z4", [NG, C]), sb("h4T", [NG * L])
        hid = sb("hid", [NCH, NG * L])

        wsum = sb("wsum", [2 * H])
        q_gain, q_bias = sb("q_gain", [1]), sb("q_bias", [1])
        sq, sumsq, head_var, head_rstd = sb("sq", [2 * HG * HD1]), sb("sumsq", [2 * HG]), sb("head_var", [2 * HG]), sb("head_rstd", [2 * HG])
        qkn = sb("qkn", [2 * HG * HD1])
        qkT1 = sb("qkT1", [NG, HG, L])
        v1 = sb("v1", [NG, HG * HD1])
        o1 = sb("o1", [HG * HD1])
        oT1 = sb("oT1", [2 * NG, L])
        with ExitStack() as whole:
            def first(name, shape):
                return whole.enter_context(nc.sbuf_tensor(name, [P] + shape, F32))

            wqk, wv = first("wqk_sb", [NG, 2 * HG * HD1]), first("wv_sb", [NG, HG * HD1])
            kx = first("kx", [NG, HG, L])
            pg1 = first("pg1", [B, C])
        wqk_lo, wv_lo = sb("wqk_lo", [NG, 2 * HG * HD1], F32R), sb("wv_lo", [NG, HG * HD1], F32R)
        wqk_hi, wv_hi = sb("wqk_hi", [NG, 2 * HG * HD1], F32R), sb("wv_hi", [NG, HG * HD1], F32R)
        NT = B
        NTE = NT * E
        S_DVE = 6
        xT = fg2[:].rearrange("p b c -> p (b c)")
        zx, zr = gates[:, 0:NT // 2, :].rearrange("p b (a c) -> p (b a) c", a=2), pg1[:]
        xgT = qkT1[:, 0:NG // 2, :, :].rearrange("p g h l -> p (g h) l")
        gate, gate_max, gate_sum = sb("gate", [2, NTE]), sb("gate_max", [NT]), sb("gate_sum", [NT])
        keys, key_hi, key_lo, key_i = sb("keys", [P]), sb("key_hi", [P]), sb("key_lo", [P]), sb("key_i", [2, P], I32)
        above, eq_part = sb("above", [P]), sb("eq_part", [P])
        hits, count = sb("hits", [TRIES // 2, P], BF16), sb("count", [TRIES // 2], BF16)
        cand, cand_from, fitting = sb("cand", [TRIES // 2 + 1]), sb("cand_from", [TRIES // 2 + 1]), sb("fitting", [1])
        fits = sb("fits", [TRIES])
        masksT = sb("masksT", [2, P], BF16)
        masks = sb("masks", [2, NTE], BF16)
        tied = sb("tied", [NTE], BF16)
        chosen = sb("chosen", [NTE], BF16)
        slot1 = sb("slot1", [NTE])
        ident_b, before_b, ones_b = sb("ident_b", [P], BF16), sb("before_b", [P], BF16), sb("ones_b", [P], BF16)
        iota_b, same_b = sb("iota_b", [P], BF16), sb("same_b", [2, P], BF16)
        S = sb("S", [NT, E, CAP], BF16)
        ST = sb("ST", [NT, E, P], BF16)
        zpart = sb("zpart", [3, NT, C], BF16)
        gr, gpart = sb("gr", [NTE]), sb("gpart", [NTE, 3], BF16)
        weight = sb("weight", [E])
        hidE = hid[:].rearrange("p c (e s) -> p e c s", e=NG)
        bw, yw, yr = sb("bw", [E, C]), sb("yw", [2, C]), sq[:].rearrange("p (a i c) -> p a i c", a=2, i=2)
        ypart = kx[:, 0:3, :, :].rearrange("p g h l -> p g (h l)").bitcast(BF16).rearrange("p g (e c) -> p g e c", e=E)

        s_x, s_small, s_l0, s_l1, s_moe = sem("x_loaded"), sem("small_loaded"), sem("l0_loaded"), sem("l1_loaded"), sem("moe_loaded")
        silu_done, ada_ready, mod_done, gates_ready, gates_done = sem("silu_done"), sem("ada_ready"), sem("mod_done"), sem("gates_ready"), sem("gates_done")
        consts_set, stat_link, var_done, rstd_done = sem("consts_set"), sem("stat_link"), sem("var_done"), sem("rstd_done")
        z_ready, zT_ready, hT_ready, qkv_ready, qkv_saved = sem("z_ready"), sem("zT_ready"), sem("hT_ready"), sem("qkv_ready"), sem("qkv_saved")
        rope_link, roped_done, qkT_ready, qT_done, kT_done, kx_done, v_done = sem("rope_link"), sem("roped_done"), sem("qkT_ready"), sem("qT_done"), sem("kT_done"), sem("kx_done"), sem("v_done")
        s_ready, max_done, sub_done, exp_done = sem("s_ready"), sem("max_done"), sem("sub_done"), sem("exp_done")
        pT_ready, pT_done, o_ready, rec_done, o_done = sem("pT_ready"), sem("pT_done"), sem("o_ready"), sem("rec_done"), sem("o_done")
        oT_ready, oT_done, proj_ready, xb_done, gated_done, res_done = sem("oT_ready"), sem("oT_done"), sem("proj_ready"), sem("xb_done"), sem("gated_done"), sem("res_done")
        z4_done, z4T_ready, h4T_done, hid_ready, hid_done, ff_ready = sem("z4_done"), sem("z4T_ready"), sem("h4T_done"), sem("hid_ready"), sem("hid_done"), sem("ff_ready")
        ffg_done, l0_done, xf_done = sem("ffg_done"), sem("l0_done"), sem("xf_done")
        wsum_done, wqk_done, z1_ready, z1T_ready, h1T_done, qk1_ready, qkv1_ready = sem("wsum_done"), sem("wqk_done"), sem("z1_ready"), sem("z1T_ready"), sem("h1T_done"), sem("qk1_ready"), sem("qkv1_ready")
        squared, sumsq_done, hvar_done, hrstd_done, qkn_done, v1_done = sem("squared"), sem("sumsq_done"), sem("hvar_done"), sem("hrstd_done"), sem("qkn_done"), sem("v1_done")
        qkT1_ready, qT1_done, kT1_done, s1_ready, max1_done, rsum1_done, exp1_done = sem("qkT1_ready"), sem("qT1_done"), sem("kT1_done"), sem("s1_ready"), sem("max1_done"), sem("rsum1_done"), sem("exp1_done")
        pT1_ready, pT1_done, o1_ready, rec1_done, o1_done = sem("pT1_ready"), sem("pT1_done"), sem("o1_ready"), sem("rec1_done"), sem("o1_done")
        oT1_ready, oT1_done, proj1_ready, res1_done = sem("oT1_ready"), sem("oT1_done"), sem("proj1_ready"), sem("res1_done")
        xT_ready, xT_done, logits_ready, gate_link, gate_exp, gate_done = sem("xT_ready"), sem("xT_done"), sem("logits_ready"), sem("gate_link"), sem("gate_exp"), sem("gate_done")
        gateT_ready, key_link, counted, totalled, cand_link, narrowed = sem("gateT_ready"), sem("key_link"), sem("counted"), sem("totalled"), sem("cand_link"), sem("narrowed")
        masksT_done, masks_ready, masks_done, tie_rank_ready, chosen_link, chosen_done = sem("masksT_done"), sem("masks_ready"), sem("masks_done"), sem("tie_rank_ready"), sem("chosen_link"), sem("chosen_done")
        slots_ready, slots_done, s_dve, s_pool, cast_done = sem("slots_ready"), sem("slots_done"), sem("s_dve"), sem("s_pool"), sem("cast_done")
        zx_done, zcast, zrest, gcast, grest = sem("zx_done"), sem("zcast"), sem("zrest"), sem("gcast"), sem("grest")
        gathered, xgT_done, weight_ready, weight_done, st_ready, st_done = sem("gathered"), sem("xgT_done"), sem("weight_ready"), sem("weight_done"), sem("st_ready"), sem("st_done")
        hidE_ready, hidE_done, y_ready, yw_done, scattered, final_done = sem("hidE_ready"), sem("hidE_done"), sem("y_ready"), sem("yw_done"), sem("scattered"), sem("final_done")
        xT_done2, bw_done, y_parts = sem("xT_done2"), sem("bw_done"), sem("y_parts")
        y_part, y_rest = [sem("y_part0"), sem("y_part1")], [sem("y_rest0"), sem("y_rest1")]
        w_split, wqk_hi_done, wv_split, h_split = sem("w_split"), sem("wqk_hi_done"), sem("wv_split"), sem("h_split")
        stat_done, moments_done = sem("stat_done"), sem("moments_done")
        s_const, s_qkv_w, s_rows, offsets_done = sem("const_loaded"), sem("qkv_w_loaded"), sem("rows_loaded"), sem("offsets_done")
        s_out = sem("out_stored")

        qkv_ps, tp_ps, pT_ps, o_ps, misc_ps = bank[0], bank[1], bank[4], bank[5], bank[6]
        s_ps = [bank[2], bank[3]]
        gate_ps = [bank[4], bank[5], bank[3], bank[7]]
        proj_ps, z4_ps = bank[7], [bank[6], bank[7]]
        hid_ps = [bank[0], bank[1], bank[2], bank[3]]
        qk_ps, v_ps, zp_ps, tp1_ps = [bank[0], bank[6]], bank[1], bank[1][:, HG * HD1:], bank[7]

        block = ctx.enter_context(nc.Block())

        @block.sync
        def _(sp):
            sp.dma_start(x[:], t["x"].rearrange("b t c -> t b c")).then_inc(s_x, 16)
            sp.dma_start(cols[:], t["cols"]).then_inc(s_small, 16)
            sp.dma_start(ada_w[:], t["ada_w"]).then_inc(s_small, 16)
            sp.dma_start(w_ada[:], t["w_ada"]).then_inc(s_small, 16)
            sp.dma_start(const[:], t["consts"]).then_inc(s_const, 16)
            sp.dma_start(qkv_w[:], t["qkv_w"]).then_inc(s_qkv_w, 16)
            sp.dma_start(rows[:], t["rows"].partition_broadcast(P)).then_inc(s_rows, 16)
            sp.dma_start(proj_w[:], t["proj_w"]).then_inc(s_l0, 16)
            sp.dma_start(fc1_w[:], t["fc1_w"]).then_inc(s_l0, 16)
            sp.dma_start(fc2_w[:], t["fc2_w"]).then_inc(s_l0, 16)
            sp.dma_start(wqk[:], t["wqk"]).then_inc(s_l1, 16)
            sp.dma_start(wv[:], t["wv"]).then_inc(s_l1, 16)
            sp.dma_start(wout[:], t["wout"]).then_inc(s_l1, 16)
            sp.dma_start(fc1s[:], t["fc1s"]).then_inc(s_moe, 16)
            sp.dma_start(fc2s[:], t["fc2s"]).then_inc(s_moe, 16)
            sp.dma_start(b2s[:], t["b2s"].partition_broadcast(P)).then_inc(s_moe, 16)
            for i in range(2):
                sp.wait_ge(final_done, NT // 2 * (i + 1))
                half = slice(i * NT // 2, (i + 1) * NT // 2)
                sp.dma_start(t["out"][half].rearrange("b t c -> t b c"), x[:, half, :]).then_inc(s_out, 16)
            sp.wait_ge(s_out, 32)

        @block.tensor
        def _(pe):
            pe.wait_ge(s_small, 48)
            pe.wait_ge(silu_done, 1)
            for i, chunk in enumerate((2, 3, 4, 5)):
                pe.matmul(bank[7][:, i * B:(i + 1) * B], ada_w[:, chunk * C:(chunk + 1) * C], silu_c[:], start=True, stop=True)
            pe.matmul(bank[7][:, 4 * B:5 * B], w_ada[:], silu_c[:], start=True, stop=True).then_inc(ada_ready, 1)
            pe.wait_ge(s_const, 16)

            def gate_rows(i):
                for j in range(2):
                    b = 2 * i + j
                    pe.matmul(gate_ps[i][:, j * 2 * C:(j + 1) * 2 * C], silu_c[:, b:b + 1].broadcast_to([P, P]),
                              ada_w[:, 0:2 * C], start=True, stop=True).then_inc(gates_ready, 1)

            def zT(b):
                pe.wait_ge(z_ready, b + 1)
                pe.transpose(misc_ps[:, 0:L], z[:], ident).then_inc(zT_ready, 1)

            def qkv(b):
                pe.wait_ge(hT_ready, b + 1)
                wait(pe, v_done, b)
                pe.matmul(qkv_ps[:, 0:3 * C], hT[:], qkv_w[:], start=True, stop=True).then_inc(qkv_ready, 1)

            def qkT(b):
                pe.wait_ge(roped_done, b + 1)
                wait(pe, qT_done, b)
                pe.transpose(tp_ps[:, 0:L], roped[:, 0:C], ident)
                pe.transpose(tp_ps[:, L:2 * L], roped[:, C:2 * C], ident).then_inc(qkT_ready, 1)

            def scores(b, g):
                n = NG * b + g
                pe.wait_ge(kx_done, n + 1)
                if g == 0:
                    pe.wait_ge(qT_done, b + 1)
                wait(pe, exp_done, n - 1)
                pe.matmul(s_ps[g % 2][:], qT0[:], kx[:, g, :, :], start=True, stop=True).then_inc(s_ready, 1)

            def probsT(b, g):
                n = NG * b + g
                pe.wait_ge(exp_done, n + 1)
                wait(pe, pT_done, n)
                for i in range(HG):
                    tr = pe.transpose(pT_ps[:, i * L:(i + 1) * L], prob[:, g, i * L:(i + 1) * L], ident)
                tr.then_inc(pT_ready, 1)

            def values(b, g):
                n = NG * b + g
                pe.wait_ge(pT_done, n + 1)
                pe.wait_ge(v_done, b + 1)
                wait(pe, o_done, n)
                for i in range(HG):
                    mm = pe.matmul(o_ps[:, i * (HD0 + 1):(i + 1) * (HD0 + 1)], probT[:, g % 2, i * L:(i + 1) * L],
                                   v0[:, b, g * HG + i, :], start=True, stop=True)
                mm.then_inc(o_ready, 1)

            def oT(b):
                pe.wait_ge(o_done, NG * (b + 1))
                wait(pe, res_done, b)
                pe.transpose(proj_ps[:, 0:L], o0[:], ident).then_inc(oT_ready, 1)

            def proj(b):
                pe.wait_ge(oT_done, b + 1)
                pe.matmul(proj_ps[:, L:L + C], oT0[:], proj_w[:], start=True, stop=True).then_inc(proj_ready, 1)

            def step(b, ahead):
                for g in range(NG):
                    two, late = back(b, g, 2), back(b, g, 3)
                    if real(two[0]):
                        probsT(*two)
                    if g == 0 and real(b - 2):
                        proj(b - 2)
                    if real(b):
                        scores(b, g)
                    if g == 0 and ahead:
                        zT(b + 1)
                    if g == 3 and real(b - 1):
                        oT(b - 1)
                    if real(late[0]):
                        values(*late)
                    if g == 0 and ahead:
                        qkv(b + 1)
                    if g == 2 and ahead:
                        qkT(b + 1)

            zT(0)
            pe.wait_ge(s_qkv_w, 16)
            qkv(0)
            for i in range(2):
                gate_rows(i)
            qkT(0)
            pe.wait_ge(mod_done, 5)
            gate_rows(2)
            pe.wait_ge(gates_done, 3)
            step(0, True)
            gate_rows(3)
            pe.wait_ge(gates_done, 4)
            pe.wait_ge(s_l0, 48)
            step(1, True)
            with pe.Fori(2, B - 1) as b:
                step(b, True)
            def z4T(half):
                pe.wait_ge(z4_done, NG * (half + 1))
                wait(pe, h4T_done, NG * half)
                for i in range(NG):
                    tr = pe.transpose(z4_ps[half][:, i * L:(i + 1) * L], z4[:, i, :], ident)
                tr.then_inc(z4T_ready, 1)

            def hidden(half, c):
                if c == 0:
                    pe.wait_ge(h4T_done, NG * (half + 1))
                wait(pe, hid_done, NCH * (half - 1) + c + 1)
                pe.matmul(hid_ps[c][:], fc1_w[:, c * P:(c + 1) * P], h4T[:], start=True, stop=True).then_inc(hid_ready, 1)

            def mlp_out(half):
                pe.wait_ge(hid_done, NCH * (half + 1))
                for i in range(NG):
                    n = NG * half + i
                    wait(pe, ffg_done, n - 1)
                    for c in range(NCH):
                        mm = pe.matmul((o_ps, misc_ps)[i % 2][:, 0:C], hid[:, c, i * L:(i + 1) * L], fc2_w[:, c, :],
                                       start=(c == 0), stop=(c == NCH - 1))
                    mm.then_inc(ff_ready, 1)

            def z1T(b):
                pe.wait_ge(z1_ready, b + 1)
                wait(pe, v1_done, NG * b)
                pe.transpose(zp_ps[:, 0:L], z[:], ident).then_inc(z1T_ready, 1)

            step(B - 1, False)
            proj(B - 2)
            probsT(B - 1, 2)
            values(B - 1, 1)
            z4T(0)
            probsT(B - 1, 3)
            values(B - 1, 2)
            values(B - 1, 3)
            oT(B - 1)
            hidden(0, 0)
            proj(B - 1)
            for c in range(1, NCH):
                hidden(0, c)
            pe.wait_ge(res_done, B)
            z4T(1)
            mlp_out(0)
            for c in range(NCH):
                hidden(1, c)
            pe.wait_ge(hid_done, NCH + 2)
            z1T(0)
            mlp_out(1)

            def split_product(out, w_hi, w_lo):
                pe.matmul(out, h_hi[:], w_hi, start=True, stop=False)
                pe.matmul(out, h_hi[:], w_lo, start=False, stop=False)
                return pe.matmul(out, h_lo[:], w_hi, start=False, stop=True)

            def qkv1(b, g):
                n = NG * b + g
                pe.wait_ge(h_split, 2 * b + 2)
                if isinstance(b, int) and b == 0:
                    pe.wait_ge(w_split, g + 1)
                if isinstance(b, int) and n == 1:
                    pe.wait_ge(ffg_done, B)
                wait(pe, qkn_done, n - 1)
                split_product(qk_ps[g % 2][:], wqk_hi[:, g, :], wqk_lo[:, g, :]).then_inc(qk1_ready, 1)
                wait(pe, v1_done, n)
                if g == 0:
                    wait(pe, res1_done, b - 1)
                split_product(v_ps[:, 0:HG * HD1], wv_hi[:, g, :], wv_lo[:, g, :]).then_inc(qkv1_ready, 1)

            def qk1T(b, g):
                n = NG * b + g
                pe.wait_ge(qkn_done, n + 1)
                wait(pe, qT1_done, n)
                for i in range(HG):
                    tr = pe.transpose(tp1_ps[:, i * L:(i + 1) * L], qkn[:, i * P:(i + 1) * P], ident)
                tr.then_inc(qkT1_ready, 1)

            def scores1(b, g):
                n = NG * b + g
                pe.wait_ge(qT1_done, n + 1)
                wait(pe, exp1_done, n)
                for i in range(2):
                    for odd in range(2):
                        rows_ = slice(odd * HD1, (odd + 1) * HD1)
                        mm = pe.matmul(s_ps[odd][:, i * L:(i + 1) * L], qkT1[rows_, g, i, :], qkT1[rows_, g, 2 + i, :], start=True, stop=True)
                mm.then_inc(s1_ready, 1)

            def probs1T(b, g):
                n = NG * b + g
                pe.wait_ge(exp1_done, n + 1)
                wait(pe, pT1_done, n)
                for i in range(HG):
                    tr = pe.transpose(pT_ps[:, i * L:(i + 1) * L], prob[:, g, i * L:(i + 1) * L], ident)
                tr.then_inc(pT1_ready, 1)

            def values1(b, g):
                n = NG * b + g
                pe.wait_ge(pT1_done, n + 1)
                wait(pe, oT1_done, n)
                for i in range(HG):
                    mm = pe.matmul(o_ps[:, i * HD1:(i + 1) * HD1], probT[:, g % 2, i * L:(i + 1) * L],
                                   v1[:, g, i * HD1:(i + 1) * HD1], start=True, stop=True)
                mm.then_inc(o1_ready, 1)

            def o1T(b, g):
                n = NG * b + g
                pe.wait_ge(o1_done, n + 1)
                for i in range(2):
                    tr = pe.transpose(o_ps[:, HG * HD1 + i * L:HG * HD1 + (i + 1) * L], o1[:, i * P:(i + 1) * P], ident)
                tr.then_inc(oT1_ready, 1)

            def proj1(b, groups=range(NG)):
                pe.wait_ge(oT1_done, NG * b + groups[-1] + 1)
                if not isinstance(b, int) or b + 2 < B:
                    pe.wait_ge(h1T_done, b + 3)
                if not isinstance(b, int) or b + 1 < B:
                    pe.wait_ge(v1_done, NG * (b + 2))
                for i in range(2 * groups[0], 2 * groups[-1] + 2):
                    mm = pe.matmul(zp_ps[:, L:L + C], oT1[:, i, :], wout[:, i, :], start=(i == 0), stop=(i == 2 * NG - 1))
                if groups[-1] == NG - 1:
                    mm.then_inc(proj1_ready, 1)

            x_ps, logit_ps = [bank[0], bank[6]], bank[7]

            def transposed_x(first, end):
                for b in range(first, end):
                    tr = pe.transpose(x_ps[b // NG][:, b % NG * P:(b % NG + 1) * P], x[:, b, :], ident)
                tr.then_inc(xT_ready, 1)

            def logits(first, end):
                pe.wait_ge(xT_done, 2 if end < B else 3)
                for b in range(first, end):
                    mm = pe.matmul(logit_ps[:, b * E:(b + 1) * E], xT[:, b * P:(b + 1) * P], col("wgate", 0, E), start=True, stop=True)
                if end == B:
                    mm.then_inc(logits_ready, 1)

            def step1(b, ahead):
                for g in range(NG):
                    one, two, three, four = (back(b, g, lag) for lag in (1, 2, 3, 4))
                    if real(b):
                        qkv1(b, g)
                    if real(three[0]):
                        probs1T(*three)
                    if real(four[0]):
                        o1T(*four)
                    if real(two[0]):
                        scores1(*two)
                    if real(three[0]):
                        values1(*three)
                    if g == NG - 1 and ahead:
                        z1T(b + 1)
                    if real(one[0]):
                        qk1T(*one)
                    if g == NG - 1 and real(b - 1):
                        proj1(b - 1, range(NG) if real(b) else range(NG - 1, NG))
                    if g == NG - 2 and not real(b):
                        logits(0, B - 1)
                        proj1(b - 1, range(NG - 1))
                    if g == 1 and not real(b):
                        pe.wait_ge(res1_done, B - 1)
                        pe.wait_ge(qkn_done, NG * B)
                        transposed_x(0, NG)
                        transposed_x(NG, B - 1)

            pe.wait_ge(wv_split, 2)
            step1(0, True)
            step1(1, True)
            with pe.Fori(2, B - 1) as b:
                step1(b, True)
            step1(B - 1, False)
            step1(B, False)

            pe.wait_ge(res1_done, B)
            transposed_x(B - 1, B)
            logits(B - 1, B)
            pe.wait_ge(gate_done, 2)
            pe.transpose(bank[3][:, 0:P], gate[:].rearrange("p a n -> p (a n)"), ident).then_inc(gateT_ready, 1)
            pe.wait_ge(cast_done, 1)
            with pe.Fori(0, 2 * STEPS) as k:
                pe.wait_ge(counted, TRIES // 2 * k + TRIES // 2)
                for a in range(2):
                    mm = pe.matmul(bank[4][:, a * TRIES // 2:(a + 1) * TRIES // 2], same_b[:, a, :], count[:], start=True, stop=True)
                mm.then_inc(totalled, 1)
            pe.wait_ge(masksT_done, 2)
            masks_ps = bank[3][:].bitcast(BF16)
            for i in range(2):
                tr = pe.transpose(masks_ps[:, i * NTE:(i + 1) * NTE], masksT[0:NTE, i, :], ident_b[0:NTE, 0:NTE])
            tr.then_inc(masks_ready, 1)
            pe.wait_ge(masks_done, 1)

            def ranks(ps, m, more):
                pe.matmul(ps[:, 0:NTE], before_b[:], m[:, 0:NTE], start=True, stop=False, skip_group_check=True)
                for i in range(1, NT):
                    mm = pe.matmul(ps[:, i * E:NTE], ones_b[:], m[:, 0:NTE - i * E], start=False, stop=(not more and i == NT - 1), skip_group_check=True)
                return mm

            ranks(bank[5], masks[:, 1, :], True)
            for i in range(NT):
                mm = pe.matmul(bank[5][:, 0:NTE].rearrange("p (t e) -> p t e", t=NT), ones_b[:],
                               bc(masks[:, 0, i * E:(i + 1) * E], [P, NT, E], 1), start=False, stop=(i == NT - 1), skip_group_check=True)
            mm.then_inc(tie_rank_ready, 1)
            pe.wait_ge(chosen_done, 1)
            ranks(bank[6], chosen[:], False).then_inc(slots_ready, 1)
            pe.wait_ge(zcast, 3)
            for tile in range(NT):
                for i in range(2):
                    if i == 0:
                        pe.wait_ge(s_dve, S_DVE * tile + NG)
                    else:
                        pe.wait_ge(s_dve, S_DVE * (tile + 1))
                        pe.wait_ge(s_pool, (E - S_DVE) * (tile + 1))
                    for part in range(3):
                        mm = pe.matmul(bank[i][:], zpart[:, part, tile, :], S[:, tile, NG * i:NG * (i + 1), :],
                                       start=(tile == 0 and part == 0), stop=(tile == NT - 1 and part == 2))
                mm.then_inc(gathered, 1)
                wait(pe, st_done, tile - 1)
                for e in range(E):
                    tr = pe.transpose(bank[3 + tile % 2][:].bitcast(BF16)[:, e * P:(e + 1) * P], S[:, tile, e, :], ident_b[:])
                tr.then_inc(st_ready, 1)
            pe.wait_ge(gcast, 3)
            for e in range(E):
                for tile in range(NT):
                    mm = pe.matmul(bank[2][:, 3 * e:3 * e + 3], S[:, tile, e, :], gpart[:, tile * E + e, :], start=(tile == 0), stop=(tile == NT - 1))
            mm.then_inc(weight_ready, 1)
            pe.wait_ge(s_moe, 48)
            for e in range(E + 1):
                if e < E:
                    pe.wait_ge(xgT_done, e // NG + 1)
                    wait(pe, hidE_done, NCH * (e - 1))
                    for c in range(NCH):
                        mm = pe.matmul(bank[5 + e % 2][:, c * CAP:(c + 1) * CAP], fc1s[:, e, c * P:(c + 1) * P], xgT[:, e, :], start=True, stop=True)
                    mm.then_inc(hidE_ready, 1)
                if e > 0:
                    pe.wait_ge(hidE_done, NCH * e)
                    if e == 1:
                        pe.wait_ge(weight_done, 1)
                    wait(pe, yw_done, e - 2)
                    for c in range(NCH):
                        mm = pe.matmul((bank[7], bank[2])[e % 2][:, 0:C], hidE[:, (e - 1) % 2, c, :], fc2s[:, e - 1, c, :], start=(c == 0), stop=(c == NCH - 1))
                    mm.then_inc(y_ready, 1)
            pe.wait_ge(st_done, NT)
            for tile in range(NT):
                wait(pe, final_done, tile - 1)
                for e in range(E):
                    if tile == 0:
                        pe.wait_ge(y_parts, e + 1)
                    for i in range(3):
                        mm = pe.matmul(bank[tile % 2][:, 0:C], ST[:, tile, e, :], ypart[:, i, e, :],
                                       start=(e == 0 and i == 0), stop=(e == E - 1 and i == 2))
                mm.then_inc(scattered, 1)

        @block.vector
        def _(dve):
            dve.memset(minus_half[:], -0.5).then_inc(consts_set, 1)
            dve.memset(v0[:, :, :, HD0:HD0 + 1], 1.0)
            dve.wait_ge(s_x, 16)
            for b in range(B):
                dve.bn_stats(stats[:, b, :], x[:, b, :]).then_inc(stat_link, 1)
            for b in range(B):
                dve.wait_ge(stat_link, b + 1)
                dve.bn_aggr(mv[:, b, :], stats[:, b, :]).then_inc(stat_link, 1)
            dve.wait_ge(stat_link, 2 * B)
            dve.tensor_scalar(var_eps[:], mv[:, :, 1], EPS0, None, ALU.add).then_inc(var_done, 1)
            dve.wait_ge(s_small, 48)
            dve.wait_ge(ada_ready, 1)

            def modulation(i, chunk, one):
                dve.tensor_scalar(mod[:, i, :], bank[7][:, i * B:(i + 1) * B], col("ada_b", chunk), one, ALU.add, ALU.add).then_inc(mod_done, 1)

            modulation(0, 2, 1.0)
            modulation(2, 4, 0.0)
            dve.wait_ge(rstd_done, 1)

            def save_gates(i):
                dve.wait_ge(gates_ready, 2 * i + 2)
                dve.tensor_tensor(gates[:, 2 * i:2 * i + 2, :], gate_ps[i][:].rearrange("p (b c) -> p b c", b=2),
                                  bc(row("ada_b"), [P, 2, 2 * C], 1), ALU.add).then_inc(gates_done, 1)

            def norm(b):
                wait(dve, zT_ready, b)
                dve.tensor_scalar(z[:], x[:, b, :], mv[:, b, 0:1], at(rstd[:], b), ALU.subtract, ALU.mult).then_inc(z_ready, 1)

            def save_qk(b):
                dve.wait_ge(qkv_ready, b + 1)
                wait(dve, rope_link, 3 * b)
                dve.tensor_tensor(qk0[:], qkv_ps[:, 0:2 * C], row("qkv_b")[:, 0:2 * C], ALU.add).then_inc(qkv_saved, 1)

            def save_v(b):
                dve.tensor_tensor(v0[:, b, :, 0:HD0], qkv_ps[:, 2 * C:3 * C].rearrange("p (h d) -> p h d", h=H),
                                  row("qkv_b")[:, 2 * C:3 * C].rearrange("p (h d) -> p h d", h=H), ALU.add).then_inc(v_done, 1)

            def row_max(b, g):
                n = NG * b + g
                dve.wait_ge(s_ready, n + 1)
                dve.tensor_reduce(neg_max[:, g, :], s_ps[g % 2][:].rearrange("p (h k) -> p h k", h=HG), AX, ALU.max, negate=True).then_inc(max_done, 1)

            def outputs(b, g):
                n = NG * b + g
                o = o_ps[:, 0:HG * (HD0 + 1)].rearrange("p (h d) -> p h d", h=HG)
                dve.wait_ge(o_ready, n + 1)
                dve.reciprocal(rinv[:, g, :], o[:, :, HD0]).then_inc(rec_done, 1)
                dve.wait_ge(rec_done, n + 1)
                if g == 0:
                    wait(dve, oT_ready, b)
                dve.tensor_tensor(o0[:, g * HG * HD0:(g + 1) * HG * HD0].rearrange("p (h d) -> p h d", h=HG), o[:, :, 0:HD0],
                                  bc(rinv[:, g, :], [P, HG, HD0], 2), ALU.mult).then_inc(o_done, 1)

            def offset(b):
                if isinstance(b, int) and b == 0:
                    dve.wait_ge(offsets_done, 1)
                dve.tensor_tensor(x[:, b, :], x[:, b, :], pg1[:, b, :], ALU.add).then_inc(xb_done, 1)

            def residual(b):
                dve.wait_ge(proj_ready, b + 1)
                dve.tensor_tensor(delta[:, 0, :], proj_ps[:, L:L + C], gates[:, b, 0:C], ALU.mult).then_inc(gated_done, 1)
                dve.wait_ge(gated_done, b + 1)
                dve.wait_ge(xb_done, b + 1)
                dve.tensor_tensor(x[:, b, :], x[:, b, :], delta[:, 0, :], ALU.add).then_inc(res_done, 1)

            def token_stats(b):
                dve.wait_ge(res_done, b + 1)
                dve.bn_stats(stats[:, b, :], x[:, b, :]).then_inc(stat_done, 1)

            def token_moments(b, norms):
                dve.wait_ge(stat_done, B * (norms - 1) + b + 1)
                dve.bn_aggr(mv[:, b, :], stats[:, b, :]).then_inc(moments_done, 1)

            def variances(half, norms, eps):
                part = slice(NG * half, NG * (half + 1))
                dve.wait_ge(moments_done, B * (norms - 1) + NG * (half + 1))
                dve.tensor_scalar(var_eps[:, part], mv[:, part, 1], eps, None, ALU.add).then_inc(var_done, 1)

            def centre(g):
                if g == 0:
                    dve.wait_ge(s_l1, 48)
                heads = slice(g * 2 * HG, (g + 1) * 2 * HG)
                w = wqk[:, g, :].rearrange("p (h d) -> p h d", d=HD1)
                dve.reduce_sum(wsum[:, heads], w, AX).then_inc(wsum_done, 1)
                dve.wait_ge(wsum_done, g + 1)
                dve.scalar_tensor_tensor(w, bc(wsum[:, heads], [P, 2 * HG, HD1], 2), -1.0 / HD1, w, ALU.mult, ALU.add).then_inc(wqk_done, 1)

            def step(b, ahead):
                for g in range(NG):
                    late = back(b, g, 4)
                    if g == 0 and ahead:
                        norm(b + 1)
                    if real(late[0]):
                        outputs(*late)
                    if g == 1 and ahead:
                        save_qk(b + 1)
                    if g == 1 and real(b - 2):
                        residual(b - 2)
                    if real(b):
                        row_max(b, g)
                    if g == 1 and ahead:
                        save_v(b + 1)
                    if g == 2 and real(b - 2):
                        token_stats(b - 2)
                    if g == 3 and real(b - 1):
                        offset(b - 1)
                    if isinstance(b, int) and b == 1:
                        centre(g)

            norm(0)
            modulation(1, 3, 1.0)
            modulation(3, 5, 0.0)
            dve.tensor_scalar(shift1[:], bank[7][:, 4 * B:5 * B], col("b_ada"), col("ln1_b"), ALU.add, ALU.add).then_inc(mod_done, 1)
            dve.wait_ge(s_rows, 16)
            save_qk(0)
            save_v(0)
            for i in range(3):
                save_gates(i)
            step(0, True)
            save_gates(3)
            step(1, True)
            with dve.Fori(2, B - 1) as b:
                step(b, True)
            for b in range(NG):
                token_moments(b, 1)
            variances(0, 1, EPS0)
            step(B - 1, False)

            def norm4(half):
                dve.wait_ge(rstd_done, half + 2)
                wait(dve, z4T_ready, half)
                for i in range(NG):
                    b = NG * half + i
                    dve.tensor_scalar(z4[:, i, :], x[:, b, :], mv[:, b, 0:1], at(rstd[:], b), ALU.subtract, ALU.mult).then_inc(z4_done, 1)

            def mlp_residual(half):
                for i in range(NG + 1):
                    b = NG * half + i
                    if i < NG:
                        dve.wait_ge(ff_ready, b + 1)
                        dve.tensor_tensor(delta[:, i % 2, :], (o_ps, misc_ps)[i % 2][:, 0:C], gates[:, b, C:2 * C], ALU.mult).then_inc(ffg_done, 1)
                    if i > 0:
                        dve.wait_ge(l0_done, b)
                        dve.bn_stats(stats[:, b - 1, :], x[:, b - 1, :]).then_inc(stat_done, 1)
                    if i < NG:
                        dve.wait_ge(ffg_done, b + 1)
                        dve.wait_ge(xf_done, b + 1)
                        dve.tensor_tensor(x[:, b, :], x[:, b, :], delta[:, i % 2, :], ALU.add).then_inc(l0_done, 1)
                    if i > 0:
                        token_moments(b - 1, 2)

            norm4(0)
            residual(B - 2)
            token_stats(B - 2)
            for g in range(NG):
                outputs(B - 1, g)
            offset(B - 1)
            residual(B - 1)
            token_stats(B - 1)
            for b in range(NG, B):
                token_moments(b, 1)
            variances(1, 1, EPS0)
            dve.wait_ge(offsets_done, 2)
            for b in range(NG):
                dve.wait_ge(z4_done, b + 1)
                dve.tensor_tensor(x[:, b, :], x[:, b, :], fg2[:, b, :], ALU.add).then_inc(xf_done, 1)
            norm4(1)
            for b in range(NG, B):
                dve.wait_ge(z4_done, b + 1)
                dve.tensor_tensor(x[:, b, :], x[:, b, :], fg2[:, b, :], ALU.add).then_inc(xf_done, 1)
            dve.tensor_scalar(q_gain[:], col("qn_g"), float(HD1) ** -0.5, None, ALU.mult)
            dve.tensor_scalar(q_bias[:], col("qn_b"), float(HD1) ** -0.5, None, ALU.mult).then_inc(consts_set, 1)
            mlp_residual(0)
            variances(0, 2, EPS1)

            def norm1(b):
                wait(dve, z1T_ready, b)
                dve.tensor_scalar(z[:], x[:, b, :], mv[:, b, 0:1], at(rstd[:], b), ALU.subtract, ALU.mult).then_inc(z1_ready, 1)

            def split_h(b):
                dve.wait_ge(h1T_done, b + 1)
                wait(dve, qkv1_ready, NG * b)
                dve.tensor_copy(h_hi[:], hT[:]).then_inc(h_split, 1)
                dve.wait_ge(h_split, 2 * b + 1)
                dve.tensor_tensor(h_lo[:], hT[:], h_hi[:].bitcast(F32), ALU.subtract).then_inc(h_split, 1)

            def row_max1(b, g):
                n = NG * b + g
                dve.wait_ge(s1_ready, n + 1)
                for a in range(2):
                    mx = dve.tensor_reduce(neg_max[:, g, 2 * a:2 * a + 2], s_ps[a][:, 0:2 * L].rearrange("p (i k) -> p i k", i=2), AX, ALU.max, negate=True)
                mx.then_inc(max1_done, 1)

            def sums(b, g):
                n = NG * b + g
                dve.wait_ge(squared, n + 1)
                dve.reduce_sum(sumsq[:], sq[:].rearrange("p (h d) -> p h d", d=HD1), AX).then_inc(sumsq_done, 1)

            def variances1(b, g):
                n = NG * b + g
                dve.wait_ge(sumsq_done, n + 1)
                wait(dve, hrstd_done, n)
                dve.tensor_scalar(head_var[:], sumsq[:], 1.0 / HD1, EPS1, ALU.mult, ALU.add).then_inc(hvar_done, 1)

            def qk_normed(b, g):
                n = NG * b + g
                dve.wait_ge(hrstd_done, n + 1)
                wait(dve, qkT1_ready, n)
                dve.tensor_tensor(qkn[:].rearrange("p (h d) -> p h d", d=HD1), qk_ps[g % 2][:].rearrange("p (h d) -> p h d", d=HD1),
                                  bc(head_rstd[:], [P, 2 * HG, HD1], 2), ALU.mult).then_inc(qkn_done, 1)

            def evac_k1T(b, g):
                n = NG * b + g
                dve.wait_ge(qkT1_ready, n + 1)
                wait(dve, s1_ready, n - NG + 1)
                dve.tensor_scalar(qkT1[:, g, 2:4, :], tp1_ps[:, 2 * L:4 * L].rearrange("p (a k) -> p a k", a=2),
                                  col("kn_g"), col("kn_b"), ALU.mult, ALU.add).then_inc(kT1_done, 1)

            def row_sums1(b, g):
                n = NG * b + g
                dve.wait_ge(exp1_done, n + 1)
                dve.reduce_sum(rsum[:, g, :], prob[:, g, :].rearrange("p (h k) -> p h k", h=HG), AX).then_inc(rsum1_done, 1)

            def row_scales1(b, g):
                n = NG * b + g
                dve.wait_ge(rsum1_done, n + 1)
                dve.reciprocal(rinv[:, g, :], rsum[:, g, :]).then_inc(rec1_done, 1)

            def outputs1(b, g):
                n = NG * b + g
                dve.wait_ge(o1_ready, n + 1)
                dve.wait_ge(rec1_done, n + 1)
                wait(dve, oT1_ready, n)
                dve.tensor_tensor(o1[:].rearrange("p (h d) -> p h d", h=HG), o_ps[:, 0:HG * HD1].rearrange("p (h d) -> p h d", h=HG),
                                  bc(rinv[:, g, :], [P, HG, HD1], 2), ALU.mult).then_inc(o1_done, 1)

            def token_stats1(b):
                dve.wait_ge(res1_done, b + 1)
                dve.bn_stats(stats[:, b, :], x[:, b, :]).then_inc(stat_done, 1)

            def residual1(b):
                dve.wait_ge(proj1_ready, b + 1)
                dve.tensor_tensor(x[:, b, :], x[:, b, :], zp_ps[:, L:L + C], ALU.add).then_inc(res1_done, 1)

            def step1(b, ahead):
                for g in range(NG):
                    one, two, three, four = (back(b, g, lag) for lag in (1, 2, 3, 4))
                    if real(two[0]):
                        evac_k1T(*two)
                    if g == 0 and real(b - 2):
                        residual1(b - 2)
                    if real(four[0]):
                        outputs1(*four)
                    if g == 0 and real(b - 2):
                        token_stats1(b - 2)
                    if real(three[0]):
                        row_sums1(*three)
                    if real(one[0]):
                        qk_normed(*one)
                    if g == NG - 2 and ahead:
                        norm1(b + 1)
                    if real(two[0]):
                        row_max1(*two)
                    if real(b):
                        sums(b, g)
                    if real(three[0]):
                        row_scales1(*three)
                    if real(b):
                        variances1(b, g)
                    if g == NG - 1 and ahead:
                        split_h(b + 1)

            dve.wait_ge(rstd_done, 4)
            norm1(0)
            dve.wait_ge(wv_split, 1)
            dve.tensor_tensor(wv_lo[:], wv[:], wv_hi[:].bitcast(F32), ALU.subtract).then_inc(wv_split, 1)
            split_h(0)
            mlp_residual(1)
            variances(1, 2, EPS1)
            step1(0, True)
            step1(1, True)
            dve.wait_ge(rstd_done, 5)
            with dve.Fori(2, B - 1) as b:
                step1(b, True)
            step1(B - 1, False)
            step1(B, False)
            residual1(B - 1)

            token_stats1(B - 1)
            for b in range(B):
                token_moments(b, 3)
            dve.wait_ge(moments_done, 3 * B)
            dve.tensor_scalar(var_eps[:], mv[:, :, 1], EPS1, None, ALU.add).then_inc(var_done, 1)
            g3 = gate[:, 0, :].rearrange("p (t e) -> p t e", e=E)
            logits = bank[7][:, 0:NTE].rearrange("p (t e) -> p t e", e=E)
            dve.wait_ge(logits_ready, 1)
            dve.reduce_max(gate_max[:], logits, AX).then_inc(gate_link, 1)
            dve.wait_ge(gate_link, 1)
            dve.tensor_tensor(g3, logits, bc(gate_max[:], [P, NT, E], 2), ALU.subtract).then_inc(gate_link, 1)
            dve.wait_ge(gate_exp, 1)
            dve.reduce_sum(gate_sum[:], g3, AX).then_inc(gate_link, 1)
            dve.wait_ge(gate_link, 3)
            dve.reciprocal(gate_max[:], gate_sum[:]).then_inc(gate_link, 1)
            dve.wait_ge(gate_link, 4)
            dve.tensor_tensor(gate[:, 1, :].rearrange("p (t e) -> p t e", e=E), g3, bc(gate_max[:], [P, NT, E], 2), ALU.mult).then_inc(gate_done, 1)
            dve.tensor_tensor(g3, g3, bc(gate_max[:], [P, NT, E], 2), ALU.mult).then_inc(gate_done, 1)
            dve.wait_ge(gateT_ready, 1)
            bits = bank[3][:, 0:P].bitcast(I32)
            dve.tensor_scalar(key_i[:, 0, :], bits, KEY_HALF, None, ALU.logical_shift_right).then_inc(key_link, 1)
            dve.tensor_scalar(key_i[:, 1, :], bits, 2 ** KEY_HALF - 1, None, ALU.bitwise_and).then_inc(key_link, 1)
            dve.wait_ge(key_link, 2)
            dve.tensor_copy(key_hi[:], key_i[:, 0, :]).then_inc(key_link, 1)
            dve.tensor_copy(key_lo[:], key_i[:, 1, :]).then_inc(key_link, 1)
            dve.wait_ge(key_link, 4)

            def search(key, start):
                width = TRIES // 2 + 1
                for step in range(STEPS):
                    n = start + step
                    tries = cst("tries")[:, step * width:(step + 1) * width]
                    tried = tries if step == 0 else cand[:]
                    for i in range(TRIES // 2):
                        dve.tensor_scalar(hits[:, i, :], key[:], tried[:, i + 1:i + 2], 0.0, ALU.is_ge, ALU.add, accum_out=count[:, i:i + 1]).then_inc(counted, 1)
                    after = cst("tries")[:, (step + 1) * width:(step + 2) * width] if step + 1 < STEPS else tries[:, 0:1].broadcast_to([P, width])
                    dve.tensor_scalar(cand_from[:], after, tried[:, 0:1], None, ALU.add).then_inc(cand_link, 1)
                    dve.wait_ge(totalled, n + 1)
                    dve.tensor_scalar(fits[:], bank[4][:, 0:TRIES], CAP - 0.5, 0.0, ALU.is_ge, ALU.add, accum_out=fitting[:]).then_inc(cand_link, 1)
                    dve.wait_ge(cand_link, 2 * n + 2)
                    dve.scalar_tensor_tensor(cand[:], fitting[:].broadcast_to([P, width]), float(TRIES ** (STEPS - 1 - step)), cand_from[:], ALU.mult, ALU.add).then_inc(narrowed, 1)
                    dve.wait_ge(narrowed, n + 1)

            search(key_hi, 0)
            dve.tensor_scalar(above[:], key_hi[:], cand[:, 0:1], 2.0 ** (KEY_HALF + 1), ALU.is_gt, ALU.mult).then_inc(key_link, 1)
            dve.tensor_scalar(eq_part[:], key_hi[:], cand[:, 0:1], None, ALU.is_equal).then_inc(key_link, 1)
            dve.tensor_scalar(key_lo[:], key_lo[:], 1.0, None, ALU.add).then_inc(key_link, 1)
            dve.wait_ge(key_link, 7)
            dve.tensor_tensor(eq_part[:], eq_part[:], key_lo[:], ALU.mult).then_inc(key_link, 1)
            dve.wait_ge(key_link, 8)
            dve.scalar_tensor_tensor(keys[:], above[:], -1.0, eq_part[:], ALU.add, ALU.add).then_inc(key_link, 1)
            dve.wait_ge(key_link, 9)
            search(keys, STEPS)
            R = slice(0, NTE)
            dve.tensor_scalar(masksT[R, 0, :], keys[R, :], cand[R, 0:1], None, ALU.is_gt).then_inc(masksT_done, 1)
            dve.tensor_scalar(masksT[R, 1, :], keys[R, :], cand[R, 0:1], None, ALU.is_equal).then_inc(masksT_done, 1)
            dve.wait_ge(masks_ready, 1)
            dve.tensor_copy(masks[:], bank[3][:].bitcast(BF16)[:, 0:2 * NTE].rearrange("p (a n) -> p a n", a=2)).then_inc(masks_done, 1)
            dve.wait_ge(masks_done, 1)
            dve.wait_ge(tie_rank_ready, 1)
            dve.scalar_tensor_tensor(tied[:], bank[5][:, 0:NTE], CAP - 0.5, masks[:, 1, :], ALU.is_lt, ALU.mult).then_inc(chosen_link, 1)
            dve.wait_ge(chosen_link, 1)
            dve.tensor_tensor(chosen[:], tied[:], masks[:, 0, :], ALU.add).then_inc(chosen_done, 1)
            dve.wait_ge(chosen_done, 1)
            dve.wait_ge(slots_ready, 1)
            dve.scalar_tensor_tensor(slot1[:], bank[6][:, 0:NTE], 1.0, chosen[:], ALU.add, ALU.mult).then_inc(slots_done, 1)
            dve.wait_ge(slots_done, 1)
            for tile in range(NT):
                for e in range(S_DVE):
                    dve.tensor_scalar(S[:, tile, e, :], iota_b[:], slot1[:, tile * E + e:tile * E + e + 1], None, ALU.is_equal).then_inc(s_dve, 1)
            dve.wait_ge(weight_ready, 1)
            dve.reduce_sum(weight[:], bank[2][:, 0:3 * E].rearrange("p (e a) -> p e a", a=3), AX).then_inc(weight_done, 1)
            for e in range(E + 2):
                if e < E:
                    dve.wait_ge(y_ready, e + 1)
                    dve.wait_ge(bw_done, e + 1)
                    dve.scalar_tensor_tensor(yw[:, e % 2, :], (bank[2], bank[7])[e % 2][:, 0:C], weight[:, e:e + 1], bw[:, e, :], ALU.mult, ALU.add).then_inc(yw_done, 1)
                for i in range(2):
                    f = e - 1 - i
                    if 0 <= f < E:
                        dve.wait_ge(y_part[i], f + 1)
                        dve.tensor_tensor(yr[:, f % 2, i, :], yw[:, f % 2, :] if i == 0 else yr[:, f % 2, 0, :], ypart[:, i, f, :], ALU.subtract).then_inc(y_rest[i], 1)
                if e < E:
                    dve.wait_ge(yw_done, e + 1)
                    dve.tensor_copy(ypart[:, 0, e, :], yw[:, e % 2, :]).then_inc(y_part[0], 1)
                for i in range(2):
                    f = e - 1 - i
                    if 0 <= f < E:
                        dve.wait_ge(y_rest[i], f + 1)
                        dve.tensor_copy(ypart[:, i + 1, f, :], yr[:, f % 2, i, :]).then_inc((y_part[1], y_parts)[i], 1)
            for tile in range(NT):
                dve.wait_ge(scattered, tile + 1)
                dve.tensor_tensor(x[:, tile, :], x[:, tile, :], bank[tile % 2][:, 0:C], ALU.add).then_inc(final_done, 1)

        @block.scalar
        def _(act):
            act.wait_ge(consts_set, 1)
            act.activation(unused[:, 0:1], minus_half[:, 0:1], ACT.Silu)
            act.wait_ge(s_small, 48)
            act.activation(silu_c[:], col("cond", 0, B), ACT.Silu).then_inc(silu_done, 1)
            act.activation(unused[:, 1:2], minus_half[:, 0:1], ACT.Exp)
            act.wait_ge(mod_done, 2)

            def evac_hT(b):
                act.wait_ge(zT_ready, b + 1)
                wait(act, qkv_ready, b)
                act.activation(hT[:], misc_ps[:, 0:L], ACT.Identity, scale=at(mod[:, 0, :], b), bias=at(mod[:, 2, :], b)).then_inc(hT_ready, 1)

            def evac_kT(b):
                act.wait_ge(qkT_ready, b + 1)
                wait(act, kx_done, NG * b)
                act.activation(kT0[:], tp_ps[:, L:2 * L], ACT.Copy).then_inc(kT_done, 1)

            def evac_qT(b):
                act.wait_ge(qkT_ready, b + 1)
                wait(act, s_ready, NG * b)
                act.activation(qT0[:], tp_ps[:, 0:L], ACT.Copy, scale=float(HD0) ** -0.5).then_inc(qT_done, 1)

            def exps(b, g):
                n = NG * b + g
                act.wait_ge(max_done, n + 1)
                for i in range(HG):
                    ex = act.activation(prob[:, g, i * L:(i + 1) * L], s_ps[g % 2][:, i * L:(i + 1) * L], ACT.Exp,
                                        bias=neg_max[:, g, i:i + 1])
                ex.then_inc(exp_done, 1)

            def evac_pT(b, g):
                n = NG * b + g
                act.wait_ge(pT_ready, n + 1)
                wait(act, o_ready, n - 1)
                act.activation(probT[:, g % 2, :], pT_ps[:], ACT.Copy).then_inc(pT_done, 1)

            def evac_oT(b):
                act.wait_ge(oT_ready, b + 1)
                wait(act, proj_ready, b)
                act.activation(oT0[:], proj_ps[:, 0:L], ACT.Copy).then_inc(oT_done, 1)

            def step(b, ahead):
                for g in range(NG):
                    one, two = back(b, g, 1), back(b, g, 2)
                    if g == 0 and real(b):
                        evac_qT(b)
                    if real(one[0]):
                        exps(*one)
                    if g == 0 and ahead:
                        evac_hT(b + 1)
                    if real(two[0]):
                        evac_pT(*two)
                    if g == 3 and real(b - 1):
                        evac_oT(b - 1)
                    if g == 2 and ahead:
                        evac_kT(b + 1)

            evac_hT(0)
            evac_kT(0)
            step(0, True)
            step(1, True)
            with act.Fori(2, B - 1) as b:
                step(b, True)
            def evac_h4T(half):
                act.wait_ge(mod_done, 5)
                act.wait_ge(z4T_ready, half + 1)
                wait(act, hid_ready, NCH * half)
                for i in range(NG):
                    b = NG * half + i
                    act.activation(h4T[:, i * L:(i + 1) * L], z4_ps[half][:, i * L:(i + 1) * L], ACT.Identity,
                                   scale=mod[:, 1, b:b + 1], bias=mod[:, 3, b:b + 1]).then_inc(h4T_done, 1)

            def evac_h1T(b):
                act.wait_ge(z1T_ready, b + 1)
                wait(act, h_split, 2 * b)
                act.activation(hT[:], zp_ps[:, 0:L], ACT.Identity, scale=col("ln1_g"), bias=at(shift1[:], b)).then_inc(h1T_done, 1)

            def gelus(half):
                for c in range(NCH):
                    act.wait_ge(hid_ready, NCH * half + c + 1)
                    wait(act, ff_ready, NG * half)
                    act.activation(hid[:, c, :], hid_ps[c][:], ACT.Gelu_apprx_tanh, bias=col("fc1_b", c)).then_inc(hid_done, 1)

            step(B - 1, False)
            exps(B - 1, 3)
            evac_pT(B - 1, 2)
            evac_pT(B - 1, 3)
            act.activation(unused[:, 2:3], minus_half[:, 0:1], ACT.Gelu_apprx_tanh)
            evac_h4T(0)
            evac_oT(B - 1)
            gelus(0)
            evac_h4T(1)
            act.wait_ge(s_l1, 48)
            act.wait_ge(xb_done, B)
            act.activation(wv_hi[:], wv[:], ACT.Copy).then_inc(wv_split, 1)
            gelus(1)
            evac_h1T(0)
            act.activation(unused[:, 3:4], minus_half[:, 0:1], ACT.Exp)

            def square(b, g):
                n = NG * b + g
                act.wait_ge(qk1_ready, n + 1)
                wait(act, sumsq_done, n)
                act.activation(sq[:], qk_ps[g % 2][:], ACT.Square).then_inc(squared, 1)

            def evac_v1(b, g):
                n = NG * b + g
                act.wait_ge(qkv1_ready, n + 1)
                wait(act, o1_ready, n - NG + 1)
                act.activation(v1[:, g, :], v_ps[:, 0:HG * HD1], ACT.Copy).then_inc(v1_done, 1)

            def evac_q1T(b, g):
                n = NG * b + g
                act.wait_ge(kT1_done, n + 1)
                wait(act, s1_ready, n - NG + 1)
                act.activation(qkT1[:, g, 0:2, :], tp1_ps[:, 0:2 * L].rearrange("p (a k) -> p a k", a=2),
                               ACT.Identity, scale=q_gain[:], bias=q_bias[:]).then_inc(qT1_done, 1)

            def exps1(b, g):
                n = NG * b + g
                act.wait_ge(max1_done, n + 1)
                for i in range(2):
                    for a in range(2):
                        ex = act.activation(prob[:, g, (2 * i + a) * L:(2 * i + a + 1) * L], s_ps[a][:, i * L:(i + 1) * L], ACT.Exp,
                                            bias=neg_max[:, g, 2 * a + i:2 * a + i + 1])
                ex.then_inc(exp1_done, 1)

            def evac_p1T(b, g):
                n = NG * b + g
                act.wait_ge(pT1_ready, n + 1)
                wait(act, o1_ready, n - 1)
                act.activation(probT[:, g % 2, :], pT_ps[:], ACT.Copy).then_inc(pT1_done, 1)

            def evac_o1T(b, g):
                n = NG * b + g
                act.wait_ge(oT1_ready, n + 1)
                wait(act, proj1_ready, b)
                act.activation(oT1[:, 2 * g:2 * g + 2, :], o_ps[:, HG * HD1:2 * HG * HD1].rearrange("p (a k) -> p a k", a=2), ACT.Copy).then_inc(oT1_done, 1)

            def evac_xT(k, first, end):
                act.wait_ge(xT_ready, k + 1)
                act.activation(xT[:, first * P:end * P], (bank[0], bank[6])[first // NG][:, first % NG * P:((end - 1) % NG + 1) * P], ACT.Copy).then_inc(xT_done, 1)

            def step1(b, ahead):
                for g in range(NG):
                    two, three, four = (back(b, g, lag) for lag in (2, 3, 4))
                    if real(two[0]):
                        evac_q1T(*two)
                    if real(three[0]):
                        evac_p1T(*three)
                    if real(four[0]):
                        evac_o1T(*four)
                    if real(b):
                        evac_v1(b, g)
                        square(b, g)
                    if g == NG - 1 and ahead:
                        evac_h1T(b + 1)
                    if real(two[0]):
                        exps1(*two)
                    if g == 1 and not real(b):
                        evac_xT(0, 0, NG)
                        evac_xT(1, NG, B - 1)

            act.wait_ge(consts_set, 2)
            step1(0, True)
            step1(1, True)
            with act.Fori(2, B - 1) as b:
                step1(b, True)
            step1(B - 1, False)
            step1(B, False)
            evac_xT(2, B - 1, B)
            act.wait_ge(gate_link, 2)
            act.activation(gate[:, 0, :], gate[:, 0, :], ACT.Exp).then_inc(gate_exp, 1)
            act.wait_ge(zx_done, NT)
            act.activation(zpart[:, 0, :, :], zx, ACT.Copy).then_inc(zcast, 1)
            for i in range(1, 3):
                act.wait_ge(zrest, i)
                act.activation(zpart[:, i, :, :], zr, ACT.Copy).then_inc(zcast, 1)
            act.wait_ge(gate_done, 2)
            act.activation(gpart[:, :, 0], gate[:, 0, :], ACT.Copy).then_inc(gcast, 1)
            for i in range(1, 3):
                act.wait_ge(grest, i)
                act.activation(gpart[:, :, i], gr[:], ACT.Copy).then_inc(gcast, 1)
            act.activation(unused[:, 4:5], minus_half[:, 0:1], ACT.Gelu_apprx_tanh)
            for tile in range(NT):
                act.wait_ge(st_ready, tile + 1)
                act.activation(ST[:, tile, :, :], bank[3 + tile % 2][:].bitcast(BF16).rearrange("p (e k) -> p e k", e=E), ACT.Copy).then_inc(st_done, 1)
            act.wait_ge(gathered, NT)
            for i in range(2):
                act.activation(xgT[:, NG * i:NG * (i + 1), :], bank[i][:].rearrange("p (e s) -> p e s", e=NG), ACT.Identity,
                               scale=col("mlp_g"), bias=col("mlp_b")).then_inc(xgT_done, 1)
            for e in range(E):
                act.wait_ge(hidE_ready, e + 1)
                wait(act, y_ready, e - 1)
                for c in range(NCH):
                    act.activation(hidE[:, e % 2, c, :], bank[5 + e % 2][:, c * CAP:(c + 1) * CAP], ACT.Gelu_apprx_tanh,
                                   bias=col("b1s", e * NCH + c)).then_inc(hidE_done, 1)

        @block.gpsimd
        def _(pool):
            pool.wait_ge(consts_set, 1)
            pool.wait_ge(var_done, 1)
            pool.tensor_tensor(rstd[:], var_eps[:], minus_half[:], ALU.pow).then_inc(rstd_done, 1)
            pool.wait_ge(s_const, 16)

            def rope(b):
                src = qk0[:].rearrange("p (h a d) -> p h a d", h=2 * H, a=2)
                dst = rope_b[:].rearrange("p (h a d) -> p h a d", h=2 * H, a=2)
                half = HD0 // 2
                pool.wait_ge(qkv_saved, b + 1)
                wait(pool, roped_done, b)
                pool.tensor_tensor(rope_a[:].rearrange("p (h d) -> p h d", h=2 * H), qk0[:].rearrange("p (h d) -> p h d", h=2 * H),
                                   bc(cst("cos"), [P, 2 * H, HD0], 1), ALU.mult).then_inc(rope_link, 1)
                for a in range(2):
                    pool.tensor_tensor(dst[:, :, a, :], src[:, :, 1 - a, :],
                                       bc(cst("sin")[:, a * half:(a + 1) * half], [P, 2 * H, half], 1), ALU.mult).then_inc(rope_link, 1)
                pool.wait_ge(rope_link, 3 * b + 3)
                wait(pool, qkT_ready, b)
                pool.tensor_tensor(roped[:], rope_a[:], rope_b[:], ALU.add).then_inc(roped_done, 1)

            def spread(b, g):
                n = NG * b + g
                pool.wait_ge(kT_done, b + 1)
                wait(pool, s_ready, n - NG + 1)
                pool.tensor_tensor(kx[:, g, :, :], bc(kT0[:], [P, HG, L], 1),
                                   bc(cst("mask")[:, g * HG:(g + 1) * HG], [P, HG, L], 2), ALU.mult).then_inc(kx_done, 1)

            def front(b):
                rope(b)
                for g in range(NG):
                    spread(b, g)

            for b in range(2):
                front(b)
            pool.wait_ge(gates_done, 4)
            pool.tensor_tensor(pg1[:], gates[:, :, 0:C], bc(row("proj_b"), [P, B, C], 1), ALU.mult).then_inc(offsets_done, 1)
            with pool.Fori(2, B) as b:
                front(b)

            def token_scales(norms, part):
                pool.wait_ge(var_done, norms)
                pool.tensor_tensor(rstd[:, part], var_eps[:, part], minus_half[:, part], ALU.pow).then_inc(rstd_done, 1)

            token_scales(2, slice(0, NG))
            pool.tensor_tensor(fg2[:], gates[:, :, C:2 * C], bc(row("fc2_b"), [P, B, C], 1), ALU.mult).then_inc(offsets_done, 1)
            for dst, name in ((ident_b, "ident"), (before_b, "before"), (iota_b, "iota1")):
                pool.tensor_copy(dst[:], cst(name))
            pool.tensor_copy(same_b[:], cst("same").rearrange("p (a k) -> p a k", a=2))
            pool.memset(ones_b[:], 1.0).then_inc(cast_done, 1)
            pool.wait_ge(wqk_done, NG)
            pool.wait_ge(s_ready, NG * B)
            for half in range(2):
                for g in range(2 * half, 2 * half + 2):
                    pool.tensor_copy(wqk_hi[:, g, :], wqk[:, g, :]).then_inc(wqk_hi_done, 1)
                    pool.wait_ge(wqk_hi_done, g + 1)
                    pool.tensor_tensor(wqk_lo[:, g, :], wqk[:, g, :], wqk_hi[:, g, :].bitcast(F32), ALU.subtract).then_inc(w_split, 1)
                token_scales(3 + half, slice(NG * (1 - half), NG * (2 - half)))
            token_scales(5, slice(NG, B))

            def head_scales(b, g):
                n = NG * b + g
                pool.wait_ge(hvar_done, n + 1)
                wait(pool, qkn_done, n)
                pool.tensor_tensor(head_rstd[:], head_var[:], minus_half[:], ALU.pow).then_inc(hrstd_done, 1)

            for g in range(NG):
                head_scales(0, g)
            with pool.Fori(1, B) as b:
                for g in range(NG):
                    head_scales(b, g)
            token_scales(6, slice(0, B))
            pool.wait_ge(rstd_done, 6)
            for b in range(NT):
                pool.tensor_scalar(zx[:, b, :], x[:, b, :], mv[:, b, 0:1], rstd[:, b:b + 1], ALU.subtract, ALU.mult).then_inc(zx_done, 1)
            pool.wait_ge(zx_done, NT)
            pool.wait_ge(zcast, 1)
            pool.tensor_tensor(zr, zx, zpart[:, 0, :, :], ALU.subtract).then_inc(zrest, 1)
            pool.wait_ge(zcast, 2)
            pool.wait_ge(zrest, 1)
            pool.tensor_tensor(zr, zr, zpart[:, 1, :, :], ALU.subtract).then_inc(zrest, 1)
            pool.wait_ge(gcast, 1)
            pool.tensor_tensor(gr[:], gate[:, 0, :], gpart[:, :, 0], ALU.subtract).then_inc(grest, 1)
            pool.wait_ge(gcast, 2)
            pool.wait_ge(grest, 1)
            pool.tensor_tensor(gr[:], gr[:], gpart[:, :, 1], ALU.subtract).then_inc(grest, 1)
            pool.wait_ge(slots_done, 1)
            for tile in range(NT):
                for e in range(S_DVE, E):
                    pool.tensor_scalar(S[:, tile, e, :], iota_b[:], slot1[:, tile * E + e:tile * E + e + 1], None, ALU.is_equal).then_inc(s_pool, 1)
            pool.wait_ge(weight_done, 1)
            pool.wait_ge(s_moe, 48)
            for e in range(E):
                pool.tensor_scalar(bw[:, e, :], b2s[:, e * C:(e + 1) * C], weight[:, e:e + 1], None, ALU.mult).then_inc(bw_done, 1)


def constants():
    c = np.zeros((P, N_CONST), np.float32)

    def put(name, a):
        c[:a.shape[0], CONST[name][0]:CONST[name][1]] = a

    put("ident", np.eye(P))
    put("before", np.triu(np.ones((P, P)), 1))
    put("iota1", np.tile(np.arange(1, P + 1), (P, 1)))
    inv = (1.0 / np.float32(10000.0) ** (np.arange(0, HD0, 2, dtype=np.float32) / HD0)).astype(np.float32)
    ang = np.arange(L, dtype=np.float32)[:, None] * inv[None, :]
    put("cos", np.concatenate([np.cos(ang), np.cos(ang)], 1))
    put("sin", np.concatenate([-np.sin(ang), np.sin(ang)], 1))
    put("mask", np.arange(P)[:, None] // HD0 == np.arange(H)[None, :])
    q = np.arange(P)
    same = (q[:, None, None] // (B * E) == np.arange(2)[None, :, None]) & (q[:, None, None] % E == q[None, None, :] % E)
    put("same", same.reshape(P, 2 * P))
    tries = np.zeros((P, STEPS, TRIES // 2 + 1))
    for step in range(STEPS):
        for i in range(TRIES // 2):
            tries[:, step, i + 1] = (2 * i + 1 + (np.arange(P) >= P // 2)) * TRIES ** (STEPS - 1 - step)
    put("tries", tries.reshape(P, -1))
    return c


def laid_out(a):
    two = lambda v: np.concatenate([v, v]).reshape(P, 1)
    vec = lambda v, n: v.reshape(n, P).T
    wqkv = a["L1_cond_Wqkv"].reshape(3, NG, HG * HD1, C)
    parts = {
        "cond": a["cond_1024"].T, "ada_b": vec(a["L0_cond_ada_b"], 6), "fc1_b": vec(a["L0_cond_fc1_b"], NCH),
        "b_ada": vec(a["L1_cond_b_ada"], 1), "ln1_g": vec(a["L1_cond_ln1_g"], 1), "ln1_b": vec(a["L1_cond_ln1_b"], 1),
        "qn_g": two(a["L1_cond_qn_g"]), "qn_b": two(a["L1_cond_qn_b"]), "kn_g": two(a["L1_cond_kn_g"]), "kn_b": two(a["L1_cond_kn_b"]),
        "mlp_g": vec(a["L1_cond_mlp_g"], 1), "mlp_b": vec(a["L1_cond_mlp_b"], 1),
        "b1s": a["L1_cond_b1s"].reshape(E * NCH, P).T, "wgate": a["L1_cond_Wgate"].T,
    }
    rows = {"qkv_b": a["L0_cond_qkv_b"], "proj_b": a["L0_cond_proj_b"], "fc2_b": a["L0_cond_fc2_b"],
            "ada_b": a["L0_cond_ada_b"][:2 * C]}
    out = {
        "x": a["x"],
        "cols": np.concatenate([parts[n] for n in COLS], 1),
        "rows": np.concatenate([rows[n] for n in ROWS]),
        "b2s": a["L1_cond_b2s"].reshape(-1),
        "consts": constants(),
        "ada_w": a["L0_cond_ada_w"].T, "w_ada": a["L1_cond_W_ada"].T,
        "qkv_w": a["L0_cond_qkv_w"].T, "proj_w": a["L0_cond_proj_w"].T,
        "fc1_w": a["L0_cond_fc1_w"].T,
        "fc2_w": a["L0_cond_fc2_w"].reshape(C, NCH, P).transpose(2, 1, 0),
        "wqk": np.concatenate([wqkv[0], wqkv[1]], 1).transpose(2, 0, 1),
        "wv": wqkv[2].transpose(2, 0, 1),
        "wout": a["L1_cond_Wout"].reshape(C, 2 * NG, P).transpose(2, 1, 0),
        "fc1s": a["L1_cond_fc1s"].transpose(2, 0, 1),
        "fc2s": a["L1_cond_fc2s"].reshape(E, C, NCH, P).transpose(3, 0, 2, 1),
    }
    return {n: np.ascontiguousarray(v) for n, v in out.items()}


def kernel(**inputs):
    import concourse.bacc as bacc
    from concourse.bass_utils import run_bass_kernel_spmd

    arrays = laid_out({n: np.asarray(v) for n, v in inputs.items()})
    nc = bacc.Bacc("TRN2", target_bir_lowering=False, num_devices=1)
    t = {n: nc.dram_tensor(f"in_{n}", v.shape, mybir.dt.from_np(v.dtype), kind="ExternalInput").ap() for n, v in arrays.items()}
    t["out"] = nc.dram_tensor("out", (B, L, C), F32, kind="ExternalOutput").ap()
    program(nc, t)
    r = run_bass_kernel_spmd(nc, [{f"in_{n}": v for n, v in arrays.items()}], core_ids=[0])
    return r.results[0]["out"]
```
